# Optimizing a Trainium2 kernel written in Bass

```python
import numpy as np
import jax
import jax.numpy as jnp

def _softmax(x, axis=-1):
    return jax.nn.softmax(x, axis=axis)

def _gelu(x):
    return jax.nn.gelu(x, approximate=True)

def _silu(x):
    return jax.nn.silu(x)

def _sigmoid(x):
    return jax.nn.sigmoid(x)

def _layernorm(x, axis=-1, eps=1e-05):
    m = jnp.mean(x, axis=axis, keepdims=True)
    v = jnp.var(x, axis=axis, keepdims=True)
    return (x - m) / jnp.sqrt(v + eps)

def _scatter_add(tgt, idx, src, axis=0):
    return tgt.at[idx].add(src)

def _segment_sum(src, seg, n):
    return jax.ops.segment_sum(src, seg, n)
kernel_name = 'mk_perceiver_d4_seqx_r4_d2b91f'

def setup_inputs(seed: int=0):
    np.random.seed(seed)
    _w = jnp.asarray

    def _rec_inputs():
        import jax
        import jax.numpy as jnp
        _rk = jax.random.key(seed)
        x = -0.0002928 + 1 * jax.random.normal(jax.random.fold_in(_rk, 1), (16, 64, 256), jnp.float32)
        _lenS = 64 - jax.random.randint(jax.random.fold_in(_rk, 7), (16,), 0, max(1, 64 // 4) + 1, jnp.int32)
        _lenS2 = 256 - jax.random.randint(jax.random.fold_in(_rk, 8), (16,), 0, max(1, 256 // 4) + 1, jnp.int32)
        _ctx_1024P = jax.random.normal(jax.random.fold_in(_rk, 11), (16, 16, 256), jnp.float32)
        _ctx_1024c = jax.random.dirichlet(jax.random.fold_in(_rk, 511), 0.3 * jnp.ones((16,), jnp.float32), (16, 256))
        _ctx_1024t = jnp.einsum('bsk,bkd->bsd', _ctx_1024c, _ctx_1024P)
        _ctx_1024t = _ctx_1024t * jax.lax.rsqrt(jnp.mean(jnp.square(_ctx_1024t)) + 1e-12) * 0.953939
        ctx_1024 = -1.39393e-06 + 0.999914 * (_ctx_1024t + 0.3 * jax.random.normal(jax.random.fold_in(_rk, 611), (16, 256, 256), jnp.float32))
        _validS = jnp.arange(64)[None, :] < _lenS[:, None]
        _validS2 = jnp.arange(256)[None, :] < _lenS2[:, None]
        _causal = jnp.tril(jnp.ones((64, 64), dtype=bool))
        mask_BxSxS2_ff0 = jnp.where(jnp.ones((16, 64, 256), dtype=bool), 0.0, -1000000000.0).astype(jnp.float32)
        mask_BxS2_if0 = jnp.where(jnp.ones((16, 256), dtype=bool), 0, 1).astype(jnp.int32)
        mask_BxS2_bf0 = jnp.logical_not(jnp.ones((16, 256), dtype=bool))
        return (x, ctx_1024, mask_BxSxS2_ff0, mask_BxS2_if0, mask_BxS2_bf0)
    x, ctx_1024, mask_BxSxS2_ff0, mask_BxS2_if0, mask_BxS2_bf0 = _rec_inputs()

    def _L0_xattn_setup():
        import jax, jax.numpy as jnp
        import numpy as np
        DIM = 256
        CTX_DIM = 256
        HEADS = 16
        DIM_HEAD = 64
        INNER = HEADS * DIM_HEAD
        FF_INNER = 4 * DIM
        EPS = 1e-05

        def layer_norm(x, g, b):
            mu = jnp.mean(x, axis=-1, keepdims=True)
            var = jnp.var(x, axis=-1, keepdims=True)
            return (x - mu) * jax.lax.rsqrt(var + EPS) * g + b
        key = jax.random.key(seed)
        ks = jax.random.split(key, 10)
        b, n, j = (2, 512, 512)
        x = jax.random.normal(ks[0], (b, n, DIM), dtype=jnp.float32)
        context = jax.random.normal(ks[1], (b, j, CTX_DIM), dtype=jnp.float32)
        mask = jnp.zeros((b, n, j), dtype=jnp.float32)
        s = 0.02
        Wq = jax.random.normal(ks[2], (DIM, INNER), dtype=jnp.float32) * s
        Wkv = jax.random.normal(ks[3], (CTX_DIM, 2 * DIM_HEAD), dtype=jnp.float32) * s
        Wout = jax.random.normal(ks[4], (INNER, DIM), dtype=jnp.float32) * s
        W1 = jax.random.normal(ks[5], (DIM, 2 * FF_INNER), dtype=jnp.float32) * s
        W2 = jax.random.normal(ks[6], (FF_INNER, DIM), dtype=jnp.float32) * s
        ln_g = jnp.ones((DIM,), jnp.float32)
        ln_b = jnp.zeros((DIM,), jnp.float32)
        cln_g = jnp.ones((CTX_DIM,), jnp.float32)
        cln_b = jnp.zeros((CTX_DIM,), jnp.float32)
        return {'x': x, 'context': context, 'mask': mask, 'ln_g': ln_g, 'ln_b': ln_b, 'cln_g': cln_g, 'cln_b': cln_b, 'Wq': Wq, 'Wkv': Wkv, 'Wout': Wout, 'W1': W1, 'W2': W2}
    _L0_xattn_all = _L0_xattn_setup()
    _L0_xattn_in = {k: v for k, v in _L0_xattn_all.items() if k in ('ln_g', 'ln_b', 'cln_g', 'cln_b', 'Wq', 'Wkv', 'Wout', 'W1', 'W2')}
    del _L0_xattn_all

    def _L0_attn_setup():
        import jax, jax.numpy as jnp
        import numpy as np
        DIM = 256
        B, S = (8, 512)
        LN_EPS = 1e-05
        key = jax.random.key(seed)
        k1, k2, k3 = jax.random.split(key, 3)
        x = jax.random.normal(k1, (B, S, DIM), dtype=jnp.float32)
        w_qkv = jax.random.normal(k2, (3 * DIM, DIM), dtype=jnp.float32) * np.sqrt(2.0 / (DIM + 3 * DIM))
        w_fc = jax.random.normal(k3, (DIM, DIM), dtype=jnp.float32) * np.sqrt(2.0 / (DIM + DIM))
        b_fc = jnp.zeros((DIM,), dtype=jnp.float32)
        gamma = jnp.ones((DIM,), dtype=jnp.float32)
        beta = jnp.zeros((DIM,), dtype=jnp.float32)
        return {'x': x, 'w_qkv': w_qkv, 'w_fc': w_fc, 'b_fc': b_fc, 'gamma': gamma, 'beta': beta}
    _L0_attn_all = _L0_attn_setup()
    _L0_attn_in = {k: v for k, v in _L0_attn_all.items() if k in ('w_qkv', 'w_fc', 'b_fc', 'gamma', 'beta')}
    del _L0_attn_all

    def _L0_ffn_setup():
        import jax, jax.numpy as jnp
        import numpy as np
        N_EXP = 8
        TOP_K = 2
        CAPACITY_FACTOR = 1.25
        key = jax.random.key(seed)
        ks = jax.random.split(key, 5)
        B, T, D = (4, 256, 256)
        H = 4 * D
        E = N_EXP
        x = jax.random.normal(ks[0], (B, T, D), jnp.float32)
        gate_w = jax.random.normal(ks[1], (D, E), jnp.float32) * 0.02
        c_fc = jax.random.normal(ks[2], (E, D, H), jnp.float32) * 0.02
        fc_bias = jnp.zeros((E, 1, H), jnp.float32)
        c_proj = jax.random.normal(ks[3], (E, H, D), jnp.float32) * 0.02
        proj_bias = jnp.zeros((E, 1, D), jnp.float32)
        return dict(x=x, gate_w=gate_w, c_fc=c_fc, fc_bias=fc_bias, c_proj=c_proj, proj_bias=proj_bias)
    _L0_ffn_all = _L0_ffn_setup()
    _L0_ffn_in = {k: v for k, v in _L0_ffn_all.items() if k in ('gate_w', 'c_fc', 'fc_bias', 'c_proj', 'proj_bias')}
    del _L0_ffn_all

    def _L1_xattn_setup():
        import jax, jax.numpy as jnp
        import numpy as np
        HEAD_NUM = 16
        NEG_INF = float('-inf')
        key = jax.random.key(seed)
        ks = jax.random.split(key, 4)
        B, S, D = (4, 512, 256)
        q = jax.random.normal(ks[0], (B, S, D), dtype=jnp.float32)
        k = jax.random.normal(ks[1], (B, S, D), dtype=jnp.float32)
        v = jax.random.normal(ks[2], (B, S, D), dtype=jnp.float32)
        W = jax.random.normal(ks[3], (D, D), dtype=jnp.float32) / np.sqrt(D)
        b = jnp.zeros((D,), dtype=jnp.float32)
        mask = jnp.zeros((B, S), dtype=jnp.int32)
        return {'q': q, 'k': k, 'v': v, 'W': W, 'b': b, 'mask': mask}
    _L1_xattn_all = _L1_xattn_setup()
    _L1_xattn_in = {k: v for k, v in _L1_xattn_all.items() if k in ('W', 'b')}
    del _L1_xattn_all

    def _L1_attn_setup():
        import jax, jax.numpy as jnp
        import numpy as np
        DIM = 256
        NH = 16
        HD = DIM // NH
        DROPE = 16
        MAXSEQ = 512
        LAT = 64
        BATCH = 2
        SEQ = 512

        def _rope_freqs(max_seq, head_dim):
            inv = 1.0 / 10000.0 ** (jnp.arange(0, head_dim, 2, dtype=jnp.float32) / head_dim)
            ang = jnp.arange(max_seq, dtype=jnp.float32)[:, None] * inv[None, :]
            return (jnp.cos(ang), jnp.sin(ang))

        def _apply_decoupled_rope(x, cosf, sinf, d_rope):
            b, d1, d2, hd = x.shape
            half = d_rope // 2
            xr = x[..., :d_rope].astype(jnp.float32).reshape(b, d1, d2, half, 2)
            xa, xb = (xr[..., 0], xr[..., 1])
            c = cosf[:d1, :half][None, :, None, :]
            s = sinf[:d1, :half][None, :, None, :]
            rot = jnp.stack([xa * c - xb * s, xa * s + xb * c], axis=-1)
            rot = rot.reshape(b, d1, d2, d_rope)
            return jnp.concatenate([rot, x[..., d_rope:]], axis=-1)
        key = jax.random.key(seed)
        ks = jax.random.split(key, 8)

        def w(k, o, i):
            return jax.random.normal(k, (o, i), jnp.float32) / np.sqrt(i).astype(np.float32)
        return {'x': jax.random.normal(ks[0], (BATCH, SEQ, DIM), jnp.float32), 'wq': w(ks[1], NH * HD, DIM), 'wk_a': w(ks[2], LAT, DIM), 'wk_b': w(ks[3], NH * HD, LAT), 'wv_a': w(ks[4], LAT, DIM), 'wv_b': w(ks[5], NH * HD, LAT), 'wo': w(ks[6], DIM, NH * HD)}
    _L1_attn_all = _L1_attn_setup()
    _L1_attn_in = {k: v for k, v in _L1_attn_all.items() if k in ('wq', 'wk_a', 'wk_b', 'wv_a', 'wv_b', 'wo')}
    del _L1_attn_all

    def _L1_ffn_setup():
        import jax, jax.numpy as jnp
        import numpy as np
        EPS = 1e-05

        def layernorm(x, w, b):
            mu = jnp.mean(x, axis=-1, keepdims=True)
            var = jnp.mean(jnp.square(x - mu), axis=-1, keepdims=True)
            return (x - mu) * jax.lax.rsqrt(var + EPS) * w + b

        def act_quant_fake(x):
            scale = 127.0 / jnp.clip(jnp.max(jnp.abs(x), axis=-1, keepdims=True), EPS, None)
            return jnp.clip(jnp.round(x * scale), -128.0, 127.0) / scale

        def weight_quant_fake(w):
            scale = 1.0 / jnp.clip(jnp.mean(jnp.abs(w)), EPS, None)
            return jnp.clip(jnp.round(w * scale), -1.0, 1.0) / scale

        def bitlinear(x, w, b):
            dqx = x + jax.lax.stop_gradient(act_quant_fake(x) - x)
            dqw = w + jax.lax.stop_gradient(weight_quant_fake(w) - w)
            return jnp.einsum('btd,hd->bth', dqx, dqw) + b
        key = jax.random.key(seed)
        ks = jax.random.split(key, 5)
        dim, hidden = (256, 1024)
        B, T = (8, 512)
        return {'x': jax.random.normal(ks[0], (B, T, dim), dtype=jnp.float32), 'ln1_w': jnp.ones((dim,), jnp.float32), 'ln1_b': jnp.zeros((dim,), jnp.float32), 'w1': jax.random.normal(ks[1], (hidden, dim), jnp.float32) * (1.0 / np.sqrt(dim)), 'b1': jax.random.normal(ks[2], (hidden,), jnp.float32) * 0.01, 'ln2_w': jnp.ones((hidden,), jnp.float32), 'ln2_b': jnp.zeros((hidden,), jnp.float32), 'w2': jax.random.normal(ks[3], (dim, hidden), jnp.float32) * (1.0 / np.sqrt(hidden)), 'b2': jax.random.normal(ks[4], (dim,), jnp.float32) * 0.01}
    _L1_ffn_all = _L1_ffn_setup()
    _L1_ffn_in = {k: v for k, v in _L1_ffn_all.items() if k in ('ln1_w', 'ln1_b', 'w1', 'b1', 'ln2_w', 'ln2_b', 'w2', 'b2')}
    del _L1_ffn_all

    def _L2_xattn_setup():
        import jax, jax.numpy as jnp
        import numpy as np
        B, T, H, NH = (4, 512, 256, 16)
        DK = H // NH

        def _proj_heads(x, W, b):
            y = x @ W.T + b
            bsz, t, _ = y.shape
            return y.reshape(bsz, t, NH, DK).transpose(0, 2, 1, 3)
        key = jax.random.key(seed)
        ks = jax.random.split(key, 12)
        scale = 1.0 / np.sqrt(H)
        inp = {'query': jax.random.normal(ks[0], (B, T, H), dtype=jnp.float32), 'key': jax.random.normal(ks[1], (B, T, H), dtype=jnp.float32), 'value': jax.random.normal(ks[2], (B, T, H), dtype=jnp.float32), 'mask': jnp.zeros((B, T), dtype=bool), 'Wq': jax.random.normal(ks[3], (H, H), dtype=jnp.float32) * scale, 'bq': jax.random.normal(ks[4], (H,), dtype=jnp.float32) * scale, 'Wk': jax.random.normal(ks[5], (H, H), dtype=jnp.float32) * scale, 'bk': jax.random.normal(ks[6], (H,), dtype=jnp.float32) * scale, 'Wv': jax.random.normal(ks[7], (H, H), dtype=jnp.float32) * scale, 'bv': jax.random.normal(ks[8], (H,), dtype=jnp.float32) * scale, 'Wo': jax.random.normal(ks[9], (H, H), dtype=jnp.float32) * scale, 'bo': jax.random.normal(ks[10], (H,), dtype=jnp.float32) * scale}
        return inp
    _L2_xattn_all = _L2_xattn_setup()
    _L2_xattn_in = {k: v for k, v in _L2_xattn_all.items() if k in ('Wq', 'bq', 'Wk', 'bk', 'Wv', 'bv', 'Wo', 'bo')}
    del _L2_xattn_all

    def _L2_attn_setup():
        import jax, jax.numpy as jnp
        import numpy as np
        import math
        IN_FEATURES = 256
        OUT_FEATURES = 256
        N_BANK = 2048
        N_LAYER = 12
        N_EMBD = 256
        key = jax.random.key(seed)
        kq, kk, kv = jax.random.split(key, 3)
        q = jax.random.normal(kq, (4, 512, IN_FEATURES), dtype=jnp.float32)
        k = 0.02 * jax.random.normal(kk, (N_BANK, IN_FEATURES), dtype=jnp.float32)
        v_std = 2.0 / N_LAYER / math.sqrt(N_EMBD)
        v = v_std * jax.random.normal(kv, (N_BANK, OUT_FEATURES), dtype=jnp.float32)
        return {'q': q, 'k': k, 'v': v}
    _L2_attn_all = _L2_attn_setup()
    _L2_attn_in = {k: v for k, v in _L2_attn_all.items() if k in ('k', 'v')}
    del _L2_attn_all

    def _L2_ffn_setup():
        import jax, jax.numpy as jnp
        import numpy as np
        HIDDEN = 256
        INTER = 1024
        N_EXPERTS = 8
        TOP_K = 2
        INIT_STD = 0.02
        key = jax.random.key(seed)
        ks = jax.random.split(key, 6)
        x = jax.random.normal(ks[0], (2, 256, HIDDEN), dtype=jnp.float32)
        Wg = jax.random.normal(ks[1], (N_EXPERTS, HIDDEN), dtype=jnp.float32) * INIT_STD
        W1 = jax.random.normal(ks[2], (N_EXPERTS, HIDDEN, INTER), dtype=jnp.float32) * INIT_STD
        b1 = jnp.zeros((N_EXPERTS, INTER), dtype=jnp.float32)
        W2 = jax.random.normal(ks[3], (N_EXPERTS, INTER, HIDDEN), dtype=jnp.float32) * INIT_STD
        b2 = jnp.zeros((N_EXPERTS, HIDDEN), dtype=jnp.float32)
        return {'x': x, 'Wg': Wg, 'W1': W1, 'b1': b1, 'W2': W2, 'b2': b2}
    _L2_ffn_all = _L2_ffn_setup()
    _L2_ffn_in = {k: v for k, v in _L2_ffn_all.items() if k in ('Wg', 'W1', 'b1', 'W2', 'b2')}
    del _L2_ffn_all

    def _L3_xattn_setup():
        import jax, jax.numpy as jnp
        import numpy as np
        D_MODEL = 256
        SCALE = 1.0 / np.sqrt(D_MODEL).astype(np.float32)
        key = jax.random.key(seed)
        ks = jax.random.split(key, 7)
        B, S, D, DK = (4, 1024, D_MODEL, 64)
        return {'query': jax.random.normal(ks[0], (B, S, D), dtype=jnp.float32), 'key': jax.random.normal(ks[1], (B, S, D), dtype=jnp.float32), 'value': jax.random.normal(ks[2], (B, S, D), dtype=jnp.float32), 'Wq': jax.random.normal(ks[3], (D, DK), dtype=jnp.float32) * (1.0 / np.sqrt(D).astype(np.float32)), 'bq': jax.random.normal(ks[4], (DK,), dtype=jnp.float32) * 0.01, 'Wo': jax.random.normal(ks[5], (DK, D), dtype=jnp.float32) * (1.0 / np.sqrt(DK).astype(np.float32)), 'bo': jax.random.normal(ks[6], (D,), dtype=jnp.float32) * 0.01}
    _L3_xattn_all = _L3_xattn_setup()
    _L3_xattn_in = {k: v for k, v in _L3_xattn_all.items() if k in ('Wq', 'bq', 'Wo', 'bo')}
    del _L3_xattn_all

    def _L3_attn_setup():
        import math
        import jax, jax.numpy as jnp
        import numpy as np
        B, S = (4, 512)
        D_MODEL, D_STATE = (256, 64)
        KSIZE, CHUNK, STEPS = (5, 16, 2)
        TOPK, LOOKBACK = (8, 64)

        def _forward(x, Wi, bi, conv_w, conv_b, Wp, bp, Wh, bh, Wq, bq, Wk, bk, Wv, bv, W1, b1, W2, b2, Wo, bo):
            bsz, seq, _ = x.shape
            dim = Wi.shape[1]
            h = x @ Wi + bi
            pos = jnp.arange(seq)[:, None] + jnp.arange(LOOKBACK)[None, :]
            valid = pos - LOOKBACK >= 0
            cidx = jnp.arange(seq)[:, None] + jnp.arange(KSIZE)[None, :]
            scale = 1.0 / math.sqrt(dim)
            for _ in range(STEPS):
                hp = jnp.pad(h, ((0, 0), (KSIZE - 1, 0), (0, 0)))
                mixed = jnp.einsum('bskd,kd->bsd', hp[:, cidx, :], conv_w) + conv_b
                ph = h.reshape(bsz, seq // CHUNK, CHUNK, dim).mean(axis=2)
                pb = jnp.repeat(ph @ Wp + bp, CHUNK, axis=1)
                q = h @ Wq + bq
                k = h @ Wk + bk
                v = h @ Wv + bv
                kp = jnp.pad(k, ((0, 0), (LOOKBACK, 0), (0, 0)))
                scores = jnp.einsum('bsd,bsld->bsl', q, kp[:, pos, :]) * scale
                scores = jnp.where(valid[None], scores, -jnp.inf)
                ts, tr = jax.lax.top_k(scores, TOPK)
                m = ts.max(axis=-1, keepdims=True)
                e = jnp.exp(ts - jnp.where(jnp.isfinite(m), m, 0.0))
                w = e / jnp.maximum(e.sum(axis=-1, keepdims=True), 1e-30)
                tok = jnp.clip(jnp.arange(seq)[None, :, None] - LOOKBACK + tr, 0, seq - 1)
                vg = jnp.take_along_axis(v, tok.reshape(bsz, seq * TOPK, 1), axis=1).reshape(bsz, seq, TOPK, dim)
                summ = jnp.einsum('bsk,bskd->bsd', w, vg)
                ui = jnp.concatenate([h, mixed, pb, summ], axis=-1)
                delta = jnp.tanh(ui @ W1 + b1) @ W2 + b2
                gate = jax.nn.sigmoid(h @ Wh + bh)[..., 2:3]
                h = h + delta * gate
            return x + (h @ Wo + bo)
        key = jax.random.key(seed)
        ks = jax.random.split(key, 12)
        gn = lambda k, shape, s: jax.random.normal(k, shape, jnp.float32) * s
        s_in = 1.0 / math.sqrt(D_MODEL)
        s_st = 1.0 / math.sqrt(D_STATE)
        inp = {}
        inp['x'] = gn(ks[0], (B, S, D_MODEL), 1.0)
        inp['Wi'] = gn(ks[1], (D_MODEL, D_STATE), s_in)
        inp['bi'] = jnp.zeros((D_STATE,), jnp.float32)
        inp['conv_w'] = gn(ks[2], (KSIZE, D_STATE), 1.0 / math.sqrt(KSIZE))
        inp['conv_b'] = jnp.zeros((D_STATE,), jnp.float32)
        inp['Wp'] = gn(ks[3], (D_STATE, D_STATE), s_st)
        inp['bp'] = jnp.zeros((D_STATE,), jnp.float32)
        inp['Wh'] = gn(ks[4], (D_STATE, 3), s_st)
        inp['bh'] = jnp.zeros((3,), jnp.float32)
        inp['Wq'] = gn(ks[5], (D_STATE, D_STATE), s_st)
        inp['bq'] = jnp.zeros((D_STATE,), jnp.float32)
        inp['Wk'] = gn(ks[6], (D_STATE, D_STATE), s_st)
        inp['bk'] = jnp.zeros((D_STATE,), jnp.float32)
        inp['Wv'] = gn(ks[7], (D_STATE, D_STATE), s_st)
        inp['bv'] = jnp.zeros((D_STATE,), jnp.float32)
        inp['W1'] = gn(ks[8], (4 * D_STATE, D_STATE), 1.0 / math.sqrt(4 * D_STATE))
        inp['b1'] = jnp.zeros((D_STATE,), jnp.float32)
        inp['W2'] = gn(ks[9], (D_STATE, D_STATE), s_st)
        inp['b2'] = jnp.zeros((D_STATE,), jnp.float32)
        inp['Wo'] = gn(ks[10], (D_STATE, D_MODEL), 0.02 * s_st)
        inp['bo'] = jnp.zeros((D_MODEL,), jnp.float32)
        return inp
    _L3_attn_all = _L3_attn_setup()
    _L3_attn_in = {k: v for k, v in _L3_attn_all.items() if k in ('Wi', 'bi', 'conv_w', 'conv_b', 'Wp', 'bp', 'Wh', 'bh', 'Wq', 'bq', 'Wk', 'bk', 'Wv', 'bv', 'W1', 'b1', 'W2', 'b2', 'Wo', 'bo')}
    del _L3_attn_all

    def _L3_ffn_setup():
        import jax, jax.numpy as jnp
        import numpy as np
        E = 8
        K = 2
        CAP_RATIO = 1.05
        key = jax.random.key(seed)
        ks = jax.random.split(key, 4)
        B, S, D, H = (2, 512, 256, 1024)
        x = jax.random.normal(ks[0], (B, S, D), jnp.float32)
        Wg = jax.random.normal(ks[1], (E, D), jnp.float32) * 0.02
        W1 = jax.random.normal(ks[2], (E, D, H), jnp.float32) * 0.02
        b1 = jnp.zeros((E, H), jnp.float32)
        W2 = jax.random.normal(ks[3], (E, H, D), jnp.float32) * 0.02
        b2 = jnp.zeros((E, D), jnp.float32)
        return {'x': x, 'Wg': Wg, 'W1': W1, 'b1': b1, 'W2': W2, 'b2': b2}
    _L3_ffn_all = _L3_ffn_setup()
    _L3_ffn_in = {k: v for k, v in _L3_ffn_all.items() if k in ('Wg', 'W1', 'b1', 'W2', 'b2')}
    del _L3_ffn_all
    return {'x': x, 'ctx_1024': ctx_1024, 'mask_BxSxS2_ff0': mask_BxSxS2_ff0, 'mask_BxS2_if0': mask_BxS2_if0, 'mask_BxS2_bf0': mask_BxS2_bf0, 'L0_xattn_ln_g': _L0_xattn_in['ln_g'], 'L0_xattn_ln_b': _L0_xattn_in['ln_b'], 'L0_xattn_cln_g': _L0_xattn_in['cln_g'], 'L0_xattn_cln_b': _L0_xattn_in['cln_b'], 'L0_xattn_Wq': _L0_xattn_in['Wq'], 'L0_xattn_Wkv': _L0_xattn_in['Wkv'], 'L0_xattn_Wout': _L0_xattn_in['Wout'], 'L0_xattn_W1': _L0_xattn_in['W1'], 'L0_xattn_W2': _L0_xattn_in['W2'], 'L0_attn_w_qkv': _L0_attn_in['w_qkv'], 'L0_attn_w_fc': _L0_attn_in['w_fc'], 'L0_attn_b_fc': _L0_attn_in['b_fc'], 'L0_attn_gamma': _L0_attn_in['gamma'], 'L0_attn_beta': _L0_attn_in['beta'], 'L0_ffn_gate_w': _L0_ffn_in['gate_w'], 'L0_ffn_c_fc': _L0_ffn_in['c_fc'], 'L0_ffn_fc_bias': _L0_ffn_in['fc_bias'], 'L0_ffn_c_proj': _L0_ffn_in['c_proj'], 'L0_ffn_proj_bias': _L0_ffn_in['proj_bias'], 'L1_xattn_W': _L1_xattn_in['W'], 'L1_xattn_b': _L1_xattn_in['b'], 'L1_attn_wq': _L1_attn_in['wq'], 'L1_attn_wk_a': _L1_attn_in['wk_a'], 'L1_attn_wk_b': _L1_attn_in['wk_b'], 'L1_attn_wv_a': _L1_attn_in['wv_a'], 'L1_attn_wv_b': _L1_attn_in['wv_b'], 'L1_attn_wo': _L1_attn_in['wo'], 'L1_ffn_ln1_w': _L1_ffn_in['ln1_w'], 'L1_ffn_ln1_b': _L1_ffn_in['ln1_b'], 'L1_ffn_w1': _L1_ffn_in['w1'], 'L1_ffn_b1': _L1_ffn_in['b1'], 'L1_ffn_ln2_w': _L1_ffn_in['ln2_w'], 'L1_ffn_ln2_b': _L1_ffn_in['ln2_b'], 'L1_ffn_w2': _L1_ffn_in['w2'], 'L1_ffn_b2': _L1_ffn_in['b2'], 'L2_xattn_Wq': _L2_xattn_in['Wq'], 'L2_xattn_bq': _L2_xattn_in['bq'], 'L2_xattn_Wk': _L2_xattn_in['Wk'], 'L2_xattn_bk': _L2_xattn_in['bk'], 'L2_xattn_Wv': _L2_xattn_in['Wv'], 'L2_xattn_bv': _L2_xattn_in['bv'], 'L2_xattn_Wo': _L2_xattn_in['Wo'], 'L2_xattn_bo': _L2_xattn_in['bo'], 'L2_attn_k': _L2_attn_in['k'], 'L2_attn_v': _L2_attn_in['v'], 'L2_ffn_Wg': _L2_ffn_in['Wg'], 'L2_ffn_W1': _L2_ffn_in['W1'], 'L2_ffn_b1': _L2_ffn_in['b1'], 'L2_ffn_W2': _L2_ffn_in['W2'], 'L2_ffn_b2': _L2_ffn_in['b2'], 'L3_xattn_Wq': _L3_xattn_in['Wq'], 'L3_xattn_bq': _L3_xattn_in['bq'], 'L3_xattn_Wo': _L3_xattn_in['Wo'], 'L3_xattn_bo': _L3_xattn_in['bo'], 'L3_attn_Wi': _L3_attn_in['Wi'], 'L3_attn_bi': _L3_attn_in['bi'], 'L3_attn_conv_w': _L3_attn_in['conv_w'], 'L3_attn_conv_b': _L3_attn_in['conv_b'], 'L3_attn_Wp': _L3_attn_in['Wp'], 'L3_attn_bp': _L3_attn_in['bp'], 'L3_attn_Wh': _L3_attn_in['Wh'], 'L3_attn_bh': _L3_attn_in['bh'], 'L3_attn_Wq': _L3_attn_in['Wq'], 'L3_attn_bq': _L3_attn_in['bq'], 'L3_attn_Wk': _L3_attn_in['Wk'], 'L3_attn_bk': _L3_attn_in['bk'], 'L3_attn_Wv': _L3_attn_in['Wv'], 'L3_attn_bv': _L3_attn_in['bv'], 'L3_attn_W1': _L3_attn_in['W1'], 'L3_attn_b1': _L3_attn_in['b1'], 'L3_attn_W2': _L3_attn_in['W2'], 'L3_attn_b2': _L3_attn_in['b2'], 'L3_attn_Wo': _L3_attn_in['Wo'], 'L3_attn_bo': _L3_attn_in['bo'], 'L3_ffn_Wg': _L3_ffn_in['Wg'], 'L3_ffn_W1': _L3_ffn_in['W1'], 'L3_ffn_b1': _L3_ffn_in['b1'], 'L3_ffn_W2': _L3_ffn_in['W2'], 'L3_ffn_b2': _L3_ffn_in['b2']}

def reference(x, ctx_1024, mask_BxSxS2_ff0, mask_BxS2_if0, mask_BxS2_bf0, L0_xattn_ln_g, L0_xattn_ln_b, L0_xattn_cln_g, L0_xattn_cln_b, L0_xattn_Wq, L0_xattn_Wkv, L0_xattn_Wout, L0_xattn_W1, L0_xattn_W2, L0_attn_w_qkv, L0_attn_w_fc, L0_attn_b_fc, L0_attn_gamma, L0_attn_beta, L0_ffn_gate_w, L0_ffn_c_fc, L0_ffn_fc_bias, L0_ffn_c_proj, L0_ffn_proj_bias, L1_xattn_W, L1_xattn_b, L1_attn_wq, L1_attn_wk_a, L1_attn_wk_b, L1_attn_wv_a, L1_attn_wv_b, L1_attn_wo, L1_ffn_ln1_w, L1_ffn_ln1_b, L1_ffn_w1, L1_ffn_b1, L1_ffn_ln2_w, L1_ffn_ln2_b, L1_ffn_w2, L1_ffn_b2, L2_xattn_Wq, L2_xattn_bq, L2_xattn_Wk, L2_xattn_bk, L2_xattn_Wv, L2_xattn_bv, L2_xattn_Wo, L2_xattn_bo, L2_attn_k, L2_attn_v, L2_ffn_Wg, L2_ffn_W1, L2_ffn_b1, L2_ffn_W2, L2_ffn_b2, L3_xattn_Wq, L3_xattn_bq, L3_xattn_Wo, L3_xattn_bo, L3_attn_Wi, L3_attn_bi, L3_attn_conv_w, L3_attn_conv_b, L3_attn_Wp, L3_attn_bp, L3_attn_Wh, L3_attn_bh, L3_attn_Wq, L3_attn_bq, L3_attn_Wk, L3_attn_bk, L3_attn_Wv, L3_attn_bv, L3_attn_W1, L3_attn_b1, L3_attn_W2, L3_attn_b2, L3_attn_Wo, L3_attn_bo, L3_ffn_Wg, L3_ffn_W1, L3_ffn_b1, L3_ffn_W2, L3_ffn_b2):
    import jax
    import jax.numpy as jnp

    def _L0_xattn_ref(x, context, mask, ln_g, ln_b, cln_g, cln_b, Wq, Wkv, Wout, W1, W2):
        import jax, jax.numpy as jnp
        import numpy as np
        DIM = 256
        CTX_DIM = 256
        HEADS = 16
        DIM_HEAD = 64
        INNER = HEADS * DIM_HEAD
        FF_INNER = 4 * DIM
        EPS = 1e-05

        def layer_norm(x, g, b):
            mu = jnp.mean(x, axis=-1, keepdims=True)
            var = jnp.var(x, axis=-1, keepdims=True)
            return (x - mu) * jax.lax.rsqrt(var + EPS) * g + b
        scale = DIM_HEAD ** (-0.5)
        xn = layer_norm(x, ln_g, ln_b)
        cn = layer_norm(context, cln_g, cln_b)
        b, n, _ = xn.shape
        q = (xn @ Wq).reshape(b, n, HEADS, DIM_HEAD).transpose(0, 2, 1, 3) * scale
        kv = cn @ Wkv
        k, v = jnp.split(kv, 2, axis=-1)
        sim = jnp.einsum('bhid,bjd->bhij', q, k) + mask[:, None, :, :]
        attn = jax.nn.softmax(sim, axis=-1)
        out = jnp.einsum('bhij,bjd->bhid', attn, v)
        out = out.transpose(0, 2, 1, 3).reshape(b, n, INNER) @ Wout
        h = xn @ W1
        val, gate = jnp.split(h, 2, axis=-1)
        out = out + jax.nn.silu(gate) * val @ W2
        return out

    def _L0_attn_ref(x, w_qkv, w_fc, b_fc, gamma, beta):
        import jax, jax.numpy as jnp
        import numpy as np
        DIM = 256
        B, S = (8, 512)
        LN_EPS = 1e-05
        scaling = DIM ** (-0.5)
        qkv = jnp.einsum('bsd,ed->bse', x, w_qkv)
        q, k, v = jnp.split(qkv, 3, axis=-1)
        att = jax.nn.softmax(jnp.einsum('bqd,bkd->bqk', q, k) * scaling, axis=-1)
        y = jnp.einsum('bqk,bvd->bqd', att, v)
        y = jnp.einsum('bqd,ed->bqe', y, w_fc) + b_fc
        h = x + y
        mu = jnp.mean(h, axis=-1, keepdims=True)
        var = jnp.var(h, axis=-1, keepdims=True)
        return (h - mu) * jax.lax.rsqrt(var + LN_EPS) * gamma + beta

    def _L0_ffn_ref(x, gate_w, c_fc, fc_bias, c_proj, proj_bias):
        import jax, jax.numpy as jnp
        import numpy as np
        N_EXP = 8
        TOP_K = 2
        CAPACITY_FACTOR = 1.25
        B, T, D = x.shape
        n = B * T
        E, k = (N_EXP, TOP_K)
        cap = int(CAPACITY_FACTOR * n * k / E)
        xt = x.reshape(n, D)
        logits = xt @ gate_w
        top_logits, top_idx = jax.lax.top_k(logits, k)
        masked = jnp.full_like(logits, -jnp.inf)
        masked = masked.at[jnp.arange(n)[:, None], top_idx].set(top_logits)
        router_probs = jax.nn.softmax(masked, axis=-1)
        exp_mask = jax.nn.one_hot(top_idx, E, dtype=jnp.int32)
        exp_mask = jnp.transpose(exp_mask, (1, 0, 2))
        exp_rank = jnp.cumsum(exp_mask.reshape(k * n, E), axis=0) - 1
        exp_rank = exp_rank.reshape(k, n, E)
        exp_mask = exp_mask * (exp_rank < cap).astype(jnp.int32)
        used_capacity = jnp.sum(exp_mask, axis=(0, 1))
        exp_rank = jnp.sum(exp_mask * exp_rank, axis=-1)
        exp_weights = exp_mask.astype(x.dtype) * router_probs[None]
        rank_oh = jax.nn.one_hot(exp_rank, cap, dtype=x.dtype)
        cb_weight = jnp.einsum('kne,knc->nec', exp_weights, rank_oh)
        sec_mask = (cb_weight != 0).astype(x.dtype)
        exp_batches = jnp.einsum('nec,nd->ecd', sec_mask, xt)
        h = jnp.einsum('ecd,edh->ech', exp_batches, c_fc) + fc_bias
        h = jax.nn.gelu(h, approximate=False)
        exp_out = jnp.einsum('ech,ehd->ecd', h, c_proj) + proj_bias
        out = jnp.einsum('nec,ecd->nd', cb_weight, exp_out)
        return out.reshape(B, T, D)

    def _L1_xattn_ref(q, k, v, W, b, mask):
        import jax, jax.numpy as jnp
        import numpy as np
        HEAD_NUM = 16
        NEG_INF = float('-inf')
        B, Sq, D = q.shape
        Sk = k.shape[1]
        H = HEAD_NUM
        dh = D // H
        qh = q.reshape(B, Sq, H, dh).transpose(0, 2, 1, 3)
        kh = k.reshape(B, Sk, H, dh).transpose(0, 2, 1, 3)
        vh = v.reshape(B, Sk, H, dh).transpose(0, 2, 1, 3)
        scores = jnp.einsum('bhqd,bhkd->bhqk', qh, kh) / jnp.sqrt(jnp.asarray(dh, q.dtype))
        pad = mask[:, None, None, :]
        causal = jnp.triu(jnp.ones((Sq, Sk), dtype=jnp.int32), k=1)[None, None]
        merged = jnp.where(causal == 1, causal, pad)
        scores = jnp.where(merged == 1, NEG_INF, scores)
        attn = jax.nn.softmax(scores, axis=-1)
        out = jnp.einsum('bhqk,bhkd->bhqd', attn, vh)
        out = out.transpose(0, 2, 1, 3).reshape(B, Sq, D)
        return out @ W.T + b

    def _L1_attn_ref(x, wq, wk_a, wk_b, wv_a, wv_b, wo):
        import jax, jax.numpy as jnp
        import numpy as np
        DIM = 256
        NH = 16
        HD = DIM // NH
        DROPE = 16
        MAXSEQ = 512
        LAT = 64
        BATCH = 2
        SEQ = 512

        def _rope_freqs(max_seq, head_dim):
            inv = 1.0 / 10000.0 ** (jnp.arange(0, head_dim, 2, dtype=jnp.float32) / head_dim)
            ang = jnp.arange(max_seq, dtype=jnp.float32)[:, None] * inv[None, :]
            return (jnp.cos(ang), jnp.sin(ang))

        def _apply_decoupled_rope(x, cosf, sinf, d_rope):
            b, d1, d2, hd = x.shape
            half = d_rope // 2
            xr = x[..., :d_rope].astype(jnp.float32).reshape(b, d1, d2, half, 2)
            xa, xb = (xr[..., 0], xr[..., 1])
            c = cosf[:d1, :half][None, :, None, :]
            s = sinf[:d1, :half][None, :, None, :]
            rot = jnp.stack([xa * c - xb * s, xa * s + xb * c], axis=-1)
            rot = rot.reshape(b, d1, d2, d_rope)
            return jnp.concatenate([rot, x[..., d_rope:]], axis=-1)
        b, s, _ = x.shape
        q = (x @ wq.T).reshape(b, s, NH, HD).transpose(0, 2, 1, 3)
        k = (x @ wk_a.T @ wk_b.T).reshape(b, s, NH, HD).transpose(0, 2, 1, 3)
        v = (x @ wv_a.T @ wv_b.T).reshape(b, s, NH, HD).transpose(0, 2, 1, 3)
        cosf, sinf = _rope_freqs(MAXSEQ, HD)
        q = _apply_decoupled_rope(q, cosf, sinf, DROPE)
        k = _apply_decoupled_rope(k, cosf, sinf, DROPE)
        scores = jnp.einsum('bhqd,bhkd->bhqk', q, k) / np.float32(np.sqrt(HD))
        attn = jax.nn.softmax(scores, axis=-1)
        out = jnp.einsum('bhqk,bhkd->bhqd', attn, v)
        out = out.transpose(0, 2, 1, 3).reshape(b, s, NH * HD)
        return out @ wo.T

    def _L1_ffn_ref(x, ln1_w, ln1_b, w1, b1, ln2_w, ln2_b, w2, b2):
        import jax, jax.numpy as jnp
        import numpy as np
        EPS = 1e-05

        def layernorm(x, w, b):
            mu = jnp.mean(x, axis=-1, keepdims=True)
            var = jnp.mean(jnp.square(x - mu), axis=-1, keepdims=True)
            return (x - mu) * jax.lax.rsqrt(var + EPS) * w + b

        def act_quant_fake(x):
            scale = 127.0 / jnp.clip(jnp.max(jnp.abs(x), axis=-1, keepdims=True), EPS, None)
            return jnp.clip(jnp.round(x * scale), -128.0, 127.0) / scale

        def weight_quant_fake(w):
            scale = 1.0 / jnp.clip(jnp.mean(jnp.abs(w)), EPS, None)
            return jnp.clip(jnp.round(w * scale), -1.0, 1.0) / scale

        def bitlinear(x, w, b):
            dqx = x + jax.lax.stop_gradient(act_quant_fake(x) - x)
            dqw = w + jax.lax.stop_gradient(weight_quant_fake(w) - w)
            return jnp.einsum('btd,hd->bth', dqx, dqw) + b
        h = layernorm(x, ln1_w, ln1_b)
        h = bitlinear(h, w1, b1)
        h = jax.nn.gelu(h, approximate=False)
        h = layernorm(h, ln2_w, ln2_b)
        out = bitlinear(h, w2, b2)
        return out

    def _L2_xattn_ref(query, key, value, mask, Wq, bq, Wk, bk, Wv, bv, Wo, bo):
        import jax, jax.numpy as jnp
        import numpy as np
        B, T, H, NH = (4, 512, 256, 16)
        DK = H // NH

        def _proj_heads(x, W, b):
            y = x @ W.T + b
            bsz, t, _ = y.shape
            return y.reshape(bsz, t, NH, DK).transpose(0, 2, 1, 3)
        q = _proj_heads(query, Wq, bq)
        k = _proj_heads(key, Wk, bk)
        v = _proj_heads(value, Wv, bv)
        scores = jnp.einsum('bhqd,bhkd->bhqk', q, k) / jnp.sqrt(jnp.asarray(DK, q.dtype))
        scores = jnp.where(mask[:, None, None, :], jnp.asarray(-1000000000.0, scores.dtype), scores)
        p_attn = jax.nn.softmax(scores, axis=-1)
        ctx = jnp.einsum('bhqk,bhkd->bhqd', p_attn, v)
        ctx = ctx.transpose(0, 2, 1, 3).reshape(query.shape[0], -1, NH * DK)
        return ctx @ Wo.T + bo

    def _L2_attn_ref(q, k, v):
        import jax, jax.numpy as jnp
        import numpy as np
        import math
        IN_FEATURES = 256
        OUT_FEATURES = 256
        N_BANK = 2048
        N_LAYER = 12
        N_EMBD = 256
        scores = jnp.einsum('btd,nd->btn', q, k)
        sqrt_n = jnp.sqrt(jnp.asarray(scores.shape[-1], scores.dtype))
        norm = jnp.linalg.norm(scores, axis=-1, keepdims=True)
        gated = jax.nn.gelu(scores / norm * sqrt_n, approximate=False)
        return jnp.einsum('btn,no->bto', gated, v)

    def _L2_ffn_ref(x, Wg, W1, b1, W2, b2):
        import jax, jax.numpy as jnp
        import numpy as np
        HIDDEN = 256
        INTER = 1024
        N_EXPERTS = 8
        TOP_K = 2
        INIT_STD = 0.02
        orig_shape = x.shape
        xt = x.reshape(-1, HIDDEN)
        T = xt.shape[0]
        logits = xt @ Wg.T
        topk_logits, topk_idx = jax.lax.top_k(logits, TOP_K)
        w = jax.nn.softmax(topk_logits, axis=-1)
        rows = jnp.arange(T)[:, None]
        gates = jnp.zeros((T, N_EXPERTS), xt.dtype).at[rows, topk_idx].add(w)
        h = jnp.einsum('th,ehi->tei', xt, W1) + b1
        h = jax.nn.gelu(h, approximate=False)
        o = jnp.einsum('tei,eih->teh', h, W2) + b2
        y = jnp.einsum('te,teh->th', gates, o)
        return y.reshape(orig_shape)

    def _L3_xattn_ref(query, key, value, Wq, bq, Wo, bo):
        import jax, jax.numpy as jnp
        import numpy as np
        D_MODEL = 256
        SCALE = 1.0 / np.sqrt(D_MODEL).astype(np.float32)
        q = query @ Wq + bq
        k = key @ Wq + bq
        v = value @ Wq + bq
        scores = jnp.einsum('bqd,bkd->bqk', q, k) * SCALE
        attn = jax.nn.softmax(scores, axis=-1)
        f = jnp.einsum('bqk,bkd->bqd', attn, v)
        return f @ Wo + bo

    def _L3_attn_ref(x, Wi, bi, conv_w, conv_b, Wp, bp, Wh, bh, Wq, bq, Wk, bk, Wv, bv, W1, b1, W2, b2, Wo, bo):
        import math
        import jax, jax.numpy as jnp
        import numpy as np
        B, S = (4, 512)
        D_MODEL, D_STATE = (256, 64)
        KSIZE, CHUNK, STEPS = (5, 16, 2)
        TOPK, LOOKBACK = (8, 64)

        def _forward(x, Wi, bi, conv_w, conv_b, Wp, bp, Wh, bh, Wq, bq, Wk, bk, Wv, bv, W1, b1, W2, b2, Wo, bo):
            bsz, seq, _ = x.shape
            dim = Wi.shape[1]
            h = x @ Wi + bi
            pos = jnp.arange(seq)[:, None] + jnp.arange(LOOKBACK)[None, :]
            valid = pos - LOOKBACK >= 0
            cidx = jnp.arange(seq)[:, None] + jnp.arange(KSIZE)[None, :]
            scale = 1.0 / math.sqrt(dim)
            for _ in range(STEPS):
                hp = jnp.pad(h, ((0, 0), (KSIZE - 1, 0), (0, 0)))
                mixed = jnp.einsum('bskd,kd->bsd', hp[:, cidx, :], conv_w) + conv_b
                ph = h.reshape(bsz, seq // CHUNK, CHUNK, dim).mean(axis=2)
                pb = jnp.repeat(ph @ Wp + bp, CHUNK, axis=1)
                q = h @ Wq + bq
                k = h @ Wk + bk
                v = h @ Wv + bv
                kp = jnp.pad(k, ((0, 0), (LOOKBACK, 0), (0, 0)))
                scores = jnp.einsum('bsd,bsld->bsl', q, kp[:, pos, :]) * scale
                scores = jnp.where(valid[None], scores, -jnp.inf)
                ts, tr = jax.lax.top_k(scores, TOPK)
                m = ts.max(axis=-1, keepdims=True)
                e = jnp.exp(ts - jnp.where(jnp.isfinite(m), m, 0.0))
                w = e / jnp.maximum(e.sum(axis=-1, keepdims=True), 1e-30)
                tok = jnp.clip(jnp.arange(seq)[None, :, None] - LOOKBACK + tr, 0, seq - 1)
                vg = jnp.take_along_axis(v, tok.reshape(bsz, seq * TOPK, 1), axis=1).reshape(bsz, seq, TOPK, dim)
                summ = jnp.einsum('bsk,bskd->bsd', w, vg)
                ui = jnp.concatenate([h, mixed, pb, summ], axis=-1)
                delta = jnp.tanh(ui @ W1 + b1) @ W2 + b2
                gate = jax.nn.sigmoid(h @ Wh + bh)[..., 2:3]
                h = h + delta * gate
            return x + (h @ Wo + bo)
        return _forward(x, Wi, bi, conv_w, conv_b, Wp, bp, Wh, bh, Wq, bq, Wk, bk, Wv, bv, W1, b1, W2, b2, Wo, bo)

    def _L3_ffn_ref(x, Wg, W1, b1, W2, b2):
        import jax, jax.numpy as jnp
        import numpy as np
        E = 8
        K = 2
        CAP_RATIO = 1.05
        B, S, D = x.shape
        T = B * S
        xf = x.reshape(T, D)
        gates = jax.nn.softmax(xf @ Wg.T, axis=-1)
        topw, topi = jax.lax.top_k(gates, K)
        C = int(round(K * T * CAP_RATIO / E))
        e_ord = topi.T.reshape(-1)
        tok_ord = jnp.tile(jnp.arange(T), K)
        oh = jax.nn.one_hot(e_ord, E, dtype=jnp.int32)
        cnt = jnp.take_along_axis(jnp.cumsum(oh, 0) - oh, e_ord[:, None], 1)[:, 0]
        within = cnt < C
        pos = jnp.where(within, cnt, C)
        x_disp = xf[tok_ord]
        buf = jnp.zeros((E, C + 1, D), xf.dtype).at[e_ord, pos].add(x_disp)[:, :C]
        h = jax.nn.gelu(jnp.einsum('ecd,edh->ech', buf, W1) + b1[:, None, :], approximate=False)
        y = jnp.einsum('ech,ehd->ecd', h, W2) + b2[:, None, :]
        y_ord = y[e_ord, jnp.minimum(pos, C - 1)] * within[:, None].astype(y.dtype)
        y_tk = y_ord.reshape(K, T, D).transpose(1, 0, 2)
        cw = topw * within.reshape(K, T).T.astype(topw.dtype)
        out = jnp.einsum('tk,tkd->td', cw, y_tk)
        return out.reshape(B, S, D)
    x = x + _L0_xattn_ref(_layernorm(x, axis=-1), ctx_1024, mask_BxSxS2_ff0, L0_xattn_ln_g, L0_xattn_ln_b, L0_xattn_cln_g, L0_xattn_cln_b, L0_xattn_Wq, L0_xattn_Wkv, L0_xattn_Wout, L0_xattn_W1, L0_xattn_W2)
    x = x + _L0_attn_ref(_layernorm(x, axis=-1), L0_attn_w_qkv, L0_attn_w_fc, L0_attn_b_fc, L0_attn_gamma, L0_attn_beta)
    x = x + _L0_ffn_ref(_layernorm(x, axis=-1), L0_ffn_gate_w, L0_ffn_c_fc, L0_ffn_fc_bias, L0_ffn_c_proj, L0_ffn_proj_bias)
    x = x + _L1_xattn_ref(_layernorm(x, axis=-1), ctx_1024, ctx_1024, L1_xattn_W, L1_xattn_b, mask_BxS2_if0)
    x = x + _L1_attn_ref(_layernorm(x, axis=-1), L1_attn_wq, L1_attn_wk_a, L1_attn_wk_b, L1_attn_wv_a, L1_attn_wv_b, L1_attn_wo)
    x = x + _L1_ffn_ref(_layernorm(x, axis=-1), L1_ffn_ln1_w, L1_ffn_ln1_b, L1_ffn_w1, L1_ffn_b1, L1_ffn_ln2_w, L1_ffn_ln2_b, L1_ffn_w2, L1_ffn_b2)
    x = x + _L2_xattn_ref(_layernorm(x, axis=-1), ctx_1024, ctx_1024, mask_BxS2_bf0, L2_xattn_Wq, L2_xattn_bq, L2_xattn_Wk, L2_xattn_bk, L2_xattn_Wv, L2_xattn_bv, L2_xattn_Wo, L2_xattn_bo)
    x = x + _L2_attn_ref(_layernorm(x, axis=-1), L2_attn_k, L2_attn_v)
    x = x + _L2_ffn_ref(_layernorm(x, axis=-1), L2_ffn_Wg, L2_ffn_W1, L2_ffn_b1, L2_ffn_W2, L2_ffn_b2)
    x = x + _L3_xattn_ref(_layernorm(x, axis=-1), ctx_1024, ctx_1024, L3_xattn_Wq, L3_xattn_bq, L3_xattn_Wo, L3_xattn_bo)
    x = x + _L3_attn_ref(_layernorm(x, axis=-1), L3_attn_Wi, L3_attn_bi, L3_attn_conv_w, L3_attn_conv_b, L3_attn_Wp, L3_attn_bp, L3_attn_Wh, L3_attn_bh, L3_attn_Wq, L3_attn_bq, L3_attn_Wk, L3_attn_bk, L3_attn_Wv, L3_attn_bv, L3_attn_W1, L3_attn_b1, L3_attn_W2, L3_attn_b2, L3_attn_Wo, L3_attn_bo)
    x = x + _L3_ffn_ref(_layernorm(x, axis=-1), L3_ffn_Wg, L3_ffn_W1, L3_ffn_b1, L3_ffn_W2, L3_ffn_b2)
    return x

_drawn_inputs = setup_inputs


def setup_inputs(seed=0):
    import zlib

    import numpy as np

    out = dict(_drawn_inputs(seed))
    spreads = {'L0_xattn_ln_g': (1.0, 0.6),
     'L0_xattn_ln_b': (0.0, 0.652),
     'L0_xattn_cln_g': (1.0, 0.2),
     'L0_xattn_cln_b': (0.0, 0.1),
     'L0_attn_b_fc': (0.0, 0.488),
     'L0_attn_gamma': (1.0, 0.2),
     'L0_attn_beta': (0.0, 0.1),
     'L0_ffn_fc_bias': (0.0, 0.408),
     'L0_ffn_proj_bias': (0.0, 0.1),
     'L1_xattn_b': (0.0, 0.1),
     'L1_ffn_ln1_w': (1.0, 0.2),
     'L1_ffn_ln1_b': (0.0, 0.1),
     'L1_ffn_ln2_w': (1.0, 0.2),
     'L1_ffn_ln2_b': (0.0, 0.1),
     'L2_ffn_b1': (0.0, 0.661),
     'L2_ffn_b2': (0.0, 0.1),
     'L3_attn_bi': (0.0, 0.8),
     'L3_attn_conv_b': (0.0, 0.8),
     'L3_attn_bp': (0.0, 0.8),
     'L3_attn_bh': (0.0, 0.8),
     'L3_attn_bq': (0.0, 0.8),
     'L3_attn_bk': (0.0, 0.8),
     'L3_attn_bv': (0.0, 0.8),
     'L3_attn_b1': (0.0, 0.8),
     'L3_attn_b2': (0.0, 0.8),
     'L3_attn_bo': (0.0, 0.1),
     'L3_ffn_b1': (0.0, 0.8),
     'L3_ffn_b2': (0.0, 0.8)}
    factors = {'L0_xattn_Wq': 6.619,
     'L1_ffn_b1': 5.748,
     'L1_ffn_b2': 8.0,
     'L2_xattn_bq': 6.922,
     'L2_xattn_bk': 8.0,
     'L3_xattn_bq': 8.0,
     'L3_xattn_bo': 8.0,
     'L3_attn_Wi': 7.246,
     'L3_attn_conv_w': 8.0,
     'L3_attn_Wp': 8.0,
     'L3_attn_Wh': 8.0,
     'L3_attn_Wq': 8.0,
     'L3_attn_Wk': 8.0,
     'L3_attn_Wv': 8.0,
     'L3_attn_W1': 8.0,
     'L3_attn_W2': 8.0,
     'L3_attn_Wo': 7.437,
     'L3_ffn_Wg': 5.342,
     'L3_ffn_W1': 6.517,
     'L3_ffn_W2': 6.094}
    for name, (base, spread) in spreads.items():
        noise = np.random.default_rng([zlib.crc32(name.encode()), seed]).standard_normal(out[name].shape)
        drawn = base * np.exp(spread * noise) if base else spread * noise
        out[name] = jnp.asarray(drawn.astype(out[name].dtype))
    for name, factor in factors.items():
        out[name] = (out[name] * factor).astype(out[name].dtype)
    return out
```

```python
from contextlib import ExitStack

import concourse.bass as bass
from concourse import mybir

ALU = mybir.AluOpType
ACT = mybir.ActivationFunctionType
F32 = mybir.dt.float32
BF16 = mybir.dt.bfloat16
I32 = mybir.dt.int32
U32 = mybir.dt.uint32
AX = mybir.AxisListType.X

P = 128
BATCH, SEQ, KEYS, D = 16, 64, 256, 256
TOKENS = BATCH * SEQ
TILES = TOKENS // P
DC = D // P
HEADS, DH = 16, 16
PAIRS = HEADS // 2
EXPERTS, HID = 8, 1024
HB = HID // P
HALF = 512
STATE, KSIZE, CHUNK = 64, 5, 16
EPS = 1e-5
ROUND = 1.5 * 2.0 ** 23
FAR = -1e30
TAKEN = -3e38

CONSTS = [
    ("ident", P, (P,)), ("tri", P, (P,)), ("ones", P, (P,)), ("batch_ones", P, (P,)),
    ("headmask", P, (8,)), ("causal", P, (SEQ,)), ("strict", P, (SEQ,)), ("experts", P, (EXPERTS,)),
    ("rope", P, (DC, P)),
]
PARAMS_A = [
    ("l0x_wk", P, (DC, P)), ("l0x_wv", P, (DC, 64)), ("l0x_wq", P, (DC, 1024)), ("l0x_w1", P, (DC, 2048)),
    ("l0x_wout", P, (8, D)), ("l0x_w2", P, (8, D)), ("l0x_ln_g", P, (D,)), ("l0x_ln_b", P, (D,)),
    ("l0x_cln_g", P, (D,)), ("l0x_cln_b", P, (D,)),
    ("l0a_wqkv", P, (DC, 3 * D)), ("l0a_wfc", P, (DC, D)), ("l0a_bfc", P, (D,)), ("l0a_gamma", P, (D,)),
    ("l0a_beta", P, (D,)),
]
PARAMS_B = [
    ("l1x_w", P, (DC, D)), ("l1x_b", P, (D,)),
    ("l1a_wq", P, (DC, D)), ("l1a_wka", P, (DC, 64)), ("l1a_wkb", P, (DC, 64)), ("l1a_wva", P, (DC, 64)),
    ("l1a_wvb", 64, (D,)), ("l1a_wo", P, (DC, D)),
    ("l1f_ln1_w", P, (D,)), ("l1f_ln1_b", P, (D,)), ("l1f_b1", P, (HID,)),
    ("l1f_ln2_w", P, (HID,)), ("l1f_ln2_b", P, (HID,)), ("l1f_b2", P, (D,)),
    ("l2x_wq", P, (DC, D)), ("l2x_wk", P, (DC, D)), ("l2x_wv", P, (DC, D)), ("l2x_wo", P, (DC, D)),
    ("l2x_bq", P, (DC,)), ("l2x_bk", P, (DC,)), ("l2x_bv", P, (D,)), ("l2x_bo", P, (D,)),
    ("l2a_k", P, (DC, 2048)), ("l2a_v", P, (16, D)),
]
BITNET = [("l1f_w1", P, (DC, HID)), ("l1f_w2", P, (HB, D))]
PARAMS_C = [
    ("l3x_wq", P, (DC, 64)), ("l3x_bq", P, (64,)), ("l3x_bqc", 64, (1,)), ("l3x_wo", 64, (D,)), ("l3x_bo", P, (D,)),
    ("l3a_wi", P, (DC, 64)), ("l3a_bi", 64, (1,)), ("l3a_conv", 64, (KSIZE,)), ("l3a_convb", 64, (1,)),
    ("l3a_wp", 64, (64,)), ("l3a_bp", 64, (1,)), ("l3a_wh", 64, (64,)), ("l3a_bh", 64, (1,)),
    ("l3a_wq", 64, (64,)), ("l3a_bq", 64, (1,)), ("l3a_wk", 64, (64,)), ("l3a_bk", 64, (1,)),
    ("l3a_wv", 64, (64,)), ("l3a_bv", 64, (64,)), ("l3a_w1", 64, (4, 64)), ("l3a_b1", 64, (1,)),
    ("l3a_w2", 64, (64,)), ("l3a_b2", 64, (1,)), ("l3a_wo", 64, (D,)), ("l3a_bo", P, (D,)),
]
ROUTER = [("gate_w", P, (DC, EXPERTS)), ("b1", P, (EXPERTS, HB)), ("b2", EXPERTS, (D,))]


def length(shape):
    n = 1
    for s in shape:
        n *= s
    return n


def width(params):
    return sum(length(s) for _, _, s in params)


def view(region, at, shape, parts=P):
    flat = region[0:parts, at:at + length(shape)]
    if len(shape) == 2:
        return flat.rearrange("p (a b) -> p a b", b=shape[1])
    if len(shape) == 3:
        return flat.rearrange("p (a b c) -> p a b c", b=shape[1], c=shape[2])
    return flat


def views(region, params):
    at, out = 0, {}
    for name, parts, shape in params:
        out[name] = view(region, at, shape, parts)
        at += length(shape)
    return out


class Work:

    def __init__(self, region):
        self.region, self.at = region, 0

    def __call__(self, *shape, parts=P):
        out = view(self.region, self.at, shape, parts)
        self.at += length(shape)
        assert self.at <= self.region.shape[1], self.at
        return out


class Chain:

    def __init__(self, eng, sem):
        self.eng, self.sem, self.n = eng, sem, 0

    def go(self, ins):
        ins.then_inc(self.sem, 1)
        self.n += 1

    def settle(self):
        self.eng.wait_ge(self.sem, self.n)

    def do(self, ins):
        self.go(ins)
        self.settle()


class Signals:

    def __init__(self, nc, ctx, count):
        self.free = [ctx.enter_context(nc.semaphore(f"signal{n}")) for n in range(count)]
        self.all = range(self.free[0].num, self.free[-1].num + 1)
        self.named = {}

    def __call__(self, name):
        if name not in self.named:
            self.named[name] = self.free[len(self.named)]
        return self.named[name]

    def forget(self):
        self.named = {}


def perceiver_kernel(nc, dram, out):
    with ExitStack() as ctx:
        build(nc, ctx, dram, out)


def build(nc, ctx, dram, out):
    def sb(name, shape, dt=F32):
        return ctx.enter_context(nc.sbuf_tensor(name, shape, dt))

    X = sb("X", [P, TILES, D])
    XNT_ALL = sb("XNT_all", [P, DC, TOKENS])
    CONST = sb("constants", [P, width(CONSTS)])
    PARAM = sb("params", [P, max(width(PARAMS_A), width(PARAMS_B), width(PARAMS_C))])
    W1Q = sb("w1_ternary", [P, DC, HID], BF16)
    W2Q = sb("w2_ternary", [P, HB, D], BF16)
    IDB = sb("identity_bf16", [P, P], BF16)
    REGION = sb("work", [P, 16384])
    STATS = sb("bn_stats", [P, 4, 2, 6])
    MV = sb("mean_var", [P, 4, 2])
    VAR, RSTD, TMP = sb("var", [P, 4]), sb("rstd", [P, 4]), sb("newton", [P, 4])
    MAXES, SUMS, RECS = sb("maxes", [P, PAIRS]), sb("sums", [P, PAIRS]), sb("recs", [P, PAIRS])
    ONE = [sb(f"scalar{n}", [P, 1]) for n in range(8)]
    GATES = sb("gates", [P, TILES, EXPERTS])
    GATE_ROWS = sb("gate_rows", [EXPERTS, TILES, P])
    GATE = sb("gate_of_expert", [P, 2, TILES])
    BIAS = sb("bias_of_expert", [P, 2, HB])
    RT = sb("router_params", [P, width(ROUTER)])
    WSCALE = sb("ternary_scales", [P, 2])

    psS = ctx.enter_context(nc.psum_tensor("psS", [P, 2048], F32))
    psA = ctx.enter_context(nc.psum_tensor("psA", [P, 1024], F32))
    psO = ctx.enter_context(nc.psum_tensor("psO", [P, 1024], F32))

    K = views(CONST, CONSTS)
    R = views(RT, ROUTER)
    ident = K["ident"]
    S = Signals(nc, ctx, 150)

    def end():
        nc.all_engine_barrier(sems_to_clear=S.all)
        S.forget()

    def stacked(name, i):
        return dram[name][bass.ds(i * P, P), :]

    def rstd_of(c, n, var, eps):
        v, y, w = VAR[:, 0:n], RSTD[:, 0:n], TMP[:, 0:n]
        c.do(nc.vector.tensor_scalar(v, var, eps, None, ALU.add))
        c.do(nc.vector.tensor_scalar(y.bitcast(I32), v.bitcast(I32), 1, None, ALU.logical_shift_right))
        c.do(nc.vector.tensor_scalar(y.bitcast(I32), y.bitcast(I32), -1.0, float(0x5F3759DF), ALU.mult, ALU.add))
        for _ in range(3):
            c.do(nc.vector.tensor_tensor(w, y, y, ALU.mult))
            c.do(nc.vector.scalar_tensor_tensor(w, w, -0.5, v, ALU.mult, ALU.mult))
            c.do(nc.vector.scalar_tensor_tensor(y, w, 1.5, y, ALU.add, ALU.mult))

    def layer_norm(c, pairs):
        n = len(pairs)
        for j, (src, _) in enumerate(pairs):
            wide = src.shape[1]
            chunks = max(1, wide // 512)
            for k in range(chunks):
                c.go(nc.vector.bn_stats(STATS[:, j, k, :], src[:, k * wide // chunks:(k + 1) * wide // chunks]))
        c.settle()
        for j in range(n):
            c.go(nc.vector.bn_aggr(MV[:, j, :], STATS[:, j, 0:chunks, :].rearrange("p k s -> p (k s)")))
        c.settle()
        rstd_of(c, n, MV[:, 0:n, 1], EPS)
        for j, (src, dst) in enumerate(pairs):
            c.go(nc.vector.tensor_scalar(dst, src, MV[:, j, 0:1], RSTD[:, j:j + 1], ALU.subtract, ALU.mult))
        c.settle()

    def affine(c, x, g, b):
        c.do(nc.vector.tensor_tensor(x, x, g, ALU.mult))
        c.do(nc.vector.tensor_tensor(x, x, b, ALU.add))

    def product(out_, lhsT, rhs, n):
        for i in range(n):
            last = nc.tensor.matmul(out_, lhsT(i), rhs(i), start=(i == 0), stop=(i == n - 1))
        return last

    def transpose_x_tensor(pe, tag, XN):
        pe.wait_ge(S(tag + " normed"), 1)
        for c in range(DC):
            last = nc.tensor.transpose(psA[:, c * P:(c + 1) * P], XN[:, c * P:(c + 1) * P], ident)
        last.then_inc(S(tag + " turned"), 1)

    def transpose_x_scalar(act, tag, XNT):
        act.wait_ge(S(tag + " turned"), 1)
        nc.scalar.copy(XNT.rearrange("p c t -> p (c t)"), psA[:, 0:D]).then_inc(S(tag + " xnT"), 1)

    def attention_tensor(pe, tag, nk, dv, query, key, value, heads, ready):
        kc = min(nk, P)
        nkc = nk // kc
        for name, count in ready:
            pe.wait_ge(S(name), count)
        for b in range(2):
            if b:
                pe.wait_ge(S(tag + " probsT"), b)
            for p in range(PAIRS):
                last = nc.tensor.matmul(psS[:, p * nk:(p + 1) * nk], query(b, p), key(b, p), start=True, stop=True)
            last.then_inc(S(tag + " scores"), 1)
            pe.wait_ge(S(tag + " probs"), b + 1)
            for i in range(PAIRS * nkc):
                last = nc.tensor.transpose(psS[0:kc, i * P:(i + 1) * P], PR[:, i * kc:(i + 1) * kc], ident)
            last.then_inc(S(tag + " probs turned"), 1)
            pe.wait_ge(S(tag + " probsT"), b + 1)
            for p in range(PAIRS):
                for s in range(2):
                    h = heads(p, s)
                    last = product(
                        psO[64 * b:64 * b + 64, h * dv:(h + 1) * dv],
                        lambda c: PT[0:kc, (p * nkc + c) * P + 64 * s:(p * nkc + c) * P + 64 * s + 64],
                        lambda c: value(b, c, h), nkc)
        last.then_inc(S(tag + " mixed"), 1)

    def attention_vector(dve, c, tag, nk, mask):
        for b in range(2):
            dve.wait_ge(S(tag + " scores"), b + 1)
            src = psS[:, 0:PAIRS * nk].rearrange("p (h k) -> p h k", k=nk)
            if mask is not None:
                sm = SM[:, 0:PAIRS * nk].rearrange("p (h k) -> p h k", k=nk)
                c.do(nc.vector.tensor_tensor(sm, src, mask(b).unsqueeze(1).broadcast_to([P, PAIRS, nk]), ALU.add))
                src = sm
            c.do(nc.vector.tensor_reduce(MAXES[:], src, AX, ALU.max))
            nc.vector.tensor_scalar(MAXES[:], MAXES[:], -1.0, None, ALU.mult).then_inc(S(tag + " max"), 1)
            dve.wait_ge(S(tag + " exp"), (b + 1) * PAIRS)
            c.do(nc.vector.reciprocal(RECS[:], SUMS[:]))
            pr = PR[:, 0:PAIRS * nk].rearrange("p (h k) -> p h k", k=nk)
            nc.vector.tensor_tensor(pr, pr, RECS[:].unsqueeze(2).broadcast_to([P, PAIRS, nk]), ALU.mult)\
                .then_inc(S(tag + " probs"), 1)

    def attention_scalar(act, tag, nk, mask):
        kc = min(nk, P)
        n = PAIRS * (nk // kc) * P
        src = psS if mask is None else SM
        for b in range(2):
            act.wait_ge(S(tag + " max"), b + 1)
            if b:
                act.wait_ge(S(tag + " probs turned"), b)
            for p in range(PAIRS):
                nc.scalar.activation(PR[:, p * nk:(p + 1) * nk], src[:, p * nk:(p + 1) * nk], ACT.Exp,
                                     bias=MAXES[:, p:p + 1], accum_out=SUMS[:, p:p + 1])\
                    .then_inc(S(tag + " exp"), 1)
            act.wait_ge(S(tag + " probs turned"), b + 1)
            nc.scalar.copy(PT[0:kc, 0:n], psS[0:kc, 0:n]).then_inc(S(tag + " probsT"), 1)

    def project_tensor(pe, tag, blocks, weight):
        pe.wait_ge(S(tag + " o"), 1)
        for i in range(blocks):
            last = nc.tensor.transpose(psS[:, i * P:(i + 1) * P], OO[:, i * P:(i + 1) * P], ident)
        last.then_inc(S(tag + " o turned"), 1)
        pe.wait_ge(S(tag + " oT"), 1)
        product(psA[:, 0:D], lambda i: OT[:, i * P:(i + 1) * P], lambda i: weight[:, i, :], blocks)\
            .then_inc(S(tag + " y"), 1)

    def project_scalar(act, tag, blocks):
        act.wait_ge(S(tag + " mixed"), 1)
        nc.scalar.copy(OO[:, 0:blocks * P], psO[:, 0:blocks * P]).then_inc(S(tag + " o"), 1)
        act.wait_ge(S(tag + " o turned"), 1)
        nc.scalar.copy(OT[:, 0:blocks * P], psS[:, 0:blocks * P]).then_inc(S(tag + " oT"), 1)

    def residual(dve, c, tag, bias):
        dve.wait_ge(S(tag + " y"), 1)
        c.do(nc.vector.tensor_tensor(XT, XT, psA[:, 0:D], ALU.add))
        if bias is not None:
            c.do(nc.vector.tensor_tensor(XT, XT, bias, ALU.add))

    def normed(c, tag, extra=None):
        layer_norm(c, [(XT, XN)])
        if extra:
            extra()
        nc.vector.tensor_copy(ONE[7][:], MV[:, 0, 0:1]).then_inc(S(tag + " normed"), 1)

    def to_experts_vector(dve, c, t):
        c.do(nc.vector.tensor_copy(X[:, bass.ds(t, 1), :], XT.unsqueeze(1)))
        normed(c, "router")
        dve.wait_ge(S("router turned"), 1)
        c.do(nc.vector.tensor_copy(XNT_ALL[:, :, bass.ds(t * P, P)], psA[:, 0:D].rearrange("p (c t) -> p c t", t=P)))

    def head_queries(c, src, tag):
        for blk in range(DC):
            for b in range(2):
                c.go(nc.vector.tensor_tensor(
                    QBD[:, 8 * (2 * blk + b):8 * (2 * blk + b) + 8, :],
                    src[:, blk, 64 * b:64 * b + 64].unsqueeze(1).broadcast_to([P, 8, SEQ]),
                    K["headmask"].unsqueeze(2).broadcast_to([P, 8, SEQ]), ALU.mult))
        c.settle()
        nc.vector.tensor_copy(ONE[6][:], MV[:, 0, 0:1]).then_inc(S(tag + " queries"), 1)

    def masked_query(b, p):
        at = 8 * (2 * (p // 4) + b) + 2 * (p % 4)
        return QBD[:, at:at + 2, :].rearrange("p h t -> p (h t)")

    def plain_heads(p, s):
        return 2 * p + s

    with nc.Block(no_gpsimd_drain=True) as block:
        @block.sync
        def _(sp):
            sp.dma_start(X[:], dram["x"]).then_inc(S("loaded"), 16)
            sp.dma_start(CONST[:], dram["consts"]).then_inc(S("loaded"), 16)
            sp.dma_start(PARAM[:, 0:width(PARAMS_A)], dram["params_a"]).then_inc(S("loaded"), 16)
            sp.wait_ge(S("loaded"), 48)
    end()

    A = views(PARAM, PARAMS_A)
    work = Work(REGION)
    XT, XN, XNT = work(D), work(D), work(DC, P)
    SM, PR, PT = work(2048), work(2048), work(2048)
    OO, OT = work(1024), work(1024)
    common = work.at
    CTX, CTXT = work(4, D), work(DC, 512)
    KT, V, QT = work(512), work(4, 64), work(2, 8, SEQ)
    MASK = work(2, KEYS)
    HH, HHT = work(1024), work(1024)
    V256 = HHT[:, 0:D]
    QK = HH[:, 0:512].rearrange("p (c t) -> p c t", t=P)

    with nc.Fori(0, TILES) as t:
        with nc.Block(no_gpsimd_drain=True) as block:
            @block.sync
            def _(sp):
                sp.dma_start(CTX.rearrange("p j d -> p (j d)"), stacked("ctx", t)).then_inc(S("ctx"), 16)
                sp.dma_start(MASK.rearrange("p b k -> p (b k)"), stacked("mask_f", t)).then_inc(S("mask"), 16)

            @block.vector
            def _(dve):
                c = Chain(dve, S("vector"))
                dve.wait_ge(S("ctx"), 16)
                layer_norm(c, [(CTX[:, j, :], CTX[:, j, :]) for j in range(4)])
                c.do(nc.vector.tensor_tensor(CTX, CTX, A["l0x_cln_g"].unsqueeze(1).broadcast_to([P, 4, D]), ALU.mult))
                nc.vector.tensor_tensor(CTX, CTX, A["l0x_cln_b"].unsqueeze(1).broadcast_to([P, 4, D]), ALU.add)\
                    .then_inc(S("ctx normed"), 1)
                c.do(nc.vector.tensor_copy(XT.unsqueeze(1), X[:, bass.ds(t, 1), :]))
                layer_norm(c, [(XT, XN)])

                def second():
                    layer_norm(c, [(XN, XN)])
                    affine(c, XN, A["l0x_ln_g"], A["l0x_ln_b"])
                normed(c, "l0x", second)
                dve.wait_ge(S("tanh"), 1)
                c.do(nc.vector.scalar_tensor_tensor(HH, OO, 1.0, psS[:, 1024:2048], ALU.add, ALU.mult))
                c.do(nc.vector.scalar_tensor_tensor(HH, HH, 0.5, psS[:, 0:1024], ALU.mult, ALU.mult))
                nc.vector.tensor_copy(ONE[5][:], HH[:, 0:1]).then_inc(S("gated"), 1)
                dve.wait_ge(S("mask"), 16)
                attention_vector(dve, c, "l0x", KEYS, lambda b: MASK[:, b, :])
                residual(dve, c, "l0x", None)
                normed(c, "l0a")
                dve.wait_ge(S("l0a qkv"), 1)
                nc.vector.tensor_copy(V256, psO[:, 0:D]).then_inc(S("l0a values"), 1)
                dve.wait_ge(S("l0a scores"), 1)
                c.do(nc.vector.tensor_reduce(ONE[0][:], psS[:, 0:64], AX, ALU.max))
                nc.vector.tensor_scalar(ONE[1][:], ONE[0][:], -1.0, None, ALU.mult).then_inc(S("l0a max"), 1)
                dve.wait_ge(S("l0a exp"), 1)
                c.do(nc.vector.reciprocal(ONE[3][:], ONE[2][:]))
                c.do(nc.vector.tensor_scalar(PR[:, 0:64], PR[:, 0:64], ONE[3][:], None, ALU.mult))
                c.do(nc.vector.tensor_reduce(ONE[4][:], PR[:, 0:64], AX, ALU.add))
                dve.wait_ge(S("l0a value sums"), 1)
                nc.vector.tensor_scalar(OO[:, 0:D], psO[:, 512:512 + D], ONE[4][:], None, ALU.mult)\
                    .then_inc(S("l0a o"), 1)
                dve.wait_ge(S("l0a y"), 1)
                c.do(nc.vector.tensor_tensor(XN, XN, psA[:, 0:D], ALU.add))
                c.do(nc.vector.tensor_tensor(XN, XN, A["l0a_bfc"], ALU.add))
                layer_norm(c, [(XN, XN)])
                affine(c, XN, A["l0a_gamma"], A["l0a_beta"])
                c.do(nc.vector.tensor_tensor(XT, XT, XN, ALU.add))
                to_experts_vector(dve, c, t)

            @block.scalar
            def _(act):
                act.wait_ge(S("ctx turned"), 1)
                nc.scalar.copy(CTXT.rearrange("p c t -> p (c t)"), psS[:, 0:1024]).then_inc(S("ctxT"), 1)
                act.wait_ge(S("l0x kv"), 1)
                nc.scalar.copy(KT, psA[:, 0:512]).then_inc(S("l0x kvs"), 1)
                nc.scalar.copy(V.rearrange("p j d -> p (j d)"), psA[:, 512:768]).then_inc(S("l0x kvs"), 1)
                transpose_x_scalar(act, "l0x", XNT)
                act.wait_ge(S("l0x q"), 1)
                nc.scalar.mul(QT.rearrange("p b h t -> p h b t"),
                              psS[:, 0:1024].rearrange("p (h b t) -> p h b t", b=2, t=SEQ), 0.125).then_inc(S("l0x qT"), 1)
                act.wait_ge(S("hidden"), 1)
                nc.scalar.activation(OO, psS[:, 1024:2048], ACT.Tanh, scale=0.5).then_inc(S("tanh"), 1)
                attention_scalar(act, "l0x", KEYS, True)
                project_scalar(act, "l0x", 8)
                act.wait_ge(S("hidden turned"), 1)
                nc.scalar.copy(HHT, psS[:, 1024:2048]).then_inc(S("hiddenT"), 1)
                transpose_x_scalar(act, "l0a", XNT)
                act.wait_ge(S("l0a qkv"), 1)
                nc.scalar.mul(QK[:, 0:2, :], psA[:, 512:768].rearrange("p (c t) -> p c t", t=P), D ** -0.5)\
                    .then_inc(S("l0a qk"), 1)
                nc.scalar.copy(QK[:, 2:4, :], psA[:, 768:1024].rearrange("p (c t) -> p c t", t=P))\
                    .then_inc(S("l0a qk"), 1)
                act.wait_ge(S("l0a max"), 1)
                nc.scalar.activation(PR[:, 0:64], psS[:, 0:64], ACT.Exp, bias=ONE[1][:], accum_out=ONE[2][:])\
                    .then_inc(S("l0a exp"), 1)
                act.wait_ge(S("l0a o turned"), 1)
                nc.scalar.copy(OT[:, 0:D], psS[:, 0:D]).then_inc(S("l0a oT"), 1)

            @block.tensor
            def _(pe):
                pe.wait_ge(S("ctx normed"), 1)
                for c in range(DC):
                    for j in range(4):
                        last = nc.tensor.transpose(psS[:, c * 512 + j * P:c * 512 + (j + 1) * P],
                                                   CTX[:, j, c * P:(c + 1) * P], ident)
                last.then_inc(S("ctx turned"), 1)
                pe.wait_ge(S("ctxT"), 1)
                product(psA[:, 0:512], lambda i: A["l0x_wk"][:, i, :], lambda i: CTXT[:, i, :], DC)
                for j in range(4):
                    last = product(psA[:, 512 + 64 * j:576 + 64 * j], lambda i: CTXT[:, i, j * P:(j + 1) * P],
                                   lambda i: A["l0x_wv"][:, i, :], DC)
                last.then_inc(S("l0x kv"), 1)
                pe.wait_ge(S("l0x kvs"), 2)
                transpose_x_tensor(pe, "l0x", XN)
                pe.wait_ge(S("l0x xnT"), 1)
                for j in range(8):
                    last = product(psS[:, j * P:(j + 1) * P], lambda i: A["l0x_wq"][:, i, j * P:(j + 1) * P],
                                   lambda i: XNT[:, i, :], DC)
                last.then_inc(S("l0x q"), 1)
                pe.wait_ge(S("l0x qT"), 1)
                for j in range(4):
                    last = product(psS[:, j * 512:(j + 1) * 512], lambda i: XNT[:, i, :],
                                   lambda i: A["l0x_w1"][:, i, j * 512:(j + 1) * 512], DC)
                last.then_inc(S("hidden"), 1)

                def query(b, p):
                    r, k = p // 4, p % 4
                    return QT[64 * r:64 * r + 64, b, 2 * k:2 * k + 2, :].rearrange("p h t -> p (h t)")

                attention_tensor(
                    pe, "l0x", KEYS, 64, query,
                    lambda b, p: KT[64 * (p // 4):64 * (p // 4) + 64, 256 * b:256 * b + 256],
                    lambda b, c, h: V[:, 2 * b + c, :], lambda p, s: 4 * (p % 4) + 2 * s + p // 4,
                    [("gated", 1)])
                pe.wait_ge(S("l0x o"), 1)
                for i in range(8):
                    last = nc.tensor.transpose(psS[:, i * P:(i + 1) * P], OO[:, i * P:(i + 1) * P], ident)
                last.then_inc(S("l0x o turned"), 1)
                for i in range(8):
                    last = nc.tensor.transpose(psS[:, 1024 + i * P:1024 + (i + 1) * P], HH[:, i * P:(i + 1) * P], ident)
                last.then_inc(S("hidden turned"), 1)
                pe.wait_ge(S("l0x oT"), 1)
                pe.wait_ge(S("hiddenT"), 1)
                product(psA[:, 0:D], lambda i: OT[:, i * P:(i + 1) * P] if i < 8 else HHT[:, (i - 8) * P:(i - 7) * P],
                        lambda i: A["l0x_wout"][:, i, :] if i < 8 else A["l0x_w2"][:, i - 8, :], 16)\
                    .then_inc(S("l0x y"), 1)
                transpose_x_tensor(pe, "l0a", XN)
                pe.wait_ge(S("l0a xnT"), 1)
                for j in range(4):
                    product(psA[:, 512 + j * P:512 + (j + 1) * P], lambda i: A["l0a_wqkv"][:, i, j * P:(j + 1) * P],
                            lambda i: XNT[:, i, :], DC)
                product(psO[:, 0:D], lambda i: XNT[:, i, :], lambda i: A["l0a_wqkv"][:, i, 2 * D:3 * D], DC)\
                    .then_inc(S("l0a qkv"), 1)
                pe.wait_ge(S("l0a qk"), 2)
                for b in range(2):
                    last = product(psS[64 * b:64 * b + 64, 0:64], lambda i: QK[:, i, 64 * b:64 * b + 64],
                                   lambda i: QK[:, 2 + i, 64 * b:64 * b + 64], DC)
                last.then_inc(S("l0a scores"), 1)
                pe.wait_ge(S("l0a values"), 1)
                nc.tensor.matmul(psO[:, 512:512 + D], K["batch_ones"], V256, start=True, stop=True)\
                    .then_inc(S("l0a value sums"), 1)
                project_tensor(pe, "l0a", DC, A["l0a_wfc"])
                transpose_x_tensor(pe, "router", XN)
        end()

    def experts(layer, capacity, softmax_first, next_params):
        work = Work(REGION)
        WEIGHTS = [work(4096), work(4096)]
        W1 = [w[:, 0:2048].rearrange("p (c h) -> p c h", h=HID) for w in WEIGHTS]
        W2 = [w[:, 2048:4096].rearrange("p (j d) -> p j d", d=D) for w in WEIGHTS]
        HT = [work(HB, HALF), work(HB, HALF)]
        router = Work(REGION[:, 8192:16384])
        LG, VALUES, TOP = router(TILES, EXPERTS), router(TILES, EXPERTS), router(TILES, 8)
        INDEX, INDEXF = router(TILES, 8), router(TILES, 8)
        CHOICE, RANK, PREFIX = router(2, TILES, EXPERTS), router(2, TILES, EXPERTS), router(2, TILES, EXPERTS)
        W = router(2, TILES)
        A8, B8 = router(TILES), router(TILES)
        choice16 = CHOICE.rearrange("p k t e -> p (k t) e")
        prefix16 = PREFIX.rearrange("p k t e -> p (k t) e")

        with nc.Block(no_gpsimd_drain=True) as block:
            @block.sync
            def _(sp):
                sp.dma_start(RT[:], dram[layer + "_router"]).then_inc(S("router params"), 16)
                sp.dma_start(WEIGHTS[0], dram[layer + "_experts"][0:P, :]).then_inc(S("weights"), 16)
                if next_params:
                    name, params = next_params
                    sp.dma_start(PARAM[:, 0:width(params)], dram[name]).then_inc(S("next params"), 16)
                sp.wait_ge(S("weights"), 16)
                if next_params:
                    sp.wait_ge(S("next params"), 16)

            @block.tensor
            def _(pe):
                pe.wait_ge(S("router params"), 16)
                for t in range(TILES):
                    last = product(psS[:, t * EXPERTS:(t + 1) * EXPERTS], lambda i: XNT_ALL[:, i, t * P:(t + 1) * P],
                                   lambda i: R["gate_w"][:, i, :], DC)
                last.then_inc(S("logits"), 1)
                if capacity:
                    pe.wait_ge(S("choices"), 1)
                    nc.tensor.matmul(psA[:, 0:128], K["tri"], choice16.rearrange("p n e -> p (n e)"),
                                     start=True, stop=True)
                    nc.tensor.matmul(psA[:, 512:640], K["ones"], choice16.rearrange("p n e -> p (n e)"),
                                     start=True, stop=True).then_inc(S("counts"), 1)
                pe.wait_ge(S("gates"), 1)
                for t in range(TILES):
                    last = nc.tensor.transpose(psO[0:EXPERTS, t * P:(t + 1) * P], GATES[:, t, :], ident)
                last.then_inc(S("gates turned"), 1)
                pe.wait_ge(S("gate rows"), 1)
                for t in range(TILES):
                    last = nc.tensor.matmul(psS[:, t * D:(t + 1) * D], GATE_ROWS[:, t, :], R["b2"], start=True, stop=True)
                last.then_inc(S("biases"), 1)

            @block.scalar
            def _(act):
                act.wait_ge(S("to exp"), 1)
                if softmax_first:
                    nc.scalar.activation(VALUES, VALUES, ACT.Exp).then_inc(S("exp"), 1)
                else:
                    nc.scalar.activation(A8, A8, ACT.Exp).then_inc(S("exp"), 1)
                act.wait_ge(S("gates turned"), 1)
                nc.scalar.copy(GATE_ROWS[:].rearrange("p t n -> p (t n)"), psO[0:EXPERTS, :]).then_inc(S("gate rows"), 1)

            @block.vector
            def _(dve):
                c = Chain(dve, S("vector"))
                dve.wait_ge(S("logits"), 1)
                c.do(nc.vector.tensor_copy(LG.rearrange("p t e -> p (t e)"), psS[:, 0:TILES * EXPERTS]))
                values = LG
                if softmax_first:
                    c.do(nc.vector.tensor_reduce(A8, LG, AX, ALU.max))
                    nc.vector.tensor_tensor(VALUES, LG, A8.unsqueeze(2).broadcast_to([P, TILES, EXPERTS]),
                                            ALU.subtract).then_inc(S("to exp"), 1)
                    dve.wait_ge(S("exp"), 1)
                    c.do(nc.vector.tensor_reduce(A8, VALUES, AX, ALU.add))
                    c.do(nc.vector.reciprocal(B8, A8))
                    c.do(nc.vector.tensor_tensor(VALUES, VALUES, B8.unsqueeze(2).broadcast_to([P, TILES, EXPERTS]),
                                                 ALU.mult))
                    values = VALUES
                for t in range(TILES):
                    c.go(nc.vector.max(TOP[:, t, :], values[:, t, :]))
                c.settle()
                for t in range(TILES):
                    c.go(nc.vector.max_index(INDEX[:, t, :].bitcast(U32), TOP[:, t, :], values[:, t, :]))
                c.settle()
                c.do(nc.vector.tensor_copy(INDEXF, INDEX.bitcast(U32)))
                for k in range(2):
                    c.go(nc.vector.tensor_tensor(
                        CHOICE[:, k, :, :], K["experts"].unsqueeze(1).broadcast_to([P, TILES, EXPERTS]),
                        INDEXF[:, :, k:k + 1].broadcast_to([P, TILES, EXPERTS]), ALU.is_equal))
                c.settle()
                if capacity:
                    nc.vector.tensor_copy(ONE[4][:], CHOICE[:, 0, 0, 0:1]).then_inc(S("choices"), 1)
                if softmax_first:
                    for k in range(2):
                        c.go(nc.vector.tensor_copy(W[:, k, :], TOP[:, :, k]))
                    c.settle()
                else:
                    nc.vector.tensor_tensor(A8, TOP[:, :, 1], TOP[:, :, 0], ALU.subtract).then_inc(S("to exp"), 1)
                    dve.wait_ge(S("exp"), 1)
                    c.do(nc.vector.tensor_scalar(B8, A8, 1.0, None, ALU.add))
                    c.do(nc.vector.reciprocal(W[:, 0, :], B8))
                    c.do(nc.vector.tensor_tensor(W[:, 1, :], A8, W[:, 0, :], ALU.mult))
                if capacity:
                    dve.wait_ge(S("counts"), 1)
                    c.do(nc.vector.memset(prefix16[:, 0, :], 0.0))
                    for n in range(1, 2 * TILES):
                        c.do(nc.vector.tensor_tensor(prefix16[:, n, :], prefix16[:, n - 1, :],
                                                     psA[:, 512 + (n - 1) * EXPERTS:512 + n * EXPERTS], ALU.add))
                    rank = RANK.rearrange("p k t e -> p (k t e)")
                    c.do(nc.vector.tensor_tensor(rank, psA[:, 0:128], PREFIX.rearrange("p k t e -> p (k t e)"), ALU.add))
                    c.do(nc.vector.tensor_scalar(rank, rank, capacity + 0.5, None, ALU.is_lt))
                    c.do(nc.vector.tensor_tensor(choice16, choice16, RANK.rearrange("p k t e -> p (k t) e"), ALU.mult))
                c.do(nc.vector.tensor_tensor(choice16, choice16,
                                             W.rearrange("p k t -> p (k t)").unsqueeze(2).broadcast_to([P, 16, EXPERTS]),
                                             ALU.mult))
                nc.vector.tensor_tensor(GATES[:], CHOICE[:, 0], CHOICE[:, 1], ALU.add).then_inc(S("gates"), 1)
                dve.wait_ge(S("biases"), 1)
                c.do(nc.vector.tensor_tensor(X[:].rearrange("p t d -> p (t d)"), X[:].rearrange("p t d -> p (t d)"),
                                             psS[:], ALU.add))
        end()

        def pair(i, last_pair):
            with nc.Block(no_gpsimd_drain=True) as block:
                @block.sync
                def _(sp):
                    sp.dma_start(WEIGHTS[1], stacked(layer + "_experts", 2 * i + 1)).then_inc(S("weights"), 16)
                    if not last_pair:
                        sp.wait_ge(S("down"), HALF // P * 2)
                        sp.dma_start(WEIGHTS[0], stacked(layer + "_experts", 2 * i + 2))\
                            .then_inc(S("next weights"), 16)
                        sp.wait_ge(S("next weights"), 16)

                @block.tensor
                def _(pe):
                    for e in range(2):
                        if e:
                            pe.wait_ge(S("weights"), 16)
                        for half in range(2):
                            for j in range(HB):
                                n = (2 * e + half) * HB + j
                                if n >= 4:
                                    pe.wait_ge(S("gelu"), n - 3)
                                product(psS[:, n % 4 * 512:(n % 4 + 1) * 512],
                                        lambda q: W1[e][:, q, j * P:(j + 1) * P],
                                        lambda q: XNT_ALL[:, q, half * HALF:(half + 1) * HALF], DC)\
                                    .then_inc(S("up"), 1)
                        for half in range(2):
                            pe.wait_ge(S("gelu"), (2 * e + half + 1) * HB)
                            for u in range(4):
                                n = (2 * e + half) * 4 + u
                                if n >= 4:
                                    pe.wait_ge(S("added"), n - 3)
                                ps = (psA, psO)[n % 4 // 2]
                                product(ps[:, n % 2 * 512:n % 2 * 512 + D],
                                        lambda q: HT[half][:, q, u * P:(u + 1) * P], lambda q: W2[e][:, q, :], HB)\
                                    .then_inc(S("down"), 1)

                @block.scalar
                def _(act):
                    act.wait_ge(S("of expert"), 4)
                    for e in range(2):
                        for half in range(2):
                            if e:
                                act.wait_ge(S("down"), (2 * (e - 1) + half + 1) * 4)
                            for j in range(HB):
                                n = (2 * e + half) * HB + j
                                act.wait_ge(S("up"), n + 1)
                                nc.scalar.activation(HT[half][:, j, :], psS[:, n % 4 * 512:(n % 4 + 1) * 512],
                                                     ACT.Gelu, bias=BIAS[:, e, j:j + 1]).then_inc(S("gelu"), 1)

                @block.vector
                def _(dve):
                    for e in range(2):
                        nc.vector.tensor_copy(BIAS[:, e:e + 1, :], R["b1"][:, bass.ds(2 * i + e, 1), :])\
                            .then_inc(S("of expert"), 1)
                        nc.vector.tensor_copy(GATE[:, e, :].unsqueeze(2), GATES[:, :, bass.ds(2 * i + e, 1)])\
                            .then_inc(S("of expert"), 1)
                    dve.wait_ge(S("of expert"), 4)
                    for n in range(16):
                        e, t = n // 8, n % 8
                        dve.wait_ge(S("down"), n + 1)
                        if e:
                            dve.wait_ge(S("added"), n - 7)
                        ps = (psA, psO)[n % 4 // 2]
                        nc.vector.scalar_tensor_tensor(X[:, t, :], ps[:, n % 2 * 512:n % 2 * 512 + D],
                                                       GATE[:, e, t:t + 1], X[:, t, :], ALU.mult, ALU.add)\
                            .then_inc(S("added"), 1)
            end()

        with nc.Fori(0, EXPERTS // 2 - 1) as i:
            pair(i, False)
        pair(EXPERTS // 2 - 1, True)

    experts("l0f", int(1.25 * TOKENS * 2 / EXPERTS), False, ("params_b", PARAMS_B))


    B = views(PARAM, PARAMS_B)
    work = Work(REGION)
    XT, XN, XNT = work(D), work(D), work(DC, P)
    SM, PR, PT = work(2048), work(2048), work(2048)
    OO, OT = work(1024), work(1024)
    QBD = work(32, SEQ)
    CTXT, KT, V = work(DC, 512), work(DC, 512), work(4, D)
    QF = work(DC, P)
    CAUSAL, KEYMASK = work(2, SEQ), work(2, KEYS)
    RAW_I = work(2 * SEQ).bitcast(I32)
    RAW_B = work(2 * KEYS // 4).bitcast(dram["mask_b"].dtype)
    V64, WKB = work(2, D, parts=64), work(D, parts=64)
    KA = OT[0:64, 0:256].rearrange("p (c t) -> p c t", t=P)
    BIT = Work(REGION)
    W1F, W2F = BIT(DC * HID), BIT(HB * D)
    BITS = [BIT(2048), BIT(2048)]

    with nc.Block(no_gpsimd_drain=True) as block:
        @block.sync
        def _(sp):
            sp.dma_start(W1F, dram["bitnet"][:, 0:2048]).then_inc(S("bitnet"), 16)
            sp.dma_start(W2F, dram["bitnet"][:, 2048:4096]).then_inc(S("bitnet"), 16)

        @block.scalar
        def _(act):
            act.wait_ge(S("bitnet"), 32)
            for n, w in enumerate((W1F, W2F)):
                nc.scalar.activation(BITS[n], w, ACT.Abs, accum_out=ONE[n][:]).then_inc(S("abs"), 1)

        @block.tensor
        def _(pe):
            for j in range(DC):
                for m in range(DC):
                    nc.tensor.matmul(psA[:, m * D + j * P:m * D + (j + 1) * P], B["l1a_wq"][:, j, m * P:(m + 1) * P],
                                     K["rope"][:, j, :], start=True, stop=True)
                last = nc.tensor.matmul(psO[0:64, j * P:(j + 1) * P], B["l1a_wkb"][:, j, :], K["rope"][:, j, :],
                                        start=True, stop=True)
            last.then_inc(S("rotated"), 1)
            pe.wait_ge(S("abs"), 2)
            for n in range(2):
                last = nc.tensor.matmul(psS[:, n:n + 1], K["ones"], ONE[n][:], start=True, stop=True)
            last.then_inc(S("abs sums"), 1)

        @block.vector
        def _(dve):
            c = Chain(dve, S("vector"))
            c.go(nc.vector.tensor_copy(IDB[:], ident))
            dve.wait_ge(S("rotated"), 1)
            c.go(nc.vector.tensor_copy(B["l1a_wq"].rearrange("p c n -> p (c n)"), psA[:, 0:2 * D]))
            dve.wait_ge(S("abs sums"), 1)
            c.do(nc.vector.tensor_scalar(WSCALE[:], psS[:, 0:2], 1.0 / (D * HID), EPS, ALU.mult, ALU.max))
            c.do(nc.vector.reciprocal(RECS[:, 0:2], WSCALE[:]))
            for n, (w, q) in enumerate(((W1F, W1Q[:]), (W2F, W2Q[:]))):
                q = q.rearrange("p a b -> p (a b)")
                c.do(nc.vector.tensor_scalar(w, w, RECS[:, n:n + 1], ROUND, ALU.mult, ALU.add))
                c.do(nc.vector.tensor_scalar(w, w, -ROUND, -1.0, ALU.add, ALU.max))
                c.do(nc.vector.tensor_scalar(q, w, 1.0, None, ALU.min))
            c.do(nc.vector.tensor_copy(WKB, psO[0:64, 0:D]))
    end()

    def quantize(c, x, q, back, scale):
        c.do(nc.vector.tensor_reduce(ONE[0][:], x, AX, ALU.max, apply_absolute_value=True))
        c.do(nc.vector.tensor_scalar(ONE[1][:], ONE[0][:], EPS, None, ALU.max))
        c.do(nc.vector.reciprocal(ONE[2][:], ONE[1][:]))
        c.do(nc.vector.tensor_scalar(ONE[3][:], ONE[2][:], 127.0, None, ALU.mult))
        c.do(nc.vector.tensor_scalar(back, ONE[1][:], 1.0 / 127.0, scale, ALU.mult, ALU.mult))
        c.do(nc.vector.tensor_scalar(x, x, ONE[3][:], ROUND, ALU.mult, ALU.add))
        c.do(nc.vector.tensor_scalar(x, x, -ROUND, -128.0, ALU.add, ALU.max))
        c.do(nc.vector.tensor_scalar(q, x, 127.0, None, ALU.min))

    Q1, Q2 = OO[:, 0:128].bitcast(BF16), OO[:, 512:1024].bitcast(BF16)
    Q1T, Q2T = OT[:, 0:128].bitcast(BF16), OT[:, 512:1024].bitcast(BF16)
    psA16, psO16 = psA[:, 0:512].bitcast(BF16), psO[:, 0:512].bitcast(BF16)

    with nc.Fori(0, TILES) as t:
        with nc.Block(no_gpsimd_drain=True) as block:
            @block.sync
            def _(sp):
                sp.dma_start(CTXT.rearrange("p c t -> p (c t)"), stacked("ctxT", t)).then_inc(S("ctxT"), 16)
                sp.dma_start(V64.rearrange("p b d -> p (b d)"), dram["ctx64"][bass.ds(t * SEQ, SEQ), :])\
                    .then_inc(S("ctx64"), 16)
                sp.dma_start(RAW_I, stacked("mask_i", t)).then_inc(S("masks"), 16)
                sp.dma_start(RAW_B, stacked("mask_b", t)).then_inc(S("masks"), 16)

            @block.vector
            def _(dve):
                c = Chain(dve, S("vector"))
                c.do(nc.vector.tensor_copy(XT.unsqueeze(1), X[:, bass.ds(t, 1), :]))
                normed(c, "l1x")
                dve.wait_ge(S("masks"), 32)
                flat = CAUSAL.rearrange("p b k -> p (b k)")
                c.do(nc.vector.tensor_scalar(flat, RAW_I, 1.0, FAR, ALU.is_equal, ALU.mult))
                c.do(nc.vector.tensor_tensor(CAUSAL, CAUSAL, K["causal"].unsqueeze(1).broadcast_to([P, 2, SEQ]), ALU.add))
                c.do(nc.vector.tensor_scalar(KEYMASK.rearrange("p b k -> p (b k)"), RAW_B, -1e9, None, ALU.mult))
                dve.wait_ge(S("l1x xnT"), 1)
                head_queries(c, XNT, "l1x")
                attention_vector(dve, c, "l1x", SEQ, lambda b: CAUSAL[:, b, :])
                residual(dve, c, "l1x", B["l1x_b"])
                normed(c, "l1a")
                dve.wait_ge(S("l1a q"), 1)
                head_queries(c, psA[:, 512:768].rearrange("p (c t) -> p c t", t=P), "l1a")
                attention_vector(dve, c, "l1a", SEQ, None)
                residual(dve, c, "l1a", None)
                layer_norm(c, [(XT, XN)])
                layer_norm(c, [(XN, XN)])
                affine(c, XN, B["l1f_ln1_w"], B["l1f_ln1_b"])
                quantize(c, XN, Q1, ONE[4][:], WSCALE[:, 0:1])
                nc.vector.tensor_copy(ONE[7][:], ONE[4][:]).then_inc(S("l1f q1"), 1)
                dve.wait_ge(S("l1f up"), 1)
                nc.vector.scalar_tensor_tensor(SM[:, 0:HID], psS[:, 0:HID], ONE[4][:], B["l1f_b1"], ALU.mult, ALU.add)\
                    .then_inc(S("l1f hidden"), 1)
                dve.wait_ge(S("l1f gelu"), 1)
                h = PR[:, 0:HID]
                layer_norm(c, [(h, h)])
                affine(c, h, B["l1f_ln2_w"], B["l1f_ln2_b"])
                quantize(c, h, Q2, ONE[5][:], WSCALE[:, 1:2])
                nc.vector.tensor_copy(ONE[7][:], ONE[5][:]).then_inc(S("l1f q2"), 1)
                dve.wait_ge(S("l1f y"), 1)
                c.do(nc.vector.scalar_tensor_tensor(XT, psA[:, 512:768], ONE[5][:], XT, ALU.mult, ALU.add))
                c.do(nc.vector.tensor_tensor(XT, XT, B["l1f_b2"], ALU.add))
                normed(c, "l2x")
                dve.wait_ge(S("l2x kv"), 1)
                nc.vector.tensor_tensor(V, psS[:, 1024:2048].rearrange("p (j d) -> p j d", d=D),
                                        B["l2x_bv"].unsqueeze(1).broadcast_to([P, 4, D]), ALU.add)\
                    .then_inc(S("l2x kvs"), 1)
                dve.wait_ge(S("l2x qT"), 2)
                head_queries(c, QF, "l2x")
                attention_vector(dve, c, "l2x", KEYS, lambda b: KEYMASK[:, b, :])
                residual(dve, c, "l2x", B["l2x_bo"])
                normed(c, "l2a")
                dve.wait_ge(S("l2a squares"), 1)
                rstd_of(c, 1, ONE[0][:], 0.0)
                nc.vector.tensor_scalar(ONE[1][:], RSTD[:, 0:1], 2048.0 ** 0.5, None, ALU.mult).then_inc(S("l2a norm"), 1)
                residual(dve, c, "l2a", None)
                to_experts_vector(dve, c, t)

            @block.scalar
            def _(act):
                transpose_x_scalar(act, "l1x", XNT)
                attention_scalar(act, "l1x", SEQ, True)
                project_scalar(act, "l1x", DC)
                transpose_x_scalar(act, "l1a", XNT)
                act.wait_ge(S("l1a latent"), 1)
                nc.scalar.copy(KA.rearrange("p c t -> p (c t)"), psO[0:64, 0:256]).then_inc(S("l1a latents"), 1)
                act.wait_ge(S("l1a kv"), 1)
                nc.scalar.copy(KT[:, :, 0:P], psO[:, 512:768].rearrange("p (c t) -> p c t", t=P)).then_inc(S("l1a kvs"), 1)
                nc.scalar.copy(V64.rearrange("p b d -> p (b d)"), psS[0:64, 0:512]).then_inc(S("l1a kvs"), 1)
                attention_scalar(act, "l1a", SEQ, None)
                project_scalar(act, "l1a", DC)
                act.wait_ge(S("l1f q1 turned"), 1)
                nc.scalar.copy(Q1T, psA16[:, 0:256]).then_inc(S("l1f q1T"), 1)
                act.wait_ge(S("l1f hidden"), 1)
                nc.scalar.activation(PR[:, 0:HID], SM[:, 0:HID], ACT.Gelu).then_inc(S("l1f gelu"), 1)
                act.wait_ge(S("l1f q2 turned"), 1)
                nc.scalar.copy(Q2T, psA16).then_inc(S("l1f q2T"), 1)
                transpose_x_scalar(act, "l2x", XNT)
                act.wait_ge(S("l2x kv"), 1)
                for i in range(DC):
                    nc.scalar.activation(KT[:, i, :], psS[:, i * 512:(i + 1) * 512], ACT.Identity,
                                         bias=B["l2x_bk"][:, i:i + 1]).then_inc(S("l2x kvs"), 1)
                act.wait_ge(S("l2x q"), 1)
                for i in range(DC):
                    nc.scalar.activation(QF[:, i, :], psA[:, 512 + i * P:512 + (i + 1) * P], ACT.Identity,
                                         bias=B["l2x_bq"][:, i:i + 1]).then_inc(S("l2x qT"), 1)
                attention_scalar(act, "l2x", KEYS, True)
                project_scalar(act, "l2x", DC)
                transpose_x_scalar(act, "l2a", XNT)
                act.wait_ge(S("l2a scores"), 1)
                nc.scalar.activation(SM, psS[:], ACT.Square, accum_out=ONE[0][:]).then_inc(S("l2a squares"), 1)
                act.wait_ge(S("l2a norm"), 1)
                nc.scalar.activation(PR, psS[:], ACT.Gelu, scale=ONE[1][:]).then_inc(S("l2a gelu"), 1)
                act.wait_ge(S("l2a gelu turned"), 1)
                nc.scalar.copy(PT, psS[:]).then_inc(S("l2a gT"), 1)

            @block.tensor
            def _(pe):
                transpose_x_tensor(pe, "l1x", XN)
                attention_tensor(pe, "l1x", SEQ, DH, masked_query, lambda b, p: CTXT[:, p // 4, KEYS * b:KEYS * b + SEQ],
                                 lambda b, c, h: V64[:, b, h * DH:(h + 1) * DH], plain_heads,
                                 [("ctxT", 16), ("ctx64", 16), ("l1x queries", 1)])
                project_tensor(pe, "l1x", DC, B["l1x_w"])
                transpose_x_tensor(pe, "l1a", XN)
                pe.wait_ge(S("l1a xnT"), 1)
                for j in range(DC):
                    product(psA[:, 512 + j * P:512 + (j + 1) * P], lambda i: B["l1a_wq"][:, i, j * P:(j + 1) * P],
                            lambda i: XNT[:, i, :], DC).then_inc(S("l1a q" if j == DC - 1 else "l1a q0"), 1)
                for j, w in enumerate(("l1a_wka", "l1a_wva")):
                    last = product(psO[0:64, j * P:(j + 1) * P], lambda i: B[w][:, i, :], lambda i: XNT[:, i, :], DC)
                last.then_inc(S("l1a latent"), 1)
                pe.wait_ge(S("l1a latents"), 1)
                for j in range(DC):
                    nc.tensor.matmul(psO[:, 512 + j * P:512 + (j + 1) * P], WKB[:, j * P:(j + 1) * P], KA[:, 0, :],
                                     start=True, stop=True)
                for b in range(2):
                    last = nc.tensor.matmul(psS[0:64, D * b:D * (b + 1)], KA[:, 1, SEQ * b:SEQ * (b + 1)], B["l1a_wvb"],
                                            start=True, stop=True)
                last.then_inc(S("l1a kv"), 1)
                attention_tensor(pe, "l1a", SEQ, DH, masked_query, lambda b, p: KT[:, p // 4, SEQ * b:SEQ * (b + 1)],
                                 lambda b, c, h: V64[:, b, h * DH:(h + 1) * DH], plain_heads,
                                 [("l1a kvs", 2), ("l1a queries", 1)])
                project_tensor(pe, "l1a", DC, B["l1a_wo"])
                pe.wait_ge(S("l1f q1"), 1)
                for i in range(DC):
                    last = nc.tensor.transpose(psA16[:, i * P:(i + 1) * P], Q1[:, i * P:(i + 1) * P], IDB[:])
                last.then_inc(S("l1f q1 turned"), 1)
                pe.wait_ge(S("l1f q1T"), 1)
                for j in range(2):
                    last = product(psS[:, j * 512:(j + 1) * 512], lambda i: Q1T[:, i * P:(i + 1) * P],
                                   lambda i: W1Q[:, i, j * 512:(j + 1) * 512], DC)
                last.then_inc(S("l1f up"), 1)
                pe.wait_ge(S("l1f q2"), 1)
                for i in range(HB):
                    last = nc.tensor.transpose(psA16[:, i * P:(i + 1) * P], Q2[:, i * P:(i + 1) * P], IDB[:])
                last.then_inc(S("l1f q2 turned"), 1)
                pe.wait_ge(S("l1f q2T"), 1)
                product(psA[:, 512:768], lambda i: Q2T[:, i * P:(i + 1) * P], lambda i: W2Q[:, i, :], HB)\
                    .then_inc(S("l1f y"), 1)
                transpose_x_tensor(pe, "l2x", XN)
                for j in range(DC):
                    product(psS[:, j * 512:(j + 1) * 512], lambda i: B["l2x_wk"][:, i, j * P:(j + 1) * P],
                            lambda i: CTXT[:, i, :], DC)
                for j in range(4):
                    last = product(psS[:, 1024 + j * D:1024 + (j + 1) * D], lambda i: CTXT[:, i, j * P:(j + 1) * P],
                                   lambda i: B["l2x_wv"][:, i, :], DC)
                last.then_inc(S("l2x kv"), 1)
                pe.wait_ge(S("l2x xnT"), 1)
                for j in range(DC):
                    last = product(psA[:, 512 + j * P:512 + (j + 1) * P], lambda i: B["l2x_wq"][:, i, j * P:(j + 1) * P],
                                   lambda i: XNT[:, i, :], DC)
                last.then_inc(S("l2x q"), 1)
                attention_tensor(pe, "l2x", KEYS, DH, masked_query, lambda b, p: KT[:, p // 4, KEYS * b:KEYS * (b + 1)],
                                 lambda b, c, h: V[:, 2 * b + c, h * DH:(h + 1) * DH], plain_heads,
                                 [("l2x kvs", 3), ("l2x queries", 1)])
                project_tensor(pe, "l2x", DC, B["l2x_wo"])
                transpose_x_tensor(pe, "l2a", XN)
                pe.wait_ge(S("l2a xnT"), 1)
                for j in range(4):
                    last = product(psS[:, j * 512:(j + 1) * 512], lambda i: XNT[:, i, :],
                                   lambda i: B["l2a_k"][:, i, j * 512:(j + 1) * 512], DC)
                last.then_inc(S("l2a scores"), 1)
                pe.wait_ge(S("l2a gelu"), 1)
                for i in range(16):
                    last = nc.tensor.transpose(psS[:, i * P:(i + 1) * P], PR[:, i * P:(i + 1) * P], ident)
                last.then_inc(S("l2a gelu turned"), 1)
                pe.wait_ge(S("l2a gT"), 1)
                product(psA[:, 0:D], lambda i: PT[:, i * P:(i + 1) * P], lambda i: B["l2a_v"][:, i, :], 16)\
                    .then_inc(S("l2a y"), 1)
                transpose_x_tensor(pe, "router", XN)
        end()

    experts("l2f", None, False, ("params_c", PARAMS_C))


    C = views(PARAM, PARAMS_C)
    work = Work(REGION)
    XT, XN, XNT = work(D), work(D), work(DC, P)
    SM, PR, PT = work(2048), work(2048), work(2048)
    OO, OT = work(1024), work(1024)
    CTXT, KT, V = work(DC, 512), work(512, parts=64), work(4, 64)
    QT = work(P, parts=64)
    H, QKT, MIXED = work(P, parts=64), work(2, P, parts=64), work(2, SEQ, parts=64)
    POOLED, POOLED_T = work(8, parts=64), work(8, CHUNK, parts=64)
    VB, PICKED, ACTIVE, GATED = work(2, SEQ, parts=64), work(P, parts=64), work(P, parts=64), work(P, parts=64)
    DELTA, PICKS_T, HALF_BH = work(P, parts=64), work(P, parts=64), work(1, parts=64)
    SCORES, REST, WEIGHT, TOP8 = work(SEQ), work(SEQ), work(SEQ), work(8)
    OO1, OT1 = OO[:, 0:64], OT[0:64, 0:P]

    with nc.Fori(0, TILES) as t:
        with nc.Block(no_gpsimd_drain=True) as block:
            @block.sync
            def _(sp):
                sp.dma_start(CTXT.rearrange("p c t -> p (c t)"), stacked("ctxT", t)).then_inc(S("ctxT"), 16)

            @block.vector
            def _(dve):
                c = Chain(dve, S("vector"))
                c.do(nc.vector.tensor_copy(XT.unsqueeze(1), X[:, bass.ds(t, 1), :]))
                normed(c, "l3x")
                c.do(nc.vector.tensor_scalar(HALF_BH, C["l3a_bh"], 0.5, None, ALU.mult))
                dve.wait_ge(S("l3x v"), 1)
                nc.vector.tensor_tensor(V, psS[:, 0:256].rearrange("p (j d) -> p j d", d=64),
                                        C["l3x_bq"].unsqueeze(1).broadcast_to([P, 4, 64]), ALU.add)\
                    .then_inc(S("l3x vs"), 1)
                dve.wait_ge(S("l3x scores"), 1)
                c.do(nc.vector.tensor_reduce(ONE[0][:], psS[:, 512:512 + KEYS], AX, ALU.max))
                nc.vector.tensor_scalar(ONE[1][:], ONE[0][:], -1.0, None, ALU.mult).then_inc(S("l3x max"), 1)
                dve.wait_ge(S("l3x exp"), 1)
                c.do(nc.vector.reciprocal(ONE[3][:], ONE[2][:]))
                nc.vector.tensor_scalar(PR[:, 0:KEYS], PR[:, 0:KEYS], ONE[3][:], None, ALU.mult)\
                    .then_inc(S("l3x probs"), 1)
                residual(dve, c, "l3x", C["l3x_bo"])
                normed(c, "l3a")
                for step in range(2):
                    if step == 0:
                        dve.wait_ge(S("l3a h"), 1)
                    hb = H.rearrange("p (b s) -> p b s", s=SEQ)
                    c.do(nc.vector.tensor_scalar(MIXED.rearrange("p b s -> p (b s)"), H,
                                                 C["l3a_conv"][:, KSIZE - 1:KSIZE], C["l3a_convb"], ALU.mult, ALU.add))
                    for back in range(1, KSIZE):
                        c.do(nc.vector.scalar_tensor_tensor(
                            MIXED[:, :, back:SEQ], hb[:, :, 0:SEQ - back],
                            C["l3a_conv"][:, KSIZE - 1 - back:KSIZE - back], MIXED[:, :, back:SEQ], ALU.mult, ALU.add))
                    c.do(nc.vector.tensor_reduce(POOLED, H.rearrange("p (g s) -> p g s", s=CHUNK), AX, ALU.add))
                    nc.vector.tensor_scalar(POOLED, POOLED, 1.0 / CHUNK, None, ALU.mult).then_inc(S("l3a pooled"), 1)
                    dve.wait_ge(S("l3a pool product"), step + 1)
                    c.do(nc.vector.tensor_scalar(POOLED_T, psA[0:64, 0:8].unsqueeze(2).broadcast_to([64, 8, CHUNK]),
                                                 C["l3a_bp"], None, ALU.add))
                    for b in range(2):
                        c.go(nc.vector.tensor_tensor(VB[:, b, :], psO[0:64, 64 * b:64 * b + 64], C["l3a_bv"], ALU.add))
                    c.settle()
                    nc.vector.tensor_copy(ONE[7][:], MV[:, 0, 0:1]).then_inc(S("l3a inputs"), 1)
                    dve.wait_ge(S("l3a scores"), step + 1)
                    c.do(nc.vector.scalar_tensor_tensor(SCORES, psS[:, 0:SEQ], STATE ** -0.5, K["strict"], ALU.mult, ALU.add))
                    c.do(nc.vector.max(TOP8, SCORES))
                    c.do(nc.vector.match_replace(REST, TOP8, SCORES, TAKEN))
                    nc.vector.tensor_scalar(ONE[0][:], TOP8[:, 0:1], FAR / 10, -1.0, ALU.max, ALU.mult)\
                        .then_inc(S("l3a max"), 1)
                    dve.wait_ge(S("l3a exp"), step + 1)
                    c.do(nc.vector.tensor_scalar(REST, REST, TAKEN / 10, None, ALU.is_lt))
                    c.do(nc.vector.tensor_tensor(WEIGHT, WEIGHT, REST, ALU.mult))
                    c.do(nc.vector.tensor_reduce(ONE[1][:], WEIGHT, AX, ALU.add))
                    c.do(nc.vector.tensor_scalar(ONE[2][:], ONE[1][:], 1e-30, None, ALU.max))
                    c.do(nc.vector.reciprocal(ONE[3][:], ONE[2][:]))
                    nc.vector.tensor_scalar(WEIGHT, WEIGHT, ONE[3][:], None, ALU.mult).then_inc(S("l3a weights"), 1)
                    dve.wait_ge(S("l3a gate"), step + 1)
                    c.do(nc.vector.tensor_scalar(GATED, GATED, 0.5, 0.5, ALU.mult, ALU.add))
                    dve.wait_ge(S("l3a delta"), step + 1)
                    c.do(nc.vector.scalar_tensor_tensor(DELTA, psA[0:64, 512:512 + P], C["l3a_b2"], GATED,
                                                        ALU.add, ALU.mult))
                    nc.vector.tensor_tensor(H, H, DELTA, ALU.add).then_inc(S("l3a updated"), 1)
                    dve.wait_ge(S("l3a updated"), step + 1)
                c.do(nc.vector.tensor_tensor(XT, XT, XN, ALU.add))
                residual(dve, c, "l3a", C["l3a_bo"])
                to_experts_vector(dve, c, t)

            @block.scalar
            def _(act):
                act.wait_ge(S("l3x k"), 1)
                nc.scalar.activation(KT, psA[0:64, 512:1024], ACT.Identity, bias=C["l3x_bqc"]).then_inc(S("l3x ks"), 1)
                transpose_x_scalar(act, "l3x", XNT)
                act.wait_ge(S("l3x q"), 1)
                nc.scalar.activation(QT, psO[0:64, 0:P], ACT.Identity, bias=C["l3x_bqc"]).then_inc(S("l3x qT"), 1)
                act.wait_ge(S("l3x max"), 1)
                act.wait_ge(S("l3x scores"), 1)
                nc.scalar.mul(ONE[4][:], ONE[1][:], D ** -0.5).then_inc(S("l3x bias"), 1)
                act.wait_ge(S("l3x bias"), 1)
                nc.scalar.activation(PR[:, 0:KEYS], psS[:, 512:512 + KEYS], ACT.Exp, bias=ONE[4][:], scale=D ** -0.5,
                                     accum_out=ONE[2][:]).then_inc(S("l3x exp"), 1)
                act.wait_ge(S("l3x probs turned"), 1)
                nc.scalar.copy(PT[:, 0:2 * P], psO[:, 512:512 + 2 * P]).then_inc(S("l3x probsT"), 1)
                act.wait_ge(S("l3x mixed"), 1)
                nc.scalar.copy(OO1, psO[:, 0:64]).then_inc(S("l3x o"), 1)
                act.wait_ge(S("l3x o turned"), 1)
                nc.scalar.copy(OT1, psS[0:64, 0:P]).then_inc(S("l3x oT"), 1)
                transpose_x_scalar(act, "l3a", XNT)
                act.wait_ge(S("l3a input product"), 1)
                nc.scalar.activation(H, psO[0:64, 0:P], ACT.Identity, bias=C["l3a_bi"]).then_inc(S("l3a h"), 1)
                for step in range(2):
                    act.wait_ge(S("l3a qk"), step + 1)
                    nc.scalar.activation(QKT[:, 0, :], psO[0:64, 512:512 + P], ACT.Identity, bias=C["l3a_bq"])\
                        .then_inc(S("l3a qks"), 1)
                    nc.scalar.activation(QKT[:, 1, :], psO[0:64, 640:640 + P], ACT.Identity, bias=C["l3a_bk"])\
                        .then_inc(S("l3a qks"), 1)
                    act.wait_ge(S("l3a gate product"), step + 1)
                    nc.scalar.activation(GATED, psA[0:64, 512:512 + P], ACT.Tanh, scale=0.5, bias=HALF_BH)\
                        .then_inc(S("l3a gate"), 1)
                    act.wait_ge(S("l3a max"), step + 1)
                    nc.scalar.activation(WEIGHT, SCORES, ACT.Exp, bias=ONE[0][:]).then_inc(S("l3a exp"), 1)
                    act.wait_ge(S("l3a weights turned"), step + 1)
                    nc.scalar.copy(PICKS_T, psS[0:64, 512:512 + P]).then_inc(S("l3a weightsT"), 1)
                    act.wait_ge(S("l3a summed"), step + 1)
                    nc.scalar.copy(PICKED, psO[0:64, 0:P]).then_inc(S("l3a picked"), 1)
                    act.wait_ge(S("l3a up"), step + 1)
                    nc.scalar.activation(ACTIVE, psS[0:64, 1024:1024 + P], ACT.Tanh, bias=C["l3a_b1"])\
                        .then_inc(S("l3a tanh"), 1)

            @block.tensor
            def _(pe):
                pe.wait_ge(S("ctxT"), 16)
                product(psA[0:64, 512:1024], lambda i: C["l3x_wq"][:, i, :], lambda i: CTXT[:, i, :], DC)\
                    .then_inc(S("l3x k"), 1)
                for j in range(4):
                    last = product(psS[:, 64 * j:64 * j + 64], lambda i: CTXT[:, i, j * P:(j + 1) * P],
                                   lambda i: C["l3x_wq"][:, i, :], DC)
                last.then_inc(S("l3x v"), 1)
                transpose_x_tensor(pe, "l3x", XN)
                pe.wait_ge(S("l3x xnT"), 1)
                product(psO[0:64, 0:P], lambda i: C["l3x_wq"][:, i, :], lambda i: XNT[:, i, :], DC)\
                    .then_inc(S("l3x q"), 1)
                pe.wait_ge(S("l3x qT"), 1)
                pe.wait_ge(S("l3x ks"), 1)
                for b in range(2):
                    last = nc.tensor.matmul(psS[64 * b:64 * b + 64, 512:512 + KEYS], QT[:, 64 * b:64 * b + 64],
                                            KT[:, KEYS * b:KEYS * (b + 1)], start=True, stop=True)
                last.then_inc(S("l3x scores"), 1)
                pe.wait_ge(S("l3x probs"), 1)
                for i in range(2):
                    last = nc.tensor.transpose(psO[:, 512 + i * P:512 + (i + 1) * P], PR[:, i * P:(i + 1) * P], ident)
                last.then_inc(S("l3x probs turned"), 1)
                pe.wait_ge(S("l3x probsT"), 1)
                pe.wait_ge(S("l3x vs"), 1)
                for b in range(2):
                    last = product(psO[64 * b:64 * b + 64, 0:64], lambda i: PT[:, i * P + 64 * b:i * P + 64 * b + 64],
                                   lambda i: V[:, 2 * b + i, :], 2)
                last.then_inc(S("l3x mixed"), 1)
                pe.wait_ge(S("l3x o"), 1)
                nc.tensor.transpose(psS[0:64, 0:P], OO1, ident).then_inc(S("l3x o turned"), 1)
                pe.wait_ge(S("l3x oT"), 1)
                nc.tensor.matmul(psA[:, 0:D], OT1, C["l3x_wo"], start=True, stop=True).then_inc(S("l3x y"), 1)
                transpose_x_tensor(pe, "l3a", XN)
                pe.wait_ge(S("l3a xnT"), 1)
                product(psO[0:64, 0:P], lambda i: C["l3a_wi"][:, i, :], lambda i: XNT[:, i, :], DC)\
                    .then_inc(S("l3a input product"), 1)
                for step in range(2):
                    if step == 0:
                        pe.wait_ge(S("l3a h"), 1)
                    else:
                        pe.wait_ge(S("l3a updated"), 1)
                    nc.tensor.matmul(psO[0:64, 512:512 + P], C["l3a_wq"], H, start=True, stop=True)
                    nc.tensor.matmul(psO[0:64, 640:640 + P], C["l3a_wk"], H, start=True, stop=True)\
                        .then_inc(S("l3a qk"), 1)
                    for b in range(2):
                        nc.tensor.matmul(psO[0:64, 64 * b:64 * b + 64], H[:, 64 * b:64 * b + 64], C["l3a_wv"],
                                         start=True, stop=True)
                    pe.wait_ge(S("l3a pooled"), step + 1)
                    nc.tensor.matmul(psA[0:64, 0:8], C["l3a_wp"], POOLED, start=True, stop=True)\
                        .then_inc(S("l3a pool product"), 1)
                    nc.tensor.matmul(psA[0:64, 512:512 + P], C["l3a_wh"], H, start=True, stop=True)\
                        .then_inc(S("l3a gate product"), 1)
                    pe.wait_ge(S("l3a qks"), 2 * step + 2)
                    for b in range(2):
                        last = nc.tensor.matmul(psS[64 * b:64 * b + 64, 0:SEQ], QKT[:, 0, 64 * b:64 * b + 64],
                                                QKT[:, 1, 64 * b:64 * b + 64], start=True, stop=True)
                    last.then_inc(S("l3a scores"), 1)
                    pe.wait_ge(S("l3a weights"), step + 1)
                    nc.tensor.transpose(psS[0:64, 512:512 + P], WEIGHT, ident).then_inc(S("l3a weights turned"), 1)
                    pe.wait_ge(S("l3a weightsT"), step + 1)
                    pe.wait_ge(S("l3a inputs"), step + 1)
                    for b in range(2):
                        last = nc.tensor.matmul(psO[0:64, 64 * b:64 * b + 64], VB[:, b, :], PICKS_T[:, 64 * b:64 * b + 64],
                                                start=True, stop=True)
                    last.then_inc(S("l3a summed"), 1)
                    pe.wait_ge(S("l3a picked"), step + 1)
                    parts = [H, MIXED.rearrange("p b s -> p (b s)"), POOLED_T.rearrange("p g s -> p (g s)"), PICKED]
                    product(psS[0:64, 1024:1024 + P], lambda i: C["l3a_w1"][:, i, :], lambda i: parts[i], 4)\
                        .then_inc(S("l3a up"), 1)
                    pe.wait_ge(S("l3a tanh"), step + 1)
                    nc.tensor.matmul(psA[0:64, 512:512 + P], C["l3a_w2"], ACTIVE, start=True, stop=True)\
                        .then_inc(S("l3a delta"), 1)
                pe.wait_ge(S("l3a updated"), 2)
                nc.tensor.matmul(psA[:, 0:D], H, C["l3a_wo"], start=True, stop=True).then_inc(S("l3a y"), 1)
                transpose_x_tensor(pe, "router", XN)
        end()

    experts("l3f", int(round(2 * TOKENS * 1.05 / EXPERTS)), True, None)

    with nc.Block(no_gpsimd_drain=True) as block:
        @block.sync
        def _(sp):
            sp.dma_start(out, X[:]).then_inc(S("stored"), 16)
            sp.wait_ge(S("stored"), 16)


def kernel(**inputs):
    import numpy as np
    import concourse.bacc as bacc
    from concourse.bass_utils import run_bass_kernel_spmd as run

    f = {k: np.asarray(v) for k, v in inputs.items()}

    def rows(w):
        return w.reshape(-1, P, w.shape[1]).transpose(1, 0, 2)

    def bcast(b):
        return np.broadcast_to(b.reshape(1, -1), (P, b.size))

    def cols(b):
        return b.reshape(-1, P).T

    def col(b):
        return b.reshape(-1, 1)

    r = np.arange(P)
    seq = r % SEQ
    inv = 1.0 / 10000.0 ** (np.arange(0, DH, 2, dtype=np.float32) / np.float32(DH))
    angle = np.arange(HEADS, dtype=np.float32)[:, None] * inv[None, :].astype(np.float32)
    rope = np.zeros((D, D), np.float32)
    for h in range(HEADS):
        for j in range(DH // 2):
            a, b = h * DH + 2 * j, h * DH + 2 * j + 1
            cos, sin = np.cos(angle[h, j]), np.sin(angle[h, j])
            rope[a, a], rope[b, a], rope[a, b], rope[b, b] = cos, -sin, sin, cos
    consts = {
        "ident": np.eye(P), "tri": r[:, None] <= r[None, :], "ones": np.ones((P, P)),
        "batch_ones": r[:, None] // SEQ == r[None, :] // SEQ,
        "headmask": (r[:, None] // DH == np.arange(8)[None, :]) * 0.25,
        "causal": np.where(np.arange(SEQ)[None, :] > seq[:, None], FAR, 0.0),
        "strict": np.where(np.arange(SEQ)[None, :] >= seq[:, None], FAR, 0.0),
        "experts": bcast(np.arange(EXPERTS)),
        "rope": np.stack([rope[i * P:(i + 1) * P, i * P:(i + 1) * P] for i in range(DC)], 1),
    }
    g = lambda layer: {k[len(layer) + 1:]: v for k, v in f.items() if k.startswith(layer + "_")}
    x0, a0, x1, a1, f1 = g("L0_xattn"), g("L0_attn"), g("L1_xattn"), g("L1_attn"), g("L1_ffn")
    x2, a2, x3, a3 = g("L2_xattn"), g("L2_attn"), g("L3_xattn"), g("L3_attn")
    wk, wv = x0["Wkv"][:, :64], x0["Wkv"][:, 64:]
    params_a = {
        "l0x_wk": rows(np.concatenate([wk, wk], 1)), "l0x_wv": rows(wv), "l0x_wq": rows(x0["Wq"]),
        "l0x_w1": rows(x0["W1"]), "l0x_wout": rows(x0["Wout"]), "l0x_w2": rows(x0["W2"]),
        "l0x_ln_g": bcast(x0["ln_g"]), "l0x_ln_b": bcast(x0["ln_b"]),
        "l0x_cln_g": bcast(x0["cln_g"]), "l0x_cln_b": bcast(x0["cln_b"]),
        "l0a_wqkv": rows(a0["w_qkv"].T), "l0a_wfc": rows(a0["w_fc"].T), "l0a_bfc": bcast(a0["b_fc"]),
        "l0a_gamma": bcast(a0["gamma"]), "l0a_beta": bcast(a0["beta"]),
    }
    params_b = {
        "l1x_w": rows(x1["W"].T), "l1x_b": bcast(x1["b"]),
        "l1a_wq": rows(a1["wq"]), "l1a_wka": rows(a1["wk_a"].T), "l1a_wkb": rows(a1["wk_b"]),
        "l1a_wva": rows(a1["wv_a"].T), "l1a_wvb": a1["wv_b"].T, "l1a_wo": rows(a1["wo"].T),
        "l1f_ln1_w": bcast(f1["ln1_w"]), "l1f_ln1_b": bcast(f1["ln1_b"]), "l1f_b1": bcast(f1["b1"]),
        "l1f_ln2_w": bcast(f1["ln2_w"]), "l1f_ln2_b": bcast(f1["ln2_b"]), "l1f_b2": bcast(f1["b2"]),
        "l2x_wq": rows(x2["Wq"].T), "l2x_wk": rows(x2["Wk"].T), "l2x_wv": rows(x2["Wv"].T),
        "l2x_wo": rows(x2["Wo"].T), "l2x_bq": cols(x2["bq"]), "l2x_bk": cols(x2["bk"]),
        "l2x_bv": bcast(x2["bv"]), "l2x_bo": bcast(x2["bo"]),
        "l2a_k": rows(a2["k"].T), "l2a_v": rows(a2["v"]),
    }
    bitnet = {"l1f_w1": rows(f1["w1"].T), "l1f_w2": rows(f1["w2"].T)}
    params_c = {
        "l3x_wq": rows(x3["Wq"]), "l3x_bq": bcast(x3["bq"]), "l3x_bqc": col(x3["bq"]), "l3x_wo": x3["Wo"],
        "l3x_bo": bcast(x3["bo"]), "l3a_wi": rows(a3["Wi"]), "l3a_bi": col(a3["bi"]), "l3a_conv": a3["conv_w"].T,
        "l3a_convb": col(a3["conv_b"]), "l3a_wp": a3["Wp"], "l3a_bp": col(a3["bp"]),
        "l3a_wh": np.broadcast_to(a3["Wh"][:, 2:3], (64, 64)), "l3a_bh": np.broadcast_to(a3["bh"][2:3], (64,)).reshape(64, 1),
        "l3a_wq": a3["Wq"], "l3a_bq": col(a3["bq"]), "l3a_wk": a3["Wk"], "l3a_bk": col(a3["bk"]),
        "l3a_wv": a3["Wv"], "l3a_bv": bcast(a3["bv"])[:64], "l3a_w1": a3["W1"].reshape(4, 64, 64).transpose(1, 0, 2),
        "l3a_b1": col(a3["b1"]), "l3a_w2": a3["W2"], "l3a_b2": col(a3["b2"]), "l3a_wo": a3["Wo"], "l3a_bo": bcast(a3["bo"]),
    }

    def pack(params, given):
        parts = []
        for name, n, shape in params:
            a = np.asarray(given[name])
            assert a.shape == (n, *shape), (name, a.shape)
            a = a.reshape(n, -1).astype(np.float32)
            parts.append(np.concatenate([a, np.zeros((P - n, a.shape[1]), np.float32)], 0))
        return np.concatenate(parts, 1)

    def experts(w1, w2):
        w1 = w1.reshape(EXPERTS, DC, P, HID).transpose(0, 2, 1, 3).reshape(EXPERTS, P, -1)
        w2 = w2.reshape(EXPERTS, HB, P, D).transpose(0, 2, 1, 3).reshape(EXPERTS, P, -1)
        return np.concatenate([w1, w2], 2)

    def router(gate_w, b1, b2):
        return pack(ROUTER, {"gate_w": rows(gate_w), "b1": b1.reshape(EXPERTS, HB, P).transpose(2, 0, 1),
                             "b2": b2.reshape(EXPERTS, D)})

    f0, f2, f3 = g("L0_ffn"), g("L2_ffn"), g("L3_ffn")
    ctx = f["ctx_1024"]
    mask_f = f["mask_BxSxS2_ff0"].reshape(TILES, 2, SEQ, KEYS).transpose(0, 2, 1, 3)
    mask_i = f["mask_BxS2_if0"].reshape(TILES, 1, 2, KEYS)[:, :, :, :SEQ]
    mask_b = f["mask_BxS2_bf0"].reshape(TILES, 1, 2, KEYS)
    arrays = {
        "x": f["x"].reshape(TILES, P, D).transpose(1, 0, 2),
        "consts": pack(CONSTS, consts), "params_a": pack(PARAMS_A, params_a), "params_b": pack(PARAMS_B, params_b),
        "params_c": pack(PARAMS_C, params_c), "bitnet": pack(BITNET, bitnet),
        "ctx": ctx.reshape(TILES, 4, P, D).transpose(0, 2, 1, 3),
        "ctx64": ctx[:, :SEQ].reshape(TILES, 2, SEQ, D).transpose(0, 2, 1, 3),
        "ctxT": ctx.reshape(TILES, 512, DC, P).transpose(0, 3, 2, 1),
        "mask_f": np.concatenate([mask_f, mask_f], 1),
        "mask_i": np.broadcast_to(mask_i, (TILES, P, 2, SEQ)),
        "mask_b": np.broadcast_to(mask_b, (TILES, P, 2, KEYS)),
        "l0f_router": router(f0["gate_w"], f0["fc_bias"], f0["proj_bias"]),
        "l2f_router": router(f2["Wg"].T, f2["b1"], f2["b2"]),
        "l3f_router": router(f3["Wg"].T, f3["b1"], f3["b2"]),
        "l0f_experts": experts(f0["c_fc"], f0["c_proj"]),
        "l2f_experts": experts(f2["W1"], f2["W2"]),
        "l3f_experts": experts(f3["W1"], f3["W2"]),
    }
    stacks = ["ctx", "ctx64", "ctxT", "mask_f", "mask_i", "mask_b", "l0f_experts", "l2f_experts", "l3f_experts"]
    for name in stacks:
        a = arrays[name]
        arrays[name] = a.reshape(a.shape[0] * a.shape[1], -1)
    arrays = {k: np.ascontiguousarray(v) for k, v in arrays.items()}
    nc = bacc.Bacc("TRN2", target_bir_lowering=False, num_devices=1)
    dram = {k: nc.dram_tensor(k, v.shape, mybir.dt.from_np(v.dtype), kind="ExternalInput").ap() for k, v in arrays.items()}
    out = nc.dram_tensor("out", (P, TILES, D), F32, kind="ExternalOutput").ap()
    perceiver_kernel(nc, dram, out)
    got = run(nc, [arrays], core_ids=[0]).results[0]["out"]
    return got.reshape(P, TILES, D).transpose(1, 0, 2).reshape(BATCH, SEQ, D)
```

```python
from contextlib import ExitStack
from itertools import zip_longest

import concourse.bass as bass
from concourse import mybir

ALU = mybir.AluOpType
ACT = mybir.ActivationFunctionType
F32 = mybir.dt.float32
BF16 = mybir.dt.bfloat16
I32 = mybir.dt.int32
U32 = mybir.dt.uint32
AX = mybir.AxisListType.X

P = 128
BATCH, SEQ, KEYS, D = 16, 64, 256, 256
TOKENS = BATCH * SEQ
TILES = TOKENS // P
DC = D // P
HEADS, DH = 16, 16
PAIRS = HEADS // 2
EXPERTS, HID = 8, 1024
HB = HID // P
HALF = 512
STATE, KSIZE, CHUNK = 64, 5, 16
EPS = 1e-5
ROUND = 1.5 * 2.0 ** 23
FAR = -1e30
TAKEN = -3e38

CONSTS = [
    ("ident", P, (P,)), ("tri", P, (P,)), ("ones", P, (P,)), ("batch_ones", P, (P,)),
    ("headmask", P, (8,)), ("causal", P, (SEQ,)), ("strict", P, (SEQ,)), ("experts", P, (EXPERTS,)),
    ("rope", P, (DC, P)),
]
PARAMS_A = [
    ("l0x_wk", P, (DC, P)), ("l0x_wv", P, (DC, 64)), ("l0x_wq", P, (DC, 1024)), ("l0x_w1", P, (DC, 2048)),
    ("l0x_wout", P, (8, D)), ("l0x_w2", P, (8, D)), ("l0x_ln_g", P, (D,)), ("l0x_ln_b", P, (D,)),
    ("l0x_cln_g", P, (D,)), ("l0x_cln_b", P, (D,)),
    ("l0a_wqkv", P, (DC, 3 * D)), ("l0a_wfc", P, (DC, D)), ("l0a_bfc", P, (D,)), ("l0a_gamma", P, (D,)),
    ("l0a_beta", P, (D,)),
]
PARAMS_B = [
    ("l1x_w", P, (DC, D)), ("l1x_b", P, (D,)),
    ("l1a_wq", P, (DC, D)), ("l1a_wka", P, (DC, 64)), ("l1a_wkb", P, (DC, 64)), ("l1a_wva", P, (DC, 64)),
    ("l1a_wvb", 64, (D,)), ("l1a_wo", P, (DC, D)),
    ("l1f_ln1_w", P, (D,)), ("l1f_ln1_b", P, (D,)), ("l1f_b1", P, (HID,)),
    ("l1f_ln2_w", P, (HID,)), ("l1f_ln2_b", P, (HID,)), ("l1f_b2", P, (D,)),
]
PARAMS_E = [
    ("l2a_k", P, (DC, 2048)), ("l2x_bq", P, (DC,)), ("l2x_bk", P, (DC,)), ("l2x_bv", P, (D,)), ("l2x_bo", P, (D,)),
    ("l2x_wk", P, (DC, D)), ("l2x_wv", P, (DC, D)),
]
PARAMS_E_LATE = [("l2x_wq", P, (DC, D)), ("l2x_wo", P, (DC, D)), ("l2a_v", P, (16, D))]
BITNET = [("l1f_w1", P, (DC, HID)), ("l1f_w2", P, (HB, D))]
PARAMS_C = [
    ("l3x_wq", P, (DC, 64)), ("l3x_bq", P, (64,)), ("l3x_bqc", 64, (1,)), ("l3x_wo", 64, (D,)), ("l3x_bo", P, (D,)),
    ("l3a_wi", P, (DC, 64)), ("l3a_bi", 64, (1,)), ("l3a_conv", 64, (KSIZE,)), ("l3a_convb", 64, (1,)),
    ("l3a_wp", 64, (64,)), ("l3a_bp", 64, (1,)), ("l3a_wh", 64, (64,)), ("l3a_bh", 64, (1,)),
    ("l3a_wq", 64, (64,)), ("l3a_bq", 64, (1,)), ("l3a_wk", 64, (64,)), ("l3a_bk", 64, (1,)),
    ("l3a_wv", 64, (64,)), ("l3a_bv", 64, (64,)), ("l3a_w1", 64, (4, 64)), ("l3a_b1", 64, (1,)),
    ("l3a_w2", 64, (64,)), ("l3a_b2", 64, (1,)), ("l3a_wo", 64, (D,)), ("l3a_bo", P, (D,)),
]
ROUTER = [("gate_w", P, (DC, EXPERTS)), ("b1", P, (EXPERTS, HB)), ("b2", EXPERTS, (D,))]


def length(shape):
    n = 1
    for s in shape:
        n *= s
    return n


def width(params):
    return sum(length(s) for _, _, s in params)


def view(region, at, shape, parts=P):
    flat = region[0:parts, at:at + length(shape)]
    if len(shape) == 2:
        return flat.rearrange("p (a b) -> p a b", b=shape[1])
    if len(shape) == 3:
        return flat.rearrange("p (a b c) -> p a b c", b=shape[1], c=shape[2])
    return flat


def views(region, params):
    at, out = 0, {}
    for name, parts, shape in params:
        out[name] = view(region, at, shape, parts)
        at += length(shape)
    return out


class Work:

    def __init__(self, region):
        self.region, self.at = region, 0

    def __call__(self, *shape, parts=P):
        out = view(self.region, self.at, shape, parts)
        self.at += length(shape)
        assert self.at <= self.region.shape[1], self.at
        return out


def in_turn(*programs):
    for _ in zip_longest(*programs):
        pass


class Chain:

    def __init__(self, eng, sem):
        self.eng, self.sem, self.n = eng, sem, 0

    def go(self, ins):
        ins.then_inc(self.sem, 1)
        self.n += 1

    def settle(self):
        self.eng.wait_ge(self.sem, self.n)

    def do(self, ins):
        self.go(ins)
        self.settle()


class Signals:

    def __init__(self, nc, ctx, count):
        self.free = [ctx.enter_context(nc.semaphore(f"signal{n}")) for n in range(count)]
        self.all = range(self.free[0].num, self.free[-1].num + 1)
        self.named = {}

    def __call__(self, name):
        if name not in self.named:
            self.named[name] = self.free[len(self.named)]
        return self.named[name]

    def forget(self):
        self.named = {}


def perceiver_kernel(nc, dram, out):
    with ExitStack() as ctx:
        build(nc, ctx, dram, out)


def build(nc, ctx, dram, out):
    def sb(name, shape, dt=F32):
        return ctx.enter_context(nc.sbuf_tensor(name, shape, dt))

    X = sb("X", [P, TILES, D])
    XNT_ALL = sb("XNT_all", [P, DC, TOKENS])
    CONST = sb("constants", [P, width(CONSTS)])
    PARAM = sb("params", [P, max(width(PARAMS_A), width(PARAMS_B) + width(PARAMS_E))])
    W1Q = sb("w1_ternary", [P, DC, HID], BF16)
    W2Q = sb("w2_ternary", [P, HB, D], BF16)
    IDB = sb("identity_bf16", [P, P], BF16)
    REGION = sb("work", [P, 21600])
    GATES = sb("gates", [P, TILES, EXPERTS])
    GATE = sb("gate_of_expert", [P, 2, TILES])
    BIAS = sb("bias_of_expert", [P, 2, HB])
    RT = sb("router_params", [P, width(ROUTER)])
    WSCALE = sb("ternary_scales", [P, 2])
    RECS2 = sb("ternary_recs", [P, 2])
    ABS = sb("ternary_abs", [P, 2])
    PS = ctx.enter_context(nc.psum_tensor("PS", [P, 4096], F32))

    K = views(CONST, CONSTS)
    R = views(RT, ROUTER)
    ident = K["ident"]
    S = Signals(nc, ctx, 150)

    class Lane:

        def __init__(self, n):
            self.n = n
            at = 2048 * n
            self.psS, self.psA, self.psO = PS[:, at:at + 1024], PS[:, at + 1024:at + 1536], PS[:, at + 1536:at + 2048]
            self.stats = sb(f"bn_stats{n}", [P, 4, 2, 6])
            self.mv = sb(f"mean_var{n}", [P, 4, 2])
            self.var, self.rstd, self.tmp = (sb(f"{x}{n}", [P, 4]) for x in ("var", "rstd", "newton"))
            self.maxes, self.sums, self.recs = (sb(f"{x}{n}", [P, PAIRS]) for x in ("maxes", "sums", "recs"))
            self.one = [sb(f"scalar{n}_{m}", [P, 1]) for m in range(8)]

        def S(self, name):
            return S(f"lane {self.n}: {name}")

    LANES = [Lane(0), Lane(1)]

    def end():
        nc.all_engine_barrier(sems_to_clear=S.all)
        S.forget()

    def stacked(name, i):
        return dram[name][bass.ds(i * P, P), :]

    def rstd_of(L, c, n, var, eps):
        v, y, w = L.var[:, 0:n], L.rstd[:, 0:n], L.tmp[:, 0:n]
        c.do(nc.vector.tensor_scalar(v, var, eps, None, ALU.add))
        c.do(nc.vector.tensor_scalar(y.bitcast(I32), v.bitcast(I32), 1, None, ALU.logical_shift_right))
        c.do(nc.vector.tensor_scalar(y.bitcast(I32), y.bitcast(I32), -1.0, float(0x5F3759DF), ALU.mult, ALU.add))
        for _ in range(3):
            c.do(nc.vector.tensor_tensor(w, y, y, ALU.mult))
            c.do(nc.vector.scalar_tensor_tensor(w, w, -0.5, v, ALU.mult, ALU.mult))
            c.do(nc.vector.scalar_tensor_tensor(y, w, 1.5, y, ALU.add, ALU.mult))

    def layer_norm(L, c, pairs):
        n = len(pairs)
        for j, (src, _) in enumerate(pairs):
            wide = src.shape[1]
            chunks = max(1, wide // 512)
            for k in range(chunks):
                c.go(nc.vector.bn_stats(L.stats[:, j, k, :], src[:, k * wide // chunks:(k + 1) * wide // chunks]))
        c.settle()
        for j in range(n):
            c.go(nc.vector.bn_aggr(L.mv[:, j, :], L.stats[:, j, 0:chunks, :].rearrange("p k s -> p (k s)")))
        c.settle()
        rstd_of(L, c, n, L.mv[:, 0:n, 1], EPS)
        for j, (src, dst) in enumerate(pairs):
            c.go(nc.vector.tensor_scalar(dst, src, L.mv[:, j, 0:1], L.rstd[:, j:j + 1], ALU.subtract, ALU.mult))
        c.settle()

    def affine(c, x, g, b):
        c.do(nc.vector.tensor_tensor(x, x, g, ALU.mult))
        c.do(nc.vector.tensor_tensor(x, x, b, ALU.add))

    def product(out_, lhsT, rhs, n, first=True, last_=True):
        for i in range(n):
            last = nc.tensor.matmul(out_, lhsT(i), rhs(i), start=(first and i == 0), stop=(last_ and i == n - 1))
        return last

    def transpose_x_tensor(L, pe, tag):
        yield
        pe.wait_ge(L.S(tag + " normed"), 1)
        for c in range(DC):
            last = nc.tensor.transpose(L.psA[:, c * P:(c + 1) * P], L.XN[:, c * P:(c + 1) * P], ident)
        last.then_inc(L.S(tag + " turned"), 1)

    def transpose_x_scalar(L, act, tag):
        yield
        act.wait_ge(L.S(tag + " turned"), 1)
        nc.scalar.copy(L.XNT.rearrange("p c t -> p (c t)"), L.psA[:, 0:D]).then_inc(L.S(tag + " xnT"), 1)

    def units(nk):
        n = min(PAIRS, 1024 // nk)
        return [(b, range(g, g + n)) for g in range(0, PAIRS, n) for b in range(2)]

    def attention_tensor(L, pe, tag, nk, dv, query, key, value, column, ready, between=None):
        kc = min(nk, P)
        nkc = nk // kc
        yield
        for name, count in ready:
            pe.wait_ge(L.S(name), count)
        for u, (b, pairs) in enumerate(units(nk)):
            if u and between:
                yield from between(u)
            for n, p in enumerate(pairs):
                last = nc.tensor.matmul(L.psS[:, n * nk:(n + 1) * nk], query(b, p), key(b, p), start=True, stop=True)
            last.then_inc(L.S(tag + " scores"), 1)
            yield
            pe.wait_ge(L.S(tag + " probs"), u + 1)
            for i in range(len(pairs) * nkc):
                last = nc.tensor.transpose(L.psS[0:kc, i * P:(i + 1) * P], L.PR[:, i * kc:(i + 1) * kc], ident)
            last.then_inc(L.S(tag + " probs turned"), 1)
            yield
            pe.wait_ge(L.S(tag + " probsT"), u + 1)
            for n, p in enumerate(pairs):
                for s in range(2):
                    at = column(p, s)
                    last = product(
                        L.psO[64 * b:64 * b + 64, at:at + dv],
                        lambda c: L.PT[0:kc, (n * nkc + c) * P + 64 * s:(n * nkc + c) * P + 64 * s + 64],
                        lambda c: value(b, c, p, s), nkc)
            last.then_inc(L.S(tag + " mixed"), 1)

    def attention_vector(L, dve, c, tag, nk, mask):
        for u, (b, pairs) in enumerate(units(nk)):
            n = len(pairs)
            yield
            dve.wait_ge(L.S(tag + " scores"), u + 1)
            src = L.psS[:, 0:n * nk].rearrange("p (h k) -> p h k", k=nk)
            if mask is not None:
                sm = L.SM[:, 0:n * nk].rearrange("p (h k) -> p h k", k=nk)
                c.do(nc.vector.tensor_tensor(sm, src, mask(b).unsqueeze(1).broadcast_to([P, n, nk]), ALU.add))
                src = sm
            c.do(nc.vector.tensor_reduce(L.maxes[:, 0:n], src, AX, ALU.max))
            nc.vector.tensor_scalar(L.maxes[:, 0:n], L.maxes[:, 0:n], -1.0, None, ALU.mult)\
                .then_inc(L.S(tag + " max"), 1)
            yield
            dve.wait_ge(L.S(tag + " exp"), (u + 1) * n)
            c.do(nc.vector.reciprocal(L.recs[:, 0:n], L.sums[:, 0:n]))
            pr = L.PR[:, 0:n * nk].rearrange("p (h k) -> p h k", k=nk)
            nc.vector.tensor_tensor(pr, pr, L.recs[:, 0:n].unsqueeze(2).broadcast_to([P, n, nk]), ALU.mult)\
                .then_inc(L.S(tag + " probs"), 1)

    def attention_scalar(L, act, tag, nk, mask, after=None):
        kc = min(nk, P)
        src = L.psS if mask is None else L.SM
        for u, (b, pairs) in enumerate(units(nk)):
            n = len(pairs)
            yield
            act.wait_ge(L.S(tag + " max"), u + 1)
            for p in range(n):
                nc.scalar.activation(L.PR[:, p * nk:(p + 1) * nk], src[:, p * nk:(p + 1) * nk], ACT.Exp,
                                     bias=L.maxes[:, p:p + 1], accum_out=L.sums[:, p:p + 1])\
                    .then_inc(L.S(tag + " exp"), 1)
            yield
            act.wait_ge(L.S(tag + " probs turned"), u + 1)
            m = n * (nk // kc) * P
            nc.scalar.copy(L.PT[0:kc, 0:m], L.psS[0:kc, 0:m]).then_inc(L.S(tag + " probsT"), 1)
            if after:
                yield from after(u)

    def project_tensor(L, pe, tag, weight):
        yield
        pe.wait_ge(L.S(tag + " o"), 1)
        for i in range(DC):
            last = nc.tensor.transpose(L.psS[:, i * P:(i + 1) * P], L.OO[:, i * P:(i + 1) * P], ident)
        last.then_inc(L.S(tag + " o turned"), 1)
        yield
        pe.wait_ge(L.S(tag + " oT"), 1)
        product(L.psA[:, 0:D], lambda i: L.OT[:, i * P:(i + 1) * P], lambda i: weight[:, i, :], DC)\
            .then_inc(L.S(tag + " y"), 1)

    def project_scalar(L, act, tag, count):
        yield
        act.wait_ge(L.S(tag + " mixed"), count)
        nc.scalar.copy(L.OO[:, 0:D], L.psO[:, 0:D]).then_inc(L.S(tag + " o"), 1)
        yield
        act.wait_ge(L.S(tag + " o turned"), 1)
        nc.scalar.copy(L.OT[:, 0:D], L.psS[:, 0:D]).then_inc(L.S(tag + " oT"), 1)

    def residual(L, dve, c, tag, bias):
        yield
        dve.wait_ge(L.S(tag + " y"), 1)
        c.do(nc.vector.tensor_tensor(L.XT, L.XT, L.psA[:, 0:D], ALU.add))
        if bias is not None:
            c.do(nc.vector.tensor_tensor(L.XT, L.XT, bias, ALU.add))

    def tell(L, name):
        nc.vector.tensor_copy(L.one[7][:], L.mv[:, 0, 0:1]).then_inc(L.S(name), 1)

    def normed(L, c, tag):
        layer_norm(L, c, [(L.XT, L.XN)])
        tell(L, tag + " normed")

    def fetch_tile(L, c, t):
        c.do(nc.vector.tensor_copy(L.XT.unsqueeze(1), X[:, bass.ds(t, 1), :]))

    def to_experts_vector(L, dve, c, t):
        c.do(nc.vector.tensor_copy(X[:, bass.ds(t, 1), :], L.XT.unsqueeze(1)))
        normed(L, c, "router")
        yield
        dve.wait_ge(L.S("router turned"), 1)
        c.do(nc.vector.tensor_copy(XNT_ALL[:, :, bass.ds(t * P, P)], L.psA[:, 0:D].rearrange("p (c t) -> p c t", t=P)))

    def head_queries(L, c, src, tag):
        for blk in range(DC):
            for b in range(2):
                at = 8 * (2 * blk + b)
                c.go(nc.vector.tensor_tensor(
                    L.QBD[:, at:at + 8, :],
                    src[:, blk, 64 * b:64 * b + 64].unsqueeze(1).broadcast_to([P, 8, SEQ]),
                    K["headmask"].unsqueeze(2).broadcast_to([P, 8, SEQ]), ALU.mult))
        c.settle()
        tell(L, tag + " queries")

    def masked_query(L):
        def query(b, p):
            at = 8 * (2 * (p // 4) + b) + 2 * (p % 4)
            return L.QBD[:, at:at + 2, :].rearrange("p h t -> p (h t)")
        return query

    def column16(p, s):
        return (2 * p + s) * DH

    def lanes_block(i, load, vector, scalar, tensor):
        with nc.Block(no_gpsimd_drain=True) as block:
            @block.sync
            def _(sp):
                for L in LANES:
                    load(L, sp, 2 * i + L.n)

            @block.vector
            def _(dve):
                in_turn(*(vector(L, dve, Chain(dve, L.S("vector")), 2 * i + L.n) for L in LANES))

            @block.scalar
            def _(act):
                in_turn(*(scalar(L, act) for L in LANES))

            @block.tensor
            def _(pe):
                in_turn(*(tensor(L, pe) for L in LANES))
        end()

    with nc.Block(no_gpsimd_drain=True) as block:
        @block.sync
        def _(sp):
            sp.dma_start(X[:], dram["x"]).then_inc(S("loaded"), 16)
            sp.dma_start(CONST[:], dram["consts"]).then_inc(S("loaded"), 16)
            sp.dma_start(PARAM[:, 0:width(PARAMS_A)], dram["params_a"]).then_inc(S("loaded"), 16)
            sp.wait_ge(S("loaded"), 48)
    end()

    A = views(PARAM, PARAMS_A)
    work = Work(REGION)
    for L in LANES:
        L.XT, L.XN, L.XNT = work(D), work(D), work(DC, P)
        L.SM, L.PR, L.PT = work(1024), work(1024), work(1024)
        L.OO, L.OT = work(512), work(512)
        L.CTX, L.CTXT = work(4, D), work(DC, 512)
        L.KT, L.V, L.QT = work(512), work(4, 64), work(2, 8, SEQ)
        L.MASK = work(2, KEYS)
        L.HH, L.HHT = work(1024), L.CTX.rearrange("p j d -> p (j d)")
        L.V256 = L.HHT[:, 0:D]
        L.QK = L.HH[:, 0:512].rearrange("p (c t) -> p c t", t=P)

    def a_load(L, sp, t):
        sp.dma_start(L.CTX.rearrange("p j d -> p (j d)"), stacked("ctx", t)).then_inc(L.S("ctx"), 16)
        sp.dma_start(L.MASK.rearrange("p b k -> p (b k)"), stacked("mask_f", t)).then_inc(L.S("mask"), 16)

    def a_vector(L, dve, c, t):
        dve.wait_ge(L.S("ctx"), 16)
        layer_norm(L, c, [(L.CTX[:, j, :], L.CTX[:, j, :]) for j in range(4)])
        c.do(nc.vector.tensor_tensor(L.CTX, L.CTX, A["l0x_cln_g"].unsqueeze(1).broadcast_to([P, 4, D]), ALU.mult))
        nc.vector.tensor_tensor(L.CTX, L.CTX, A["l0x_cln_b"].unsqueeze(1).broadcast_to([P, 4, D]), ALU.add)\
            .then_inc(L.S("ctx normed"), 1)
        fetch_tile(L, c, t)
        yield
        layer_norm(L, c, [(L.XT, L.XN)])
        layer_norm(L, c, [(L.XN, L.XN)])
        affine(c, L.XN, A["l0x_ln_g"], A["l0x_ln_b"])
        tell(L, "l0x normed")
        for h in range(2):
            yield
            dve.wait_ge(L.S("tanh"), h + 1)
            hh = L.HH[:, 512 * h:512 * h + 512]
            c.do(nc.vector.scalar_tensor_tensor(hh, L.OO, 1.0, L.psS[:, 512:1024], ALU.add, ALU.mult))
            nc.vector.scalar_tensor_tensor(hh, hh, 0.5, L.psS[:, 0:512], ALU.mult, ALU.mult)\
                .then_inc(L.S("gated"), 1)
        dve.wait_ge(L.S("mask"), 16)
        yield from attention_vector(L, dve, c, "l0x", KEYS, lambda b: L.MASK[:, b, :])
        yield from residual(L, dve, c, "l0x", None)
        normed(L, c, "l0a")
        yield
        dve.wait_ge(L.S("l0a qkv"), 1)
        nc.vector.tensor_copy(L.V256, L.psO[:, 0:D]).then_inc(L.S("l0a values"), 1)
        yield
        dve.wait_ge(L.S("l0a scores"), 1)
        c.do(nc.vector.tensor_reduce(L.one[0][:], L.psS[:, 512:576], AX, ALU.max))
        nc.vector.tensor_scalar(L.one[1][:], L.one[0][:], -1.0, None, ALU.mult).then_inc(L.S("l0a max"), 1)
        yield
        dve.wait_ge(L.S("l0a exp"), 1)
        c.do(nc.vector.reciprocal(L.one[3][:], L.one[2][:]))
        c.do(nc.vector.tensor_scalar(L.PR[:, 0:64], L.PR[:, 0:64], L.one[3][:], None, ALU.mult))
        c.do(nc.vector.tensor_reduce(L.one[4][:], L.PR[:, 0:64], AX, ALU.add))
        dve.wait_ge(L.S("l0a value sums"), 1)
        nc.vector.tensor_scalar(L.OO[:, 0:D], L.psO[:, 0:D], L.one[4][:], None, ALU.mult).then_inc(L.S("l0a o"), 1)
        yield
        dve.wait_ge(L.S("l0a y"), 1)
        c.do(nc.vector.tensor_tensor(L.XN, L.XN, L.psA[:, 0:D], ALU.add))
        c.do(nc.vector.tensor_tensor(L.XN, L.XN, A["l0a_bfc"], ALU.add))
        layer_norm(L, c, [(L.XN, L.XN)])
        affine(c, L.XN, A["l0a_gamma"], A["l0a_beta"])
        c.do(nc.vector.tensor_tensor(L.XT, L.XT, L.XN, ALU.add))
        yield from to_experts_vector(L, dve, c, t)

    def a_scalar(L, act):
        yield
        act.wait_ge(L.S("ctx turned"), 1)
        nc.scalar.copy(L.CTXT.rearrange("p c t -> p (c t)"), L.psS).then_inc(L.S("ctxT"), 1)
        yield
        act.wait_ge(L.S("l0x kv"), 1)
        nc.scalar.copy(L.KT, L.psA).then_inc(L.S("l0x kvs"), 1)
        nc.scalar.copy(L.V.rearrange("p j d -> p (j d)"), L.psO[:, 0:256]).then_inc(L.S("l0x kvs"), 1)
        yield from transpose_x_scalar(L, act, "l0x")
        yield
        act.wait_ge(L.S("l0x q"), 1)
        nc.scalar.mul(L.QT.rearrange("p b h t -> p h b t"),
                      L.psS.rearrange("p (h b t) -> p h b t", b=2, t=SEQ), 0.125).then_inc(L.S("l0x qT"), 1)
        for h in range(2):
            yield
            act.wait_ge(L.S("hidden"), h + 1)
            nc.scalar.activation(L.OO, L.psS[:, 512:1024], ACT.Tanh, scale=0.5).then_inc(L.S("tanh"), 1)
        yield
        act.wait_ge(L.S("hidden turned"), 1)
        nc.scalar.copy(L.HHT, L.psS).then_inc(L.S("hiddenT"), 1)

        def evict(u):
            if u % 2:
                yield
                act.wait_ge(L.S("l0x mixed"), u + 1)
                nc.scalar.copy(L.OO, L.psO).then_inc(L.S("l0x o"), 1)
                yield
                act.wait_ge(L.S("l0x o turned"), u // 2 + 1)
                nc.scalar.copy(L.OT, L.psS[:, 0:512]).then_inc(L.S("l0x oT"), 1)

        yield from attention_scalar(L, act, "l0x", KEYS, True, evict)
        yield from transpose_x_scalar(L, act, "l0a")
        yield
        act.wait_ge(L.S("l0a qkv"), 1)
        nc.scalar.mul(L.QK[:, 0:2, :], L.psS[:, 0:256].rearrange("p (c t) -> p c t", t=P), D ** -0.5)\
            .then_inc(L.S("l0a qk"), 1)
        nc.scalar.copy(L.QK[:, 2:4, :], L.psS[:, 256:512].rearrange("p (c t) -> p c t", t=P))\
            .then_inc(L.S("l0a qk"), 1)
        yield
        act.wait_ge(L.S("l0a max"), 1)
        nc.scalar.activation(L.PR[:, 0:64], L.psS[:, 512:576], ACT.Exp, bias=L.one[1][:], accum_out=L.one[2][:])\
            .then_inc(L.S("l0a exp"), 1)
        yield
        act.wait_ge(L.S("l0a o turned"), 1)
        nc.scalar.copy(L.OT[:, 0:D], L.psS[:, 0:D]).then_inc(L.S("l0a oT"), 1)

    def a_tensor(L, pe):
        yield
        pe.wait_ge(L.S("ctx normed"), 1)
        for c in range(DC):
            for j in range(4):
                last = nc.tensor.transpose(L.psS[:, c * 512 + j * P:c * 512 + (j + 1) * P],
                                           L.CTX[:, j, c * P:(c + 1) * P], ident)
        last.then_inc(L.S("ctx turned"), 1)
        yield
        pe.wait_ge(L.S("ctxT"), 1)
        product(L.psA, lambda i: A["l0x_wk"][:, i, :], lambda i: L.CTXT[:, i, :], DC)
        for j in range(4):
            last = product(L.psO[:, 64 * j:64 + 64 * j], lambda i: L.CTXT[:, i, j * P:(j + 1) * P],
                           lambda i: A["l0x_wv"][:, i, :], DC)
        last.then_inc(L.S("l0x kv"), 1)
        yield
        pe.wait_ge(L.S("l0x kvs"), 2)
        yield from transpose_x_tensor(L, pe, "l0x")
        yield
        pe.wait_ge(L.S("l0x xnT"), 1)
        for j in range(8):
            last = product(L.psS[:, j * P:(j + 1) * P], lambda i: A["l0x_wq"][:, i, j * P:(j + 1) * P],
                           lambda i: L.XNT[:, i, :], DC)
        last.then_inc(L.S("l0x q"), 1)
        yield
        pe.wait_ge(L.S("l0x qT"), 1)
        for h in range(2):
            for j in range(2):
                last = product(L.psS[:, j * 512:(j + 1) * 512], lambda i: L.XNT[:, i, :],
                               lambda i: A["l0x_w1"][:, i, (2 * h + j) * 512:(2 * h + j + 1) * 512], DC)
            last.then_inc(L.S("hidden"), 1)
            yield
            pe.wait_ge(L.S("gated"), h + 1)
        for i in range(8):
            last = nc.tensor.transpose(L.psS[:, i * P:(i + 1) * P], L.HH[:, i * P:(i + 1) * P], ident)
        last.then_inc(L.S("hidden turned"), 1)
        yield
        pe.wait_ge(L.S("hiddenT"), 1)
        product(L.psA[:, 0:D], lambda i: L.HHT[:, i * P:(i + 1) * P], lambda i: A["l0x_w2"][:, i, :], 8, last_=False)

        def query(b, p):
            r, k = p // 4, p % 4
            return L.QT[64 * r:64 * r + 64, b, 2 * k:2 * k + 2, :].rearrange("p h t -> p (h t)")

        def out_of_four_pairs(u):
            if u % 2 == 0:
                g = u // 2 - 1
                yield
                pe.wait_ge(L.S("l0x o"), g + 1)
                for i in range(4):
                    last = nc.tensor.transpose(L.psS[:, i * P:(i + 1) * P], L.OO[:, i * P:(i + 1) * P], ident)
                last.then_inc(L.S("l0x o turned"), 1)
                yield
                pe.wait_ge(L.S("l0x oT"), g + 1)
                last = product(L.psA[:, 0:D], lambda i: L.OT[:, i * P:(i + 1) * P],
                               lambda i: A["l0x_wout"][:, 4 * g + i, :], 4, first=False, last_=(g == 1))
                if g == 1:
                    last.then_inc(L.S("l0x y"), 1)

        yield from attention_tensor(
            L, pe, "l0x", KEYS, 64, query,
            lambda b, p: L.KT[64 * (p // 4):64 * (p // 4) + 64, 256 * b:256 * b + 256],
            lambda b, c, p, s: L.V[:, 2 * b + c, :], lambda p, s: 64 * (2 * (p % 4) + s),
            [("gated", 2)], out_of_four_pairs)
        yield from out_of_four_pairs(4)
        yield from transpose_x_tensor(L, pe, "l0a")
        yield
        pe.wait_ge(L.S("l0a xnT"), 1)
        for j in range(4):
            product(L.psS[:, j * P:(j + 1) * P], lambda i: A["l0a_wqkv"][:, i, j * P:(j + 1) * P],
                    lambda i: L.XNT[:, i, :], DC)
        product(L.psO[:, 0:D], lambda i: L.XNT[:, i, :], lambda i: A["l0a_wqkv"][:, i, 2 * D:3 * D], DC)\
            .then_inc(L.S("l0a qkv"), 1)
        yield
        pe.wait_ge(L.S("l0a qk"), 2)
        for b in range(2):
            last = product(L.psS[64 * b:64 * b + 64, 512:576], lambda i: L.QK[:, i, 64 * b:64 * b + 64],
                           lambda i: L.QK[:, 2 + i, 64 * b:64 * b + 64], DC)
        last.then_inc(L.S("l0a scores"), 1)
        pe.wait_ge(L.S("l0a values"), 1)
        nc.tensor.matmul(L.psO[:, 0:D], K["batch_ones"], L.V256, start=True, stop=True)\
            .then_inc(L.S("l0a value sums"), 1)
        yield from project_tensor(L, pe, "l0a", A["l0a_wfc"])
        yield from transpose_x_tensor(L, pe, "router")

    with nc.Fori(0, TILES // 2) as i:
        lanes_block(i, a_load, a_vector, a_scalar, a_tensor)

    def experts(layer, capacity, softmax_first, next_params):
        work = Work(REGION)
        PSA, PSO = PS[:, 2048:3072], PS[:, 3072:4096]
        WEIGHTS = [work(4096), work(4096)]
        W1 = [w[:, 0:2048].rearrange("p (c h) -> p c h", h=HID) for w in WEIGHTS]
        W2 = [w[:, 2048:4096].rearrange("p (j d) -> p j d", d=D) for w in WEIGHTS]
        HT = [work(HB, HALF), work(HB, HALF)]
        router = Work(REGION[:, 8192:16384])
        LG, VALUES, TOP = router(TILES, EXPERTS), router(TILES, EXPERTS), router(TILES, 8)
        INDEX, INDEXF = router(TILES, 8), router(TILES, 8)
        CHOICE, RANK, PREFIX = router(2, TILES, EXPERTS), router(2, TILES, EXPERTS), router(2, TILES, EXPERTS)
        W = router(2, TILES)
        GATE_ROWS = router(TILES, P, parts=EXPERTS)
        A8, B8 = router(TILES), router(TILES)
        choice16 = CHOICE.rearrange("p k t e -> p (k t) e")
        prefix16 = PREFIX.rearrange("p k t e -> p (k t) e")

        with nc.Block(no_gpsimd_drain=True) as block:
            @block.sync
            def _(sp):
                sp.dma_start(RT[:], dram[layer + "_router"]).then_inc(S("router params"), 16)
                sp.dma_start(WEIGHTS[0], dram[layer + "_experts"][0:P, :]).then_inc(S("weights"), 16)
                for name, at, params in next_params:
                    sp.dma_start(PARAM[:, at:at + width(params)], dram[name]).then_inc(S("next params"), 16)
                sp.wait_ge(S("weights"), 16)
                if next_params:
                    sp.wait_ge(S("next params"), 16 * len(next_params))

            @block.tensor
            def _(pe):
                pe.wait_ge(S("router params"), 16)
                for t in range(TILES):
                    last = product(PS[:, t * EXPERTS:(t + 1) * EXPERTS], lambda i: XNT_ALL[:, i, t * P:(t + 1) * P],
                                   lambda i: R["gate_w"][:, i, :], DC)
                last.then_inc(S("logits"), 1)
                if capacity:
                    pe.wait_ge(S("choices"), 1)
                    nc.tensor.matmul(PSA[:, 0:128], K["tri"], choice16.rearrange("p n e -> p (n e)"),
                                     start=True, stop=True)
                    nc.tensor.matmul(PSA[:, 512:640], K["ones"], choice16.rearrange("p n e -> p (n e)"),
                                     start=True, stop=True).then_inc(S("counts"), 1)
                pe.wait_ge(S("gates"), 1)
                for t in range(TILES):
                    last = nc.tensor.transpose(PSO[0:EXPERTS, t * P:(t + 1) * P], GATES[:, t, :], ident)
                last.then_inc(S("gates turned"), 1)
                pe.wait_ge(S("gate rows"), 1)
                for t in range(TILES):
                    last = nc.tensor.matmul(PS[:, t * D:(t + 1) * D], GATE_ROWS[:, t, :], R["b2"], start=True, stop=True)
                last.then_inc(S("biases"), 1)

            @block.scalar
            def _(act):
                act.wait_ge(S("to exp"), 1)
                if softmax_first:
                    nc.scalar.activation(VALUES, VALUES, ACT.Exp).then_inc(S("exp"), 1)
                else:
                    nc.scalar.activation(A8, A8, ACT.Exp).then_inc(S("exp"), 1)
                act.wait_ge(S("gates turned"), 1)
                nc.scalar.copy(GATE_ROWS.rearrange("p t n -> p (t n)"), PSO[0:EXPERTS, :]).then_inc(S("gate rows"), 1)

            @block.vector
            def _(dve):
                c = Chain(dve, S("vector"))
                dve.wait_ge(S("logits"), 1)
                c.do(nc.vector.tensor_copy(LG.rearrange("p t e -> p (t e)"), PS[:, 0:TILES * EXPERTS]))
                values = LG
                if softmax_first:
                    c.do(nc.vector.tensor_reduce(A8, LG, AX, ALU.max))
                    nc.vector.tensor_tensor(VALUES, LG, A8.unsqueeze(2).broadcast_to([P, TILES, EXPERTS]),
                                            ALU.subtract).then_inc(S("to exp"), 1)
                    dve.wait_ge(S("exp"), 1)
                    c.do(nc.vector.tensor_reduce(A8, VALUES, AX, ALU.add))
                    c.do(nc.vector.reciprocal(B8, A8))
                    c.do(nc.vector.tensor_tensor(VALUES, VALUES, B8.unsqueeze(2).broadcast_to([P, TILES, EXPERTS]),
                                                 ALU.mult))
                    values = VALUES
                for t in range(TILES):
                    c.go(nc.vector.max(TOP[:, t, :], values[:, t, :]))
                c.settle()
                for t in range(TILES):
                    c.go(nc.vector.max_index(INDEX[:, t, :].bitcast(U32), TOP[:, t, :], values[:, t, :]))
                c.settle()
                c.do(nc.vector.tensor_copy(INDEXF, INDEX.bitcast(U32)))
                for k in range(2):
                    c.go(nc.vector.tensor_tensor(
                        CHOICE[:, k, :, :], K["experts"].unsqueeze(1).broadcast_to([P, TILES, EXPERTS]),
                        INDEXF[:, :, k:k + 1].broadcast_to([P, TILES, EXPERTS]), ALU.is_equal))
                c.settle()
                if capacity:
                    nc.vector.tensor_copy(RECS2[:, 0:1], CHOICE[:, 0, 0, 0:1]).then_inc(S("choices"), 1)
                if softmax_first:
                    for k in range(2):
                        c.go(nc.vector.tensor_copy(W[:, k, :], TOP[:, :, k]))
                    c.settle()
                else:
                    nc.vector.tensor_tensor(A8, TOP[:, :, 1], TOP[:, :, 0], ALU.subtract).then_inc(S("to exp"), 1)
                    dve.wait_ge(S("exp"), 1)
                    c.do(nc.vector.tensor_scalar(B8, A8, 1.0, None, ALU.add))
                    c.do(nc.vector.reciprocal(W[:, 0, :], B8))
                    c.do(nc.vector.tensor_tensor(W[:, 1, :], A8, W[:, 0, :], ALU.mult))
                if capacity:
                    dve.wait_ge(S("counts"), 1)
                    c.do(nc.vector.memset(prefix16[:, 0, :], 0.0))
                    for n in range(1, 2 * TILES):
                        c.do(nc.vector.tensor_tensor(prefix16[:, n, :], prefix16[:, n - 1, :],
                                                     PSA[:, 512 + (n - 1) * EXPERTS:512 + n * EXPERTS], ALU.add))
                    rank = RANK.rearrange("p k t e -> p (k t e)")
                    c.do(nc.vector.tensor_tensor(rank, PSA[:, 0:128], PREFIX.rearrange("p k t e -> p (k t e)"), ALU.add))
                    c.do(nc.vector.tensor_scalar(rank, rank, capacity + 0.5, None, ALU.is_lt))
                    c.do(nc.vector.tensor_tensor(choice16, choice16, RANK.rearrange("p k t e -> p (k t) e"), ALU.mult))
                c.do(nc.vector.tensor_tensor(choice16, choice16,
                                             W.rearrange("p k t -> p (k t)").unsqueeze(2).broadcast_to([P, 16, EXPERTS]),
                                             ALU.mult))
                nc.vector.tensor_tensor(GATES[:], CHOICE[:, 0], CHOICE[:, 1], ALU.add).then_inc(S("gates"), 1)
                dve.wait_ge(S("biases"), 1)
                c.do(nc.vector.tensor_tensor(X[:].rearrange("p t d -> p (t d)"), X[:].rearrange("p t d -> p (t d)"),
                                             PS[:, 0:2048], ALU.add))
        end()

        def pair(i, last_pair):
            with nc.Block(no_gpsimd_drain=True) as block:
                @block.sync
                def _(sp):
                    sp.dma_start(WEIGHTS[1], stacked(layer + "_experts", 2 * i + 1)).then_inc(S("weights"), 16)
                    if not last_pair:
                        sp.wait_ge(S("down"), HALF // P * 2)
                        sp.dma_start(WEIGHTS[0], stacked(layer + "_experts", 2 * i + 2))\
                            .then_inc(S("next weights"), 16)
                        sp.wait_ge(S("next weights"), 16)

                @block.tensor
                def _(pe):
                    for e in range(2):
                        if e:
                            pe.wait_ge(S("weights"), 16)
                        for half in range(2):
                            for j in range(HB):
                                n = (2 * e + half) * HB + j
                                if n >= 4:
                                    pe.wait_ge(S("gelu"), n - 3)
                                product(PS[:, n % 4 * 512:(n % 4 + 1) * 512],
                                        lambda q: W1[e][:, q, j * P:(j + 1) * P],
                                        lambda q: XNT_ALL[:, q, half * HALF:(half + 1) * HALF], DC)\
                                    .then_inc(S("up"), 1)
                        for half in range(2):
                            pe.wait_ge(S("gelu"), (2 * e + half + 1) * HB)
                            for u in range(4):
                                n = (2 * e + half) * 4 + u
                                if n >= 4:
                                    pe.wait_ge(S("added"), n - 3)
                                ps = (PSA, PSO)[n % 4 // 2]
                                product(ps[:, n % 2 * 512:n % 2 * 512 + D],
                                        lambda q: HT[half][:, q, u * P:(u + 1) * P], lambda q: W2[e][:, q, :], HB)\
                                    .then_inc(S("down"), 1)

                @block.scalar
                def _(act):
                    act.wait_ge(S("of expert"), 4)
                    for e in range(2):
                        for half in range(2):
                            if e:
                                act.wait_ge(S("down"), (2 * (e - 1) + half + 1) * 4)
                            for j in range(HB):
                                n = (2 * e + half) * HB + j
                                act.wait_ge(S("up"), n + 1)
                                nc.scalar.activation(HT[half][:, j, :], PS[:, n % 4 * 512:(n % 4 + 1) * 512],
                                                     ACT.Gelu, bias=BIAS[:, e, j:j + 1]).then_inc(S("gelu"), 1)

                @block.vector
                def _(dve):
                    for e in range(2):
                        nc.vector.tensor_copy(BIAS[:, e:e + 1, :], R["b1"][:, bass.ds(2 * i + e, 1), :])\
                            .then_inc(S("of expert"), 1)
                        nc.vector.tensor_copy(GATE[:, e, :].unsqueeze(2), GATES[:, :, bass.ds(2 * i + e, 1)])\
                            .then_inc(S("of expert"), 1)
                    dve.wait_ge(S("of expert"), 4)
                    for n in range(16):
                        e, t = n // 8, n % 8
                        dve.wait_ge(S("down"), n + 1)
                        if e:
                            dve.wait_ge(S("added"), n - 7)
                        ps = (PSA, PSO)[n % 4 // 2]
                        nc.vector.scalar_tensor_tensor(X[:, t, :], ps[:, n % 2 * 512:n % 2 * 512 + D],
                                                       GATE[:, e, t:t + 1], X[:, t, :], ALU.mult, ALU.add)\
                            .then_inc(S("added"), 1)
            end()

        with nc.Fori(0, EXPERTS // 2 - 1) as i:
            pair(i, False)
        pair(EXPERTS // 2 - 1, True)

    experts("l0f", int(1.25 * TOKENS * 2 / EXPERTS), False,
            [("params_b", 0, PARAMS_B), ("params_e", width(PARAMS_B), PARAMS_E)])

    B = views(PARAM, PARAMS_B)
    WKB = sb("l1a_wkb_rotated", [64, D])
    bit = Work(REGION)
    W1F, W2F = bit(DC * HID), bit(HB * D)
    SIZES = [bit(2048), bit(2048)]

    with nc.Block(no_gpsimd_drain=True) as block:
        @block.sync
        def _(sp):
            sp.dma_start(W1F, dram["bitnet"][:, 0:2048]).then_inc(S("bitnet"), 16)
            sp.dma_start(W2F, dram["bitnet"][:, 2048:4096]).then_inc(S("bitnet"), 16)

        @block.scalar
        def _(act):
            act.wait_ge(S("bitnet"), 32)
            for n, w in enumerate((W1F, W2F)):
                nc.scalar.activation(SIZES[n], w, ACT.Abs, accum_out=ABS[:, n:n + 1]).then_inc(S("abs"), 1)

        @block.tensor
        def _(pe):
            for j in range(DC):
                for m in range(DC):
                    nc.tensor.matmul(PS[:, m * D + j * P:m * D + (j + 1) * P], B["l1a_wq"][:, j, m * P:(m + 1) * P],
                                     K["rope"][:, j, :], start=True, stop=True)
                last = nc.tensor.matmul(PS[0:64, 512 + j * P:512 + (j + 1) * P], B["l1a_wkb"][:, j, :],
                                        K["rope"][:, j, :], start=True, stop=True)
            last.then_inc(S("rotated"), 1)
            pe.wait_ge(S("abs"), 2)
            nc.tensor.matmul(PS[:, 1024:1026], K["ones"], ABS[:], start=True, stop=True).then_inc(S("abs sums"), 1)

        @block.vector
        def _(dve):
            c = Chain(dve, S("vector"))
            c.go(nc.vector.tensor_copy(IDB[:], ident))
            dve.wait_ge(S("rotated"), 1)
            c.go(nc.vector.tensor_copy(B["l1a_wq"].rearrange("p c n -> p (c n)"), PS[:, 0:2 * D]))
            c.go(nc.vector.tensor_copy(WKB[:], PS[0:64, 512:512 + D]))
            dve.wait_ge(S("abs sums"), 1)
            c.do(nc.vector.tensor_scalar(WSCALE[:], PS[:, 1024:1026], 1.0 / (D * HID), EPS, ALU.mult, ALU.max))
            c.do(nc.vector.reciprocal(RECS2[:], WSCALE[:]))
            for n, (w, q) in enumerate(((W1F, W1Q[:]), (W2F, W2Q[:]))):
                q = q.rearrange("p a b -> p (a b)")
                c.do(nc.vector.tensor_scalar(w, w, RECS2[:, n:n + 1], ROUND, ALU.mult, ALU.add))
                c.do(nc.vector.tensor_scalar(w, w, -ROUND, -1.0, ALU.add, ALU.max))
                c.do(nc.vector.tensor_scalar(q, w, 1.0, None, ALU.min))
    end()

    work = Work(REGION)
    for L in LANES:
        L.XT, L.XN, L.XNT = work(D), work(D), work(DC, P)
        L.SM, L.PR, L.PT = work(1024), work(1024), work(1024)
        L.OO, L.OT = work(512), work(512)
        L.QBD = work(32, SEQ)
        L.CTXT64, L.KT = work(DC, 2 * SEQ), work(DC, P)
        L.V64, L.KA = work(2, D, parts=64), work(2, P, parts=64)
        L.CAUSAL = work(2, SEQ)
        L.RAW_I = work(2 * SEQ).bitcast(I32)
        L.Q1, L.Q2 = L.OT[:, 0:128].bitcast(BF16), L.OO.bitcast(BF16)
        L.Q1T, L.Q2T = L.OT[:, 128:256].bitcast(BF16), L.OT.bitcast(BF16)
        L.psA16 = L.psA.bitcast(BF16)

    def quantize(L, c, x, q, back, scale):
        one = L.one
        c.do(nc.vector.tensor_reduce(one[0][:], x, AX, ALU.max, apply_absolute_value=True))
        c.do(nc.vector.tensor_scalar(one[1][:], one[0][:], EPS, None, ALU.max))
        c.do(nc.vector.reciprocal(one[2][:], one[1][:]))
        c.go(nc.vector.tensor_scalar(one[3][:], one[2][:], 127.0, None, ALU.mult))
        c.go(nc.vector.tensor_scalar(back, one[1][:], 1.0 / 127.0, scale, ALU.mult, ALU.mult))
        c.settle()
        c.do(nc.vector.tensor_scalar(x, x, one[3][:], ROUND, ALU.mult, ALU.add))
        c.do(nc.vector.tensor_scalar(x, x, -ROUND, -128.0, ALU.add, ALU.max))
        c.do(nc.vector.tensor_scalar(q, x, 127.0, None, ALU.min))

    def b_load(L, sp, t):
        sp.dma_start(L.RAW_I, stacked("mask_i", t)).then_inc(L.S("mask"), 16)
        sp.dma_start(L.CTXT64.rearrange("p c t -> p (c t)"), stacked("ctxT64", t)).then_inc(L.S("ctxT"), 16)
        sp.dma_start(L.V64.rearrange("p b d -> p (b d)"), dram["ctx64"][bass.ds(t * SEQ, SEQ), :])\
            .then_inc(L.S("ctx64"), 16)

    def b_vector(L, dve, c, t):
        fetch_tile(L, c, t)
        normed(L, c, "l1x")
        yield
        dve.wait_ge(L.S("mask"), 16)
        c.do(nc.vector.tensor_scalar(L.CAUSAL.rearrange("p b k -> p (b k)"), L.RAW_I, 1.0, FAR, ALU.is_equal, ALU.mult))
        c.do(nc.vector.tensor_tensor(L.CAUSAL, L.CAUSAL, K["causal"].unsqueeze(1).broadcast_to([P, 2, SEQ]), ALU.add))
        yield
        dve.wait_ge(L.S("l1x turned"), 1)
        head_queries(L, c, L.psA[:, 0:D].rearrange("p (c t) -> p c t", t=P), "l1x")
        yield from attention_vector(L, dve, c, "l1x", SEQ, lambda b: L.CAUSAL[:, b, :])
        yield from residual(L, dve, c, "l1x", B["l1x_b"])
        normed(L, c, "l1a")
        yield
        dve.wait_ge(L.S("l1a q"), 1)
        head_queries(L, c, L.psS[:, 0:D].rearrange("p (c t) -> p c t", t=P), "l1a")
        yield from attention_vector(L, dve, c, "l1a", SEQ, None)
        yield from residual(L, dve, c, "l1a", None)
        layer_norm(L, c, [(L.XT, L.XN)])
        layer_norm(L, c, [(L.XN, L.XN)])
        affine(c, L.XN, B["l1f_ln1_w"], B["l1f_ln1_b"])
        quantize(L, c, L.XN, L.Q1, L.one[4][:], WSCALE[:, 0:1])
        tell(L, "l1f q1")
        yield
        dve.wait_ge(L.S("l1f up"), 1)
        nc.vector.scalar_tensor_tensor(L.SM, L.psS, L.one[4][:], B["l1f_b1"], ALU.mult, ALU.add)\
            .then_inc(L.S("l1f hidden"), 1)
        yield
        dve.wait_ge(L.S("l1f gelu"), 1)
        layer_norm(L, c, [(L.PR, L.PR)])
        affine(c, L.PR, B["l1f_ln2_w"], B["l1f_ln2_b"])
        quantize(L, c, L.PR, L.Q2, L.one[5][:], WSCALE[:, 1:2])
        tell(L, "l1f q2")
        yield
        dve.wait_ge(L.S("l1f y"), 1)
        c.do(nc.vector.scalar_tensor_tensor(L.XT, L.psO[:, 0:D], L.one[5][:], L.XT, ALU.mult, ALU.add))
        c.do(nc.vector.tensor_tensor(L.XT, L.XT, B["l1f_b2"], ALU.add))
        c.do(nc.vector.tensor_copy(X[:, bass.ds(t, 1), :], L.XT.unsqueeze(1)))

    def b_scalar(L, act):
        yield from attention_scalar(L, act, "l1x", SEQ, True)
        yield from project_scalar(L, act, "l1x", 2)
        yield from transpose_x_scalar(L, act, "l1a")
        yield
        act.wait_ge(L.S("l1a latent"), 1)
        nc.scalar.copy(L.KA.rearrange("p c t -> p (c t)"), L.psO[0:64, 0:256]).then_inc(L.S("l1a latents"), 1)
        yield
        act.wait_ge(L.S("l1a kv"), 1)
        nc.scalar.copy(L.KT.rearrange("p c t -> p (c t)"), L.psS[:, 512:768]).then_inc(L.S("l1a kvs"), 1)
        nc.scalar.copy(L.V64.rearrange("p b d -> p (b d)"), L.psA[0:64, :]).then_inc(L.S("l1a kvs"), 1)
        yield from attention_scalar(L, act, "l1a", SEQ, None)
        yield from project_scalar(L, act, "l1a", 2)
        yield
        act.wait_ge(L.S("l1f q1 turned"), 1)
        nc.scalar.copy(L.Q1T, L.psA16[:, 0:256]).then_inc(L.S("l1f q1T"), 1)
        yield
        act.wait_ge(L.S("l1f hidden"), 1)
        nc.scalar.activation(L.PR, L.SM, ACT.Gelu).then_inc(L.S("l1f gelu"), 1)
        yield
        act.wait_ge(L.S("l1f q2 turned"), 1)
        nc.scalar.copy(L.Q2T, L.psA16).then_inc(L.S("l1f q2T"), 1)

    def b_tensor(L, pe):
        yield from transpose_x_tensor(L, pe, "l1x")
        value = lambda b, c, p, s: L.V64[:, b, column16(p, s):column16(p, s) + DH]
        yield from attention_tensor(L, pe, "l1x", SEQ, DH, masked_query(L),
                                    lambda b, p: L.CTXT64[:, p // 4, SEQ * b:SEQ * (b + 1)], value, column16,
                                    [("ctxT", 16), ("ctx64", 16), ("l1x queries", 1)])
        yield from project_tensor(L, pe, "l1x", B["l1x_w"])
        yield from transpose_x_tensor(L, pe, "l1a")
        yield
        pe.wait_ge(L.S("l1a xnT"), 1)
        for j in range(DC):
            last = product(L.psS[:, j * P:(j + 1) * P], lambda i: B["l1a_wq"][:, i, j * P:(j + 1) * P],
                           lambda i: L.XNT[:, i, :], DC)
        last.then_inc(L.S("l1a q"), 1)
        for j, w in enumerate(("l1a_wka", "l1a_wva")):
            last = product(L.psO[0:64, j * P:(j + 1) * P], lambda i: B[w][:, i, :], lambda i: L.XNT[:, i, :], DC)
        last.then_inc(L.S("l1a latent"), 1)
        yield
        pe.wait_ge(L.S("l1a latents"), 1)
        for j in range(DC):
            nc.tensor.matmul(L.psS[:, 512 + j * P:512 + (j + 1) * P], WKB[:, j * P:(j + 1) * P], L.KA[:, 0, :],
                             start=True, stop=True)
        for b in range(2):
            last = nc.tensor.matmul(L.psA[0:64, D * b:D * (b + 1)], L.KA[:, 1, SEQ * b:SEQ * (b + 1)], B["l1a_wvb"],
                                    start=True, stop=True)
        last.then_inc(L.S("l1a kv"), 1)
        yield from attention_tensor(L, pe, "l1a", SEQ, DH, masked_query(L),
                                    lambda b, p: L.KT[:, p // 4, SEQ * b:SEQ * (b + 1)], value, column16,
                                    [("l1a kvs", 2), ("l1a queries", 1)])
        yield from project_tensor(L, pe, "l1a", B["l1a_wo"])
        yield
        pe.wait_ge(L.S("l1f q1"), 1)
        for i in range(DC):
            last = nc.tensor.transpose(L.psA16[:, i * P:(i + 1) * P], L.Q1[:, i * P:(i + 1) * P], IDB[:])
        last.then_inc(L.S("l1f q1 turned"), 1)
        yield
        pe.wait_ge(L.S("l1f q1T"), 1)
        for j in range(2):
            last = product(L.psS[:, j * 512:(j + 1) * 512], lambda i: L.Q1T[:, i * P:(i + 1) * P],
                           lambda i: W1Q[:, i, j * 512:(j + 1) * 512], DC)
        last.then_inc(L.S("l1f up"), 1)
        yield
        pe.wait_ge(L.S("l1f q2"), 1)
        for i in range(HB):
            last = nc.tensor.transpose(L.psA16[:, i * P:(i + 1) * P], L.Q2[:, i * P:(i + 1) * P], IDB[:])
        last.then_inc(L.S("l1f q2 turned"), 1)
        yield
        pe.wait_ge(L.S("l1f q2T"), 1)
        product(L.psO[:, 0:D], lambda i: L.Q2T[:, i * P:(i + 1) * P], lambda i: W2Q[:, i, :], HB)\
            .then_inc(L.S("l1f y"), 1)

    with nc.Fori(0, TILES // 2) as i:
        lanes_block(i, b_load, b_vector, b_scalar, b_tensor)

    E = views(PARAM[:, width(PARAMS_B):], PARAMS_E)
    E.update(views(PARAM, PARAMS_E_LATE))
    work = Work(REGION)
    for L in LANES:
        L.XT, L.XN, L.XNT = work(D), work(D), work(DC, P)
        L.SM, L.PR, L.PT = work(1024), work(1024), work(1024)
        L.OO, L.OT = work(D), work(D)
        L.QBD = work(32, SEQ)
        L.CTXT, L.KT, L.V = work(DC, 512), work(DC, 512), work(4, D)
        L.QF = work(DC, P)
        L.KEYMASK = work(2, KEYS)
        L.RAW_B = work(2 * KEYS // 4).bitcast(dram["mask_b"].dtype)

    with nc.Block(no_gpsimd_drain=True) as block:
        @block.sync
        def _(sp):
            sp.dma_start(PARAM[:, 0:width(PARAMS_E_LATE)], dram["params_e_late"]).then_inc(S("late params"), 16)
            sp.wait_ge(S("late params"), 16)
    end()

    def e_load(L, sp, t):
        sp.dma_start(L.CTXT.rearrange("p c t -> p (c t)"), stacked("ctxT", t)).then_inc(L.S("ctxT"), 16)
        sp.dma_start(L.RAW_B, stacked("mask_b", t)).then_inc(L.S("mask"), 16)

    def e_vector(L, dve, c, t):
        fetch_tile(L, c, t)
        normed(L, c, "l2x")
        yield
        dve.wait_ge(L.S("mask"), 16)
        c.do(nc.vector.tensor_scalar(L.KEYMASK.rearrange("p b k -> p (b k)"), L.RAW_B, -1e9, None, ALU.mult))
        yield
        dve.wait_ge(L.S("l2x v"), 1)
        for j, ps in enumerate((L.psA, L.psO)):
            nc.vector.tensor_tensor(L.V[:, 2 * j:2 * j + 2, :], ps.rearrange("p (j d) -> p j d", d=D),
                                    E["l2x_bv"].unsqueeze(1).broadcast_to([P, 2, D]), ALU.add)\
                .then_inc(L.S("l2x vs"), 1)
        yield
        dve.wait_ge(L.S("l2x qT"), 2)
        head_queries(L, c, L.QF, "l2x")
        yield from attention_vector(L, dve, c, "l2x", KEYS, lambda b: L.KEYMASK[:, b, :])
        yield from residual(L, dve, c, "l2x", E["l2x_bo"])
        normed(L, c, "l2a")
        yield
        dve.wait_ge(L.S("l2a squares"), 3)
        c.do(nc.vector.tensor_tensor(L.one[0][:], L.one[1][:], L.one[2][:], ALU.add))
        c.do(nc.vector.tensor_tensor(L.one[0][:], L.one[0][:], L.one[3][:], ALU.add))
        rstd_of(L, c, 1, L.one[0][:], 0.0)
        nc.vector.tensor_scalar(L.one[4][:], L.rstd[:, 0:1], 2048.0 ** 0.5, None, ALU.mult)\
            .then_inc(L.S("l2a norm"), 1)
        yield from residual(L, dve, c, "l2a", None)
        yield from to_experts_vector(L, dve, c, t)

    def e_scalar(L, act):
        yield
        act.wait_ge(L.S("l2x k"), 1)
        for i in range(DC):
            nc.scalar.activation(L.KT[:, i, :], L.psS[:, i * 512:(i + 1) * 512], ACT.Identity,
                                 bias=E["l2x_bk"][:, i:i + 1]).then_inc(L.S("l2x ks"), 1)
        yield from transpose_x_scalar(L, act, "l2x")
        yield
        act.wait_ge(L.S("l2x q"), 1)
        for i in range(DC):
            nc.scalar.activation(L.QF[:, i, :], L.psS[:, i * P:(i + 1) * P], ACT.Identity,
                                 bias=E["l2x_bq"][:, i:i + 1]).then_inc(L.S("l2x qT"), 1)
        yield from attention_scalar(L, act, "l2x", KEYS, True)
        yield from project_scalar(L, act, "l2x", 4)
        yield from transpose_x_scalar(L, act, "l2a")
        yield
        act.wait_ge(L.S("l2a scores"), 1)
        nc.scalar.activation(L.PT, L.psS, ACT.Square, accum_out=L.one[1][:]).then_inc(L.S("l2a squares"), 1)
        nc.scalar.activation(L.SM[:, 0:512], L.psA, ACT.Square, accum_out=L.one[2][:]).then_inc(L.S("l2a squares"), 1)
        nc.scalar.activation(L.SM[:, 512:1024], L.psO, ACT.Square, accum_out=L.one[3][:])\
            .then_inc(L.S("l2a squares"), 1)
        yield
        act.wait_ge(L.S("l2a norm"), 1)
        nc.scalar.activation(L.PR, L.psS, ACT.Gelu, scale=L.one[4][:]).then_inc(L.S("l2a gelu"), 1)
        nc.scalar.activation(L.SM[:, 0:512], L.psA, ACT.Gelu, scale=L.one[4][:]).then_inc(L.S("l2a gelu"), 1)
        nc.scalar.activation(L.SM[:, 512:1024], L.psO, ACT.Gelu, scale=L.one[4][:]).then_inc(L.S("l2a gelu"), 1)
        for h in range(2):
            yield
            act.wait_ge(L.S("l2a gelu turned"), h + 1)
            if h:
                act.wait_ge(L.S("l2a half"), 1)
            nc.scalar.copy(L.PT, L.psS).then_inc(L.S("l2a gT"), 1)

    def e_tensor(L, pe):
        pe.wait_ge(L.S("ctxT"), 16)
        for j in range(DC):
            last = product(L.psS[:, j * 512:(j + 1) * 512], lambda i: E["l2x_wk"][:, i, j * P:(j + 1) * P],
                           lambda i: L.CTXT[:, i, :], DC)
        last.then_inc(L.S("l2x k"), 1)
        for j in range(4):
            ps = (L.psA, L.psO)[j // 2]
            last = product(ps[:, j % 2 * D:(j % 2 + 1) * D], lambda i: L.CTXT[:, i, j * P:(j + 1) * P],
                           lambda i: E["l2x_wv"][:, i, :], DC)
        last.then_inc(L.S("l2x v"), 1)
        yield
        pe.wait_ge(L.S("l2x vs"), 2)
        yield from transpose_x_tensor(L, pe, "l2x")
        yield
        pe.wait_ge(L.S("l2x xnT"), 1)
        pe.wait_ge(L.S("l2x ks"), 2)
        for j in range(DC):
            last = product(L.psS[:, j * P:(j + 1) * P], lambda i: E["l2x_wq"][:, i, j * P:(j + 1) * P],
                           lambda i: L.XNT[:, i, :], DC)
        last.then_inc(L.S("l2x q"), 1)
        yield from attention_tensor(
            L, pe, "l2x", KEYS, DH, masked_query(L), lambda b, p: L.KT[:, p // 4, KEYS * b:KEYS * (b + 1)],
            lambda b, c, p, s: L.V[:, 2 * b + c, column16(p, s):column16(p, s) + DH], column16,
            [("l2x queries", 1)])
        yield from project_tensor(L, pe, "l2x", E["l2x_wo"])
        yield from transpose_x_tensor(L, pe, "l2a")
        yield
        pe.wait_ge(L.S("l2a xnT"), 1)
        for j, ps in enumerate((L.psS[:, 0:512], L.psS[:, 512:1024], L.psA, L.psO)):
            last = product(ps, lambda i: L.XNT[:, i, :], lambda i: E["l2a_k"][:, i, j * 512:(j + 1) * 512], DC)
        last.then_inc(L.S("l2a scores"), 1)
        yield
        pe.wait_ge(L.S("l2a gelu"), 3)
        for h, g in enumerate((L.PR, L.SM)):
            for i in range(8):
                last = nc.tensor.transpose(L.psS[:, i * P:(i + 1) * P], g[:, i * P:(i + 1) * P], ident)
            last.then_inc(L.S("l2a gelu turned"), 1)
            yield
            pe.wait_ge(L.S("l2a gT"), h + 1)
            last = product(L.psA[:, 0:D], lambda i: L.PT[:, i * P:(i + 1) * P], lambda i: E["l2a_v"][:, 8 * h + i, :], 8,
                           first=(h == 0), last_=(h == 1))
            last.then_inc(L.S("l2a y" if h else "l2a half"), 1)
        yield from transpose_x_tensor(L, pe, "router")

    with nc.Fori(0, TILES // 2) as i:
        lanes_block(i, e_load, e_vector, e_scalar, e_tensor)

    experts("l2f", None, False, [("params_c", 0, PARAMS_C)])

    C = views(PARAM, PARAMS_C)
    work = Work(REGION)
    for L in LANES:
        L.XT, L.XN, L.XNT = work(D), work(D), work(DC, P)
        L.PR, L.PT = work(KEYS), work(KEYS)
        L.OO, L.OT = work(64), work(P, parts=64)
        L.CTXT, L.KT, L.V = work(DC, 512), work(512, parts=64), work(4, 64)
        L.QT = work(P, parts=64)
        L.H, L.QKT, L.MIXED = work(P, parts=64), work(2, P, parts=64), work(2, SEQ, parts=64)
        L.POOLED, L.POOLED_T = work(8, parts=64), work(8, CHUNK, parts=64)
        L.VB, L.PICKED, L.ACTIVE, L.GATED = work(2, SEQ, parts=64), work(P, parts=64), work(P, parts=64), work(P, parts=64)
        L.DELTA, L.PICKS_T, L.HALF_BH = work(P, parts=64), work(P, parts=64), work(1, parts=64)
        L.SCORES, L.REST, L.WEIGHT, L.TOP8 = work(SEQ), work(SEQ), work(SEQ), work(8)

    def c_load(L, sp, t):
        sp.dma_start(L.CTXT.rearrange("p c t -> p (c t)"), stacked("ctxT", t)).then_inc(L.S("ctxT"), 16)

    def c_vector(L, dve, c, t):
        one = L.one
        fetch_tile(L, c, t)
        normed(L, c, "l3x")
        c.do(nc.vector.tensor_scalar(L.HALF_BH, C["l3a_bh"], 0.5, None, ALU.mult))
        yield
        dve.wait_ge(L.S("l3x v"), 1)
        nc.vector.tensor_tensor(L.V, L.psS[:, 0:256].rearrange("p (j d) -> p j d", d=64),
                                C["l3x_bq"].unsqueeze(1).broadcast_to([P, 4, 64]), ALU.add)\
            .then_inc(L.S("l3x vs"), 1)
        yield
        dve.wait_ge(L.S("l3x scores"), 1)
        c.do(nc.vector.tensor_reduce(one[0][:], L.psS[:, 512:512 + KEYS], AX, ALU.max))
        nc.vector.tensor_scalar(one[1][:], one[0][:], -(D ** -0.5), None, ALU.mult).then_inc(L.S("l3x max"), 1)
        yield
        dve.wait_ge(L.S("l3x exp"), 1)
        c.do(nc.vector.reciprocal(one[3][:], one[2][:]))
        nc.vector.tensor_scalar(L.PR, L.PR, one[3][:], None, ALU.mult).then_inc(L.S("l3x probs"), 1)
        yield from residual(L, dve, c, "l3x", C["l3x_bo"])
        normed(L, c, "l3a")
        for step in range(2):
            yield
            if step == 0:
                dve.wait_ge(L.S("l3a h"), 1)
            hb = L.H.rearrange("p (b s) -> p b s", s=SEQ)
            c.do(nc.vector.tensor_reduce(L.POOLED, L.H.rearrange("p (g s) -> p g s", s=CHUNK), AX, ALU.add))
            nc.vector.tensor_scalar(L.POOLED, L.POOLED, 1.0 / CHUNK, None, ALU.mult).then_inc(L.S("l3a pooled"), 1)
            c.do(nc.vector.tensor_scalar(L.MIXED.rearrange("p b s -> p (b s)"), L.H,
                                         C["l3a_conv"][:, KSIZE - 1:KSIZE], C["l3a_convb"], ALU.mult, ALU.add))
            for back in range(1, KSIZE):
                c.do(nc.vector.scalar_tensor_tensor(
                    L.MIXED[:, :, back:SEQ], hb[:, :, 0:SEQ - back],
                    C["l3a_conv"][:, KSIZE - 1 - back:KSIZE - back], L.MIXED[:, :, back:SEQ], ALU.mult, ALU.add))
            yield
            dve.wait_ge(L.S("l3a scores"), step + 1)
            c.do(nc.vector.scalar_tensor_tensor(L.SCORES, L.psS[:, 0:SEQ], STATE ** -0.5, K["strict"],
                                                ALU.mult, ALU.add))
            c.do(nc.vector.max(L.TOP8, L.SCORES))
            nc.vector.tensor_scalar(one[0][:], L.TOP8[:, 0:1], FAR / 10, -1.0, ALU.max, ALU.mult)\
                .then_inc(L.S("l3a max"), 1)
            c.do(nc.vector.match_replace(L.REST, L.TOP8, L.SCORES, TAKEN))
            c.do(nc.vector.tensor_scalar(L.REST, L.REST, TAKEN / 10, None, ALU.is_lt))
            dve.wait_ge(L.S("l3a pool product"), step + 1)
            c.go(nc.vector.tensor_scalar(L.POOLED_T, L.psS[0:64, 512:520].unsqueeze(2).broadcast_to([64, 8, CHUNK]),
                                         C["l3a_bp"], None, ALU.add))
            for b in range(2):
                c.go(nc.vector.tensor_tensor(L.VB[:, b, :], L.psA[0:64, 64 * b:64 * b + 64], C["l3a_bv"], ALU.add))
            c.settle()
            tell(L, "l3a inputs")
            yield
            dve.wait_ge(L.S("l3a exp"), step + 1)
            c.do(nc.vector.tensor_tensor(L.WEIGHT, L.WEIGHT, L.REST, ALU.mult))
            c.do(nc.vector.tensor_reduce(one[1][:], L.WEIGHT, AX, ALU.add))
            c.do(nc.vector.tensor_scalar(one[2][:], one[1][:], 1e-30, None, ALU.max))
            c.do(nc.vector.reciprocal(one[3][:], one[2][:]))
            nc.vector.tensor_scalar(L.WEIGHT, L.WEIGHT, one[3][:], None, ALU.mult).then_inc(L.S("l3a weights"), 1)
            yield
            dve.wait_ge(L.S("l3a gate"), step + 1)
            c.do(nc.vector.tensor_scalar(L.GATED, L.GATED, 0.5, 0.5, ALU.mult, ALU.add))
            dve.wait_ge(L.S("l3a delta"), step + 1)
            c.do(nc.vector.scalar_tensor_tensor(L.DELTA, L.psA[0:64, 256:256 + P], C["l3a_b2"], L.GATED,
                                                ALU.add, ALU.mult))
            nc.vector.tensor_tensor(L.H, L.H, L.DELTA, ALU.add).then_inc(L.S("l3a updated"), 1)
            dve.wait_ge(L.S("l3a updated"), step + 1)
        c.do(nc.vector.tensor_tensor(L.XT, L.XT, L.XN, ALU.add))
        yield from residual(L, dve, c, "l3a", C["l3a_bo"])
        yield from to_experts_vector(L, dve, c, t)

    def c_scalar(L, act):
        yield
        act.wait_ge(L.S("l3x k"), 1)
        nc.scalar.activation(L.KT, L.psA[0:64, :], ACT.Identity, bias=C["l3x_bqc"]).then_inc(L.S("l3x ks"), 1)
        yield from transpose_x_scalar(L, act, "l3x")
        yield
        act.wait_ge(L.S("l3x q"), 1)
        nc.scalar.activation(L.QT, L.psO[0:64, 0:P], ACT.Identity, bias=C["l3x_bqc"]).then_inc(L.S("l3x qT"), 1)
        yield
        act.wait_ge(L.S("l3x max"), 1)
        nc.scalar.activation(L.PR, L.psS[:, 512:512 + KEYS], ACT.Exp, bias=L.one[1][:], scale=D ** -0.5,
                             accum_out=L.one[2][:]).then_inc(L.S("l3x exp"), 1)
        yield
        act.wait_ge(L.S("l3x probs turned"), 1)
        nc.scalar.copy(L.PT, L.psA[:, 0:2 * P]).then_inc(L.S("l3x probsT"), 1)
        yield
        act.wait_ge(L.S("l3x mixed"), 1)
        nc.scalar.copy(L.OO, L.psO[:, 0:64]).then_inc(L.S("l3x o"), 1)
        yield
        act.wait_ge(L.S("l3x o turned"), 1)
        nc.scalar.copy(L.OT, L.psS[0:64, 0:P]).then_inc(L.S("l3x oT"), 1)
        yield from transpose_x_scalar(L, act, "l3a")
        yield
        act.wait_ge(L.S("l3a input product"), 1)
        nc.scalar.activation(L.H, L.psO[0:64, 0:P], ACT.Identity, bias=C["l3a_bi"]).then_inc(L.S("l3a h"), 1)
        for step in range(2):
            yield
            act.wait_ge(L.S("l3a qk"), step + 1)
            for j, bias in enumerate(("l3a_bq", "l3a_bk")):
                nc.scalar.activation(L.QKT[:, j, :], L.psO[0:64, j * P:(j + 1) * P], ACT.Identity, bias=C[bias])\
                    .then_inc(L.S("l3a qks"), 1)
            nc.scalar.activation(L.GATED, L.psO[0:64, 2 * P:3 * P], ACT.Tanh, scale=0.5, bias=L.HALF_BH)\
                .then_inc(L.S("l3a gate"), 1)
            yield
            act.wait_ge(L.S("l3a max"), step + 1)
            nc.scalar.activation(L.WEIGHT, L.SCORES, ACT.Exp, bias=L.one[0][:]).then_inc(L.S("l3a exp"), 1)
            yield
            act.wait_ge(L.S("l3a weights turned"), step + 1)
            nc.scalar.copy(L.PICKS_T, L.psS[0:64, 512:512 + P]).then_inc(L.S("l3a weightsT"), 1)
            yield
            act.wait_ge(L.S("l3a summed"), step + 1)
            nc.scalar.copy(L.PICKED, L.psO[0:64, 0:P]).then_inc(L.S("l3a picked"), 1)
            yield
            act.wait_ge(L.S("l3a up"), step + 1)
            nc.scalar.activation(L.ACTIVE, L.psS[0:64, 0:P], ACT.Tanh, bias=C["l3a_b1"]).then_inc(L.S("l3a tanh"), 1)

    def c_tensor(L, pe):
        pe.wait_ge(L.S("ctxT"), 16)
        product(L.psA[0:64, :], lambda i: C["l3x_wq"][:, i, :], lambda i: L.CTXT[:, i, :], DC)\
            .then_inc(L.S("l3x k"), 1)
        for j in range(4):
            last = product(L.psS[:, 64 * j:64 * j + 64], lambda i: L.CTXT[:, i, j * P:(j + 1) * P],
                           lambda i: C["l3x_wq"][:, i, :], DC)
        last.then_inc(L.S("l3x v"), 1)
        yield
        pe.wait_ge(L.S("l3x ks"), 1)
        yield from transpose_x_tensor(L, pe, "l3x")
        yield
        pe.wait_ge(L.S("l3x xnT"), 1)
        product(L.psO[0:64, 0:P], lambda i: C["l3x_wq"][:, i, :], lambda i: L.XNT[:, i, :], DC)\
            .then_inc(L.S("l3x q"), 1)
        yield
        pe.wait_ge(L.S("l3x qT"), 1)
        for b in range(2):
            last = nc.tensor.matmul(L.psS[64 * b:64 * b + 64, 512:512 + KEYS], L.QT[:, 64 * b:64 * b + 64],
                                    L.KT[:, KEYS * b:KEYS * (b + 1)], start=True, stop=True)
        last.then_inc(L.S("l3x scores"), 1)
        yield
        pe.wait_ge(L.S("l3x probs"), 1)
        for i in range(2):
            last = nc.tensor.transpose(L.psA[:, i * P:(i + 1) * P], L.PR[:, i * P:(i + 1) * P], ident)
        last.then_inc(L.S("l3x probs turned"), 1)
        yield
        pe.wait_ge(L.S("l3x probsT"), 1)
        pe.wait_ge(L.S("l3x vs"), 1)
        for b in range(2):
            last = product(L.psO[64 * b:64 * b + 64, 0:64], lambda i: L.PT[:, i * P + 64 * b:i * P + 64 * b + 64],
                           lambda i: L.V[:, 2 * b + i, :], 2)
        last.then_inc(L.S("l3x mixed"), 1)
        yield
        pe.wait_ge(L.S("l3x o"), 1)
        nc.tensor.transpose(L.psS[0:64, 0:P], L.OO, ident).then_inc(L.S("l3x o turned"), 1)
        yield
        pe.wait_ge(L.S("l3x oT"), 1)
        nc.tensor.matmul(L.psA[:, 0:D], L.OT, C["l3x_wo"], start=True, stop=True).then_inc(L.S("l3x y"), 1)
        yield from transpose_x_tensor(L, pe, "l3a")
        yield
        pe.wait_ge(L.S("l3a xnT"), 1)
        product(L.psO[0:64, 0:P], lambda i: C["l3a_wi"][:, i, :], lambda i: L.XNT[:, i, :], DC)\
            .then_inc(L.S("l3a input product"), 1)
        for step in range(2):
            yield
            if step == 0:
                pe.wait_ge(L.S("l3a h"), 1)
            else:
                pe.wait_ge(L.S("l3a updated"), 1)
            nc.tensor.matmul(L.psO[0:64, 0:P], C["l3a_wq"], L.H, start=True, stop=True)
            nc.tensor.matmul(L.psO[0:64, P:2 * P], C["l3a_wk"], L.H, start=True, stop=True)
            nc.tensor.matmul(L.psO[0:64, 2 * P:3 * P], C["l3a_wh"], L.H, start=True, stop=True)\
                .then_inc(L.S("l3a qk"), 1)
            for b in range(2):
                nc.tensor.matmul(L.psA[0:64, 64 * b:64 * b + 64], L.H[:, 64 * b:64 * b + 64], C["l3a_wv"],
                                 start=True, stop=True)
            pe.wait_ge(L.S("l3a pooled"), step + 1)
            nc.tensor.matmul(L.psS[0:64, 512:520], C["l3a_wp"], L.POOLED, start=True, stop=True)\
                .then_inc(L.S("l3a pool product"), 1)
            yield
            pe.wait_ge(L.S("l3a qks"), 2 * step + 2)
            for b in range(2):
                last = nc.tensor.matmul(L.psS[64 * b:64 * b + 64, 0:SEQ], L.QKT[:, 0, 64 * b:64 * b + 64],
                                        L.QKT[:, 1, 64 * b:64 * b + 64], start=True, stop=True)
            last.then_inc(L.S("l3a scores"), 1)
            yield
            pe.wait_ge(L.S("l3a weights"), step + 1)
            nc.tensor.transpose(L.psS[0:64, 512:512 + P], L.WEIGHT, ident).then_inc(L.S("l3a weights turned"), 1)
            yield
            pe.wait_ge(L.S("l3a weightsT"), step + 1)
            pe.wait_ge(L.S("l3a inputs"), step + 1)
            pe.wait_ge(L.S("l3a gate"), step + 1)
            for b in range(2):
                last = nc.tensor.matmul(L.psO[0:64, 64 * b:64 * b + 64], L.VB[:, b, :], L.PICKS_T[:, 64 * b:64 * b + 64],
                                        start=True, stop=True)
            last.then_inc(L.S("l3a summed"), 1)
            yield
            pe.wait_ge(L.S("l3a picked"), step + 1)
            parts = [L.H, L.MIXED.rearrange("p b s -> p (b s)"), L.POOLED_T.rearrange("p g s -> p (g s)"), L.PICKED]
            product(L.psS[0:64, 0:P], lambda i: C["l3a_w1"][:, i, :], lambda i: parts[i], 4)\
                .then_inc(L.S("l3a up"), 1)
            yield
            pe.wait_ge(L.S("l3a tanh"), step + 1)
            nc.tensor.matmul(L.psA[0:64, 256:256 + P], C["l3a_w2"], L.ACTIVE, start=True, stop=True)\
                .then_inc(L.S("l3a delta"), 1)
        yield
        pe.wait_ge(L.S("l3a updated"), 2)
        nc.tensor.matmul(L.psA[:, 0:D], L.H, C["l3a_wo"], start=True, stop=True).then_inc(L.S("l3a y"), 1)
        yield from transpose_x_tensor(L, pe, "router")

    with nc.Fori(0, TILES // 2) as i:
        lanes_block(i, c_load, c_vector, c_scalar, c_tensor)

    experts("l3f", int(round(2 * TOKENS * 1.05 / EXPERTS)), True, [])

    with nc.Block(no_gpsimd_drain=True) as block:
        @block.sync
        def _(sp):
            sp.dma_start(out, X[:]).then_inc(S("stored"), 16)
            sp.wait_ge(S("stored"), 16)


def kernel(**inputs):
    import numpy as np
    import concourse.bacc as bacc
    from concourse.bass_utils import run_bass_kernel_spmd as run

    f = {k: np.asarray(v) for k, v in inputs.items()}

    def rows(w):
        return w.reshape(-1, P, w.shape[1]).transpose(1, 0, 2)

    def bcast(b):
        return np.broadcast_to(b.reshape(1, -1), (P, b.size))

    def cols(b):
        return b.reshape(-1, P).T

    def col(b):
        return b.reshape(-1, 1)

    r = np.arange(P)
    seq = r % SEQ
    inv = 1.0 / 10000.0 ** (np.arange(0, DH, 2, dtype=np.float32) / np.float32(DH))
    angle = np.arange(HEADS, dtype=np.float32)[:, None] * inv[None, :].astype(np.float32)
    rope = np.zeros((D, D), np.float32)
    for h in range(HEADS):
        for j in range(DH // 2):
            a, b = h * DH + 2 * j, h * DH + 2 * j + 1
            cos, sin = np.cos(angle[h, j]), np.sin(angle[h, j])
            rope[a, a], rope[b, a], rope[a, b], rope[b, b] = cos, -sin, sin, cos
    consts = {
        "ident": np.eye(P), "tri": r[:, None] <= r[None, :], "ones": np.ones((P, P)),
        "batch_ones": r[:, None] // SEQ == r[None, :] // SEQ,
        "headmask": (r[:, None] // DH == np.arange(8)[None, :]) * 0.25,
        "causal": np.where(np.arange(SEQ)[None, :] > seq[:, None], FAR, 0.0),
        "strict": np.where(np.arange(SEQ)[None, :] >= seq[:, None], FAR, 0.0),
        "experts": bcast(np.arange(EXPERTS)),
        "rope": np.stack([rope[i * P:(i + 1) * P, i * P:(i + 1) * P] for i in range(DC)], 1),
    }
    g = lambda layer: {k[len(layer) + 1:]: v for k, v in f.items() if k.startswith(layer + "_")}
    x0, a0, x1, a1, f1 = g("L0_xattn"), g("L0_attn"), g("L1_xattn"), g("L1_attn"), g("L1_ffn")
    x2, a2, x3, a3 = g("L2_xattn"), g("L2_attn"), g("L3_xattn"), g("L3_attn")
    wk, wv = x0["Wkv"][:, :64], x0["Wkv"][:, 64:]
    wout = x0["Wout"].reshape(4, 2, 2, 64, D).transpose(2, 0, 1, 3, 4).reshape(8, P, D).transpose(1, 0, 2)
    params_a = {
        "l0x_wk": rows(np.concatenate([wk, wk], 1)), "l0x_wv": rows(wv), "l0x_wq": rows(x0["Wq"]),
        "l0x_w1": rows(x0["W1"].reshape(D, 2, 2, 512).transpose(0, 2, 1, 3).reshape(D, 2048)), "l0x_wout": wout, "l0x_w2": rows(x0["W2"]),
        "l0x_ln_g": bcast(x0["ln_g"]), "l0x_ln_b": bcast(x0["ln_b"]),
        "l0x_cln_g": bcast(x0["cln_g"]), "l0x_cln_b": bcast(x0["cln_b"]),
        "l0a_wqkv": rows(a0["w_qkv"].T), "l0a_wfc": rows(a0["w_fc"].T), "l0a_bfc": bcast(a0["b_fc"]),
        "l0a_gamma": bcast(a0["gamma"]), "l0a_beta": bcast(a0["beta"]),
    }
    params_b = {
        "l1x_w": rows(x1["W"].T), "l1x_b": bcast(x1["b"]),
        "l1a_wq": rows(a1["wq"]), "l1a_wka": rows(a1["wk_a"].T), "l1a_wkb": rows(a1["wk_b"]),
        "l1a_wva": rows(a1["wv_a"].T), "l1a_wvb": a1["wv_b"].T, "l1a_wo": rows(a1["wo"].T),
        "l1f_ln1_w": bcast(f1["ln1_w"]), "l1f_ln1_b": bcast(f1["ln1_b"]), "l1f_b1": bcast(f1["b1"]),
        "l1f_ln2_w": bcast(f1["ln2_w"]), "l1f_ln2_b": bcast(f1["ln2_b"]), "l1f_b2": bcast(f1["b2"]),
    }
    params_e = {
        "l2x_wq": rows(x2["Wq"].T), "l2x_wk": rows(x2["Wk"].T), "l2x_wv": rows(x2["Wv"].T),
        "l2x_wo": rows(x2["Wo"].T), "l2x_bq": cols(x2["bq"]), "l2x_bk": cols(x2["bk"]),
        "l2x_bv": bcast(x2["bv"]), "l2x_bo": bcast(x2["bo"]),
        "l2a_k": rows(a2["k"].T), "l2a_v": rows(a2["v"]),
    }
    bitnet = {"l1f_w1": rows(f1["w1"].T), "l1f_w2": rows(f1["w2"].T)}
    params_c = {
        "l3x_wq": rows(x3["Wq"]), "l3x_bq": bcast(x3["bq"]), "l3x_bqc": col(x3["bq"]), "l3x_wo": x3["Wo"],
        "l3x_bo": bcast(x3["bo"]), "l3a_wi": rows(a3["Wi"]), "l3a_bi": col(a3["bi"]), "l3a_conv": a3["conv_w"].T,
        "l3a_convb": col(a3["conv_b"]), "l3a_wp": a3["Wp"], "l3a_bp": col(a3["bp"]),
        "l3a_wh": np.broadcast_to(a3["Wh"][:, 2:3], (64, 64)), "l3a_bh": np.broadcast_to(a3["bh"][2:3], (64,)).reshape(64, 1),
        "l3a_wq": a3["Wq"], "l3a_bq": col(a3["bq"]), "l3a_wk": a3["Wk"], "l3a_bk": col(a3["bk"]),
        "l3a_wv": a3["Wv"], "l3a_bv": bcast(a3["bv"])[:64], "l3a_w1": a3["W1"].reshape(4, 64, 64).transpose(1, 0, 2),
        "l3a_b1": col(a3["b1"]), "l3a_w2": a3["W2"], "l3a_b2": col(a3["b2"]), "l3a_wo": a3["Wo"], "l3a_bo": bcast(a3["bo"]),
    }

    def pack(params, given):
        parts = []
        for name, n, shape in params:
            a = np.asarray(given[name])
            assert a.shape == (n, *shape), (name, a.shape)
            a = a.reshape(n, -1).astype(np.float32)
            parts.append(np.concatenate([a, np.zeros((P - n, a.shape[1]), np.float32)], 0))
        return np.concatenate(parts, 1)

    def experts(w1, w2):
        w1 = w1.reshape(EXPERTS, DC, P, HID).transpose(0, 2, 1, 3).reshape(EXPERTS, P, -1)
        w2 = w2.reshape(EXPERTS, HB, P, D).transpose(0, 2, 1, 3).reshape(EXPERTS, P, -1)
        return np.concatenate([w1, w2], 2)

    def router(gate_w, b1, b2):
        return pack(ROUTER, {"gate_w": rows(gate_w), "b1": b1.reshape(EXPERTS, HB, P).transpose(2, 0, 1),
                             "b2": b2.reshape(EXPERTS, D)})

    f0, f2, f3 = g("L0_ffn"), g("L2_ffn"), g("L3_ffn")
    ctx = f["ctx_1024"]
    mask_f = f["mask_BxSxS2_ff0"].reshape(TILES, 2, SEQ, KEYS).transpose(0, 2, 1, 3)
    mask_i = f["mask_BxS2_if0"].reshape(TILES, 1, 2, KEYS)[:, :, :, :SEQ]
    mask_b = f["mask_BxS2_bf0"].reshape(TILES, 1, 2, KEYS)
    arrays = {
        "x": f["x"].reshape(TILES, P, D).transpose(1, 0, 2),
        "consts": pack(CONSTS, consts), "params_a": pack(PARAMS_A, params_a), "params_b": pack(PARAMS_B, params_b),
        "params_e": pack(PARAMS_E, params_e), "params_e_late": pack(PARAMS_E_LATE, params_e),
        "params_c": pack(PARAMS_C, params_c), "bitnet": pack(BITNET, bitnet),
        "ctx": ctx.reshape(TILES, 4, P, D).transpose(0, 2, 1, 3),
        "ctx64": ctx[:, :SEQ].reshape(TILES, 2, SEQ, D).transpose(0, 2, 1, 3),
        "ctxT64": ctx[:, :SEQ].reshape(TILES, 2 * SEQ, DC, P).transpose(0, 3, 2, 1),
        "ctxT": ctx.reshape(TILES, 512, DC, P).transpose(0, 3, 2, 1),
        "mask_f": np.concatenate([mask_f, mask_f], 1),
        "mask_i": np.broadcast_to(mask_i, (TILES, P, 2, SEQ)),
        "mask_b": np.broadcast_to(mask_b, (TILES, P, 2, KEYS)),
        "l0f_router": router(f0["gate_w"], f0["fc_bias"], f0["proj_bias"]),
        "l2f_router": router(f2["Wg"].T, f2["b1"], f2["b2"]),
        "l3f_router": router(f3["Wg"].T, f3["b1"], f3["b2"]),
        "l0f_experts": experts(f0["c_fc"], f0["c_proj"]),
        "l2f_experts": experts(f2["W1"], f2["W2"]),
        "l3f_experts": experts(f3["W1"], f3["W2"]),
    }
    stacks = ["ctx", "ctx64", "ctxT", "ctxT64", "mask_f", "mask_i", "mask_b", "l0f_experts", "l2f_experts", "l3f_experts"]
    for name in stacks:
        a = arrays[name]
        arrays[name] = a.reshape(a.shape[0] * a.shape[1], -1)
    arrays = {k: np.ascontiguousarray(v) for k, v in arrays.items()}
    nc = bacc.Bacc("TRN2", target_bir_lowering=False, num_devices=1)
    dram = {k: nc.dram_tensor(k, v.shape, mybir.dt.from_np(v.dtype), kind="ExternalInput").ap() for k, v in arrays.items()}
    out = nc.dram_tensor("out", (P, TILES, D), F32, kind="ExternalOutput").ap()
    perceiver_kernel(nc, dram, out)
    got = run(nc, [arrays], core_ids=[0]).results[0]["out"]
    return got.reshape(P, TILES, D).transpose(1, 0, 2).reshape(BATCH, SEQ, D)
```

```python
from contextlib import ExitStack
from itertools import zip_longest

import concourse.bass as bass
from concourse import mybir

ALU = mybir.AluOpType
ACT = mybir.ActivationFunctionType
F32 = mybir.dt.float32
BF16 = mybir.dt.bfloat16
I32 = mybir.dt.int32
U32 = mybir.dt.uint32
AX = mybir.AxisListType.X

P = 128
BATCH, SEQ, KEYS, D = 16, 64, 256, 256
TOKENS = BATCH * SEQ
TILES = TOKENS // P
DC = D // P
HEADS, DH = 16, 16
PAIRS = HEADS // 2
EXPERTS, HID = 8, 1024
HB = HID // P
HALF = 512
STATE, KSIZE, CHUNK = 64, 5, 16
EXPERT_ROW = 2 * DC * HID + HB + D
FREE_BLOCK = 2 * P
FREE_BLOCKS = (2 * TOKENS + EXPERTS * (FREE_BLOCK - 1)) // FREE_BLOCK
SLOTS = FREE_BLOCKS * FREE_BLOCK
CLEARING = 4 * P
CLEARINGS = -(-SLOTS // CLEARING) + 1
EPS = 1e-5
ROUND = 1.5 * 2.0 ** 23
FAR = -1e30
TAKEN = -3e38

CONSTS = [
    ("ident", P, (P,)), ("tri", P, (P,)), ("ones", P, (P,)), ("batch_ones", P, (P,)),
    ("headmask", P, (8,)), ("causal", P, (SEQ,)), ("strict", P, (SEQ,)), ("experts", P, (EXPERTS,)),
    ("blocks", P, (FREE_BLOCKS,)), ("spill", P, (2 * TILES,)),
    ("rope", P, (DC, P)),
]
PARAMS_A = [
    ("l0x_wk", P, (DC, P)), ("l0x_wv", P, (DC, 64)), ("l0x_wq", P, (DC, 1024)), ("l0x_w1", P, (DC, 2048)),
    ("l0x_wout", P, (8, D)), ("l0x_w2", P, (8, D)), ("l0x_ln_g", P, (D,)), ("l0x_ln_b", P, (D,)),
    ("l0x_cln_g", P, (D,)), ("l0x_cln_b", P, (D,)),
    ("l0a_wqkv", P, (DC, 3 * D)), ("l0a_wfc", P, (DC, D)), ("l0a_bfc", P, (D,)), ("l0a_gamma", P, (D,)),
    ("l0a_beta", P, (D,)),
]
PARAMS_B = [
    ("l1x_w", P, (DC, D)), ("l1x_b", P, (D,)),
    ("l1a_wq", P, (DC, D)), ("l1a_wka", P, (DC, 64)), ("l1a_wkb", P, (DC, 64)), ("l1a_wva", P, (DC, 64)),
    ("l1a_wvb", 64, (D,)), ("l1a_wo", P, (DC, D)),
    ("l1f_ln1_w", P, (D,)), ("l1f_ln1_b", P, (D,)), ("l1f_b1", P, (HID,)),
    ("l1f_ln2_w", P, (HID,)), ("l1f_ln2_b", P, (HID,)), ("l1f_b2", P, (D,)),
]
PARAMS_E = [
    ("l2a_k", P, (DC, 2048)), ("l2x_bq", P, (DC,)), ("l2x_bk", P, (DC,)), ("l2x_bv", P, (D,)), ("l2x_bo", P, (D,)),
    ("l2x_wk", P, (DC, D)), ("l2x_wv", P, (DC, D)),
]
PARAMS_E_LATE = [("l2x_wq", P, (DC, D)), ("l2x_wo", P, (DC, D)), ("l2a_v", P, (16, D))]
BITNET = [("l1f_w1", P, (DC, HID)), ("l1f_w2", P, (HB, D))]
PARAMS_C = [
    ("l3x_wq", P, (DC, 64)), ("l3x_bq", P, (64,)), ("l3x_bqc", 64, (1,)), ("l3x_wo", 64, (D,)), ("l3x_bo", P, (D,)),
    ("l3a_wi", P, (DC, 64)), ("l3a_bi", 64, (1,)), ("l3a_conv", 64, (KSIZE,)), ("l3a_convb", 64, (1,)),
    ("l3a_wp", 64, (64,)), ("l3a_bp", 64, (1,)), ("l3a_wh", 64, (64,)), ("l3a_bh", 64, (1,)),
    ("l3a_wq", 64, (64,)), ("l3a_bq", 64, (1,)), ("l3a_wk", 64, (64,)), ("l3a_bk", 64, (1,)),
    ("l3a_wv", 64, (64,)), ("l3a_bv", 64, (64,)), ("l3a_w1", 64, (4, 64)), ("l3a_b1", 64, (1,)),
    ("l3a_w2", 64, (64,)), ("l3a_b2", 64, (1,)), ("l3a_wo", 64, (D,)), ("l3a_bo", P, (D,)),
]


def length(shape):
    n = 1
    for s in shape:
        n *= s
    return n


def width(params):
    return sum(length(s) for _, _, s in params)


def view(region, at, shape, parts=P):
    flat = region[0:parts, at:at + length(shape)]
    if len(shape) == 2:
        return flat.rearrange("p (a b) -> p a b", b=shape[1])
    if len(shape) == 3:
        return flat.rearrange("p (a b c) -> p a b c", b=shape[1], c=shape[2])
    return flat


def views(region, params):
    at, out = 0, {}
    for name, parts, shape in params:
        out[name] = view(region, at, shape, parts)
        at += length(shape)
    return out


class Work:

    def __init__(self, region):
        self.region, self.at = region, 0

    def __call__(self, *shape, parts=P):
        out = view(self.region, self.at, shape, parts)
        self.at += length(shape)
        assert self.at <= self.region.shape[1], self.at
        return out


def in_turn(*programs):
    for _ in zip_longest(*programs):
        pass


class Chain:

    def __init__(self, eng, sem):
        self.eng, self.sem, self.n = eng, sem, 0

    def go(self, ins):
        ins.then_inc(self.sem, 1)
        self.n += 1

    def settle(self):
        self.eng.wait_ge(self.sem, self.n)

    def do(self, ins):
        self.go(ins)
        self.settle()


class Signals:

    def __init__(self, nc, ctx, count):
        self.free = [ctx.enter_context(nc.semaphore(f"signal{n}")) for n in range(count)]
        self.all = range(self.free[0].num, self.free[-1].num + 1)
        self.named = {}

    def __call__(self, name):
        if name not in self.named:
            self.named[name] = self.free[len(self.named)]
        return self.named[name]

    def forget(self):
        self.named = {}


def perceiver_kernel(nc, dram, out):
    with ExitStack() as ctx:
        build(nc, ctx, dram, out)


def build(nc, ctx, dram, out):
    def sb(name, shape, dt=F32):
        return ctx.enter_context(nc.sbuf_tensor(name, shape, dt))

    X = sb("X", [P, TILES, D])
    XNT_ALL = sb("XNT_all", [P, DC, TOKENS])
    CONST = sb("constants", [P, width(CONSTS)])
    PARAM = sb("params", [P, max(width(PARAMS_A), width(PARAMS_B) + width(PARAMS_E))])
    W1Q = sb("w1_ternary", [P, DC, HID], BF16)
    W2Q = sb("w2_ternary", [P, HB, D], BF16)
    IDB = sb("identity_bf16", [P, P], BF16)
    REGION = sb("work", [P, 21600])
    XN_ALL = sb("XN_all", [P, TILES, D])
    GATE_W = sb("gate_w", [P, DC * EXPERTS])
    WEIGHT = sb("weight_of_choice", [P, 2 * TILES])
    WSCALE = sb("ternary_scales", [P, 2])
    RECS2 = sb("ternary_recs", [P, 2])
    ABS = sb("ternary_abs", [P, 2])
    PS = ctx.enter_context(nc.psum_tensor("PS", [P, 4096], F32))

    K = views(CONST, CONSTS)
    TURNED = [PS[:, 2048:2560], PS[:, 2560:3072]]
    DOWN = [PS[:, 3072:3072 + D], PS[:, 3584:3584 + D]]
    ident = K["ident"]
    S = Signals(nc, ctx, 132)
    PARAMS_LOADED = ctx.enter_context(nc.semaphore("params_loaded"))
    SCATTERED = ctx.enter_context(nc.semaphore("scattered"))
    FETCHED_Y = [ctx.enter_context(nc.semaphore(f"fetched{n}")) for n in range(2 * TILES)]
    SLOTS_CLEARED = ctx.enter_context(nc.semaphore("slots_cleared"))
    slots_in = nc.dram_tensor("slots_in", (SLOTS + 2 * TOKENS, D), F32).ap()
    slots_out = nc.dram_tensor("slots_out", (SLOTS + 1, D), F32).ap()

    class Lane:

        def __init__(self, n):
            self.n = n
            at = 2048 * n
            self.psS, self.psA, self.psO = PS[:, at:at + 1024], PS[:, at + 1024:at + 1536], PS[:, at + 1536:at + 2048]
            self.stats = sb(f"bn_stats{n}", [P, 4, 2, 6])
            self.mv = sb(f"mean_var{n}", [P, 4, 2])
            self.var, self.rstd, self.tmp = (sb(f"{x}{n}", [P, 4]) for x in ("var", "rstd", "newton"))
            self.maxes, self.sums, self.recs = (sb(f"{x}{n}", [P, PAIRS]) for x in ("maxes", "sums", "recs"))
            self.one = [sb(f"scalar{n}_{m}", [P, 1]) for m in range(8)]

        def S(self, name):
            return S(f"lane {self.n}: {name}")

    LANES = [Lane(0), Lane(1)]

    def end():
        nc.all_engine_barrier(sems_to_clear=S.all)
        S.forget()

    def stacked(name, i):
        return dram[name][bass.ds(i * P, P), :]

    def rstd_of(L, c, n, var, eps):
        v, y, w = L.var[:, 0:n], L.rstd[:, 0:n], L.tmp[:, 0:n]
        c.do(nc.vector.tensor_scalar(v, var, eps, None, ALU.add))
        c.do(nc.vector.tensor_scalar(y.bitcast(I32), v.bitcast(I32), 1, None, ALU.logical_shift_right))
        c.do(nc.vector.tensor_scalar(y.bitcast(I32), y.bitcast(I32), -1.0, float(0x5F3759DF), ALU.mult, ALU.add))
        for _ in range(3):
            c.do(nc.vector.tensor_tensor(w, y, y, ALU.mult))
            c.do(nc.vector.scalar_tensor_tensor(w, w, -0.5, v, ALU.mult, ALU.mult))
            c.do(nc.vector.scalar_tensor_tensor(y, w, 1.5, y, ALU.add, ALU.mult))

    def layer_norm(L, c, pairs):
        n = len(pairs)
        for j, (src, _) in enumerate(pairs):
            wide = src.shape[1]
            chunks = max(1, wide // 512)
            for k in range(chunks):
                c.go(nc.vector.bn_stats(L.stats[:, j, k, :], src[:, k * wide // chunks:(k + 1) * wide // chunks]))
        c.settle()
        for j in range(n):
            c.go(nc.vector.bn_aggr(L.mv[:, j, :], L.stats[:, j, 0:chunks, :].rearrange("p k s -> p (k s)")))
        c.settle()
        rstd_of(L, c, n, L.mv[:, 0:n, 1], EPS)
        for j, (src, dst) in enumerate(pairs):
            c.go(nc.vector.tensor_scalar(dst, src, L.mv[:, j, 0:1], L.rstd[:, j:j + 1], ALU.subtract, ALU.mult))
        c.settle()

    def affine(c, x, g, b):
        c.do(nc.vector.tensor_tensor(x, x, g, ALU.mult))
        c.do(nc.vector.tensor_tensor(x, x, b, ALU.add))

    def product(out_, lhsT, rhs, n, first=True, last_=True):
        for i in range(n):
            last = nc.tensor.matmul(out_, lhsT(i), rhs(i), start=(first and i == 0), stop=(last_ and i == n - 1))
        return last

    def transpose_x_tensor(L, pe, tag):
        yield
        pe.wait_ge(L.S(tag + " normed"), 1)
        for c in range(DC):
            last = nc.tensor.transpose(L.psA[:, c * P:(c + 1) * P], L.XN[:, c * P:(c + 1) * P], ident)
        last.then_inc(L.S(tag + " turned"), 1)

    def transpose_x_scalar(L, act, tag):
        yield
        act.wait_ge(L.S(tag + " turned"), 1)
        nc.scalar.copy(L.XNT.rearrange("p c t -> p (c t)"), L.psA[:, 0:D]).then_inc(L.S(tag + " xnT"), 1)

    def units(nk):
        n = min(PAIRS, 1024 // nk)
        return [(b, range(g, g + n)) for g in range(0, PAIRS, n) for b in range(2)]

    def attention_tensor(L, pe, tag, nk, dv, query, key, value, column, ready, between=None):
        kc = min(nk, P)
        nkc = nk // kc
        yield
        for name, count in ready:
            pe.wait_ge(L.S(name), count)
        for u, (b, pairs) in enumerate(units(nk)):
            if u and between:
                yield from between(u)
            for n, p in enumerate(pairs):
                last = nc.tensor.matmul(L.psS[:, n * nk:(n + 1) * nk], query(b, p), key(b, p), start=True, stop=True)
            last.then_inc(L.S(tag + " scores"), 1)
            yield
            pe.wait_ge(L.S(tag + " probs"), u + 1)
            for i in range(len(pairs) * nkc):
                last = nc.tensor.transpose(L.psS[0:kc, i * P:(i + 1) * P], L.PR[:, i * kc:(i + 1) * kc], ident)
            last.then_inc(L.S(tag + " probs turned"), 1)
            yield
            pe.wait_ge(L.S(tag + " probsT"), u + 1)
            for n, p in enumerate(pairs):
                for s in range(2):
                    at = column(p, s)
                    last = product(
                        L.psO[64 * b:64 * b + 64, at:at + dv],
                        lambda c: L.PT[0:kc, (n * nkc + c) * P + 64 * s:(n * nkc + c) * P + 64 * s + 64],
                        lambda c: value(b, c, p, s), nkc)
            last.then_inc(L.S(tag + " mixed"), 1)

    def attention_vector(L, dve, c, tag, nk, mask):
        for u, (b, pairs) in enumerate(units(nk)):
            n = len(pairs)
            yield
            dve.wait_ge(L.S(tag + " scores"), u + 1)
            src = L.psS[:, 0:n * nk].rearrange("p (h k) -> p h k", k=nk)
            if mask is not None:
                sm = L.SM[:, 0:n * nk].rearrange("p (h k) -> p h k", k=nk)
                c.do(nc.vector.tensor_tensor(sm, src, mask(b).unsqueeze(1).broadcast_to([P, n, nk]), ALU.add))
                src = sm
            c.do(nc.vector.tensor_reduce(L.maxes[:, 0:n], src, AX, ALU.max))
            nc.vector.tensor_scalar(L.maxes[:, 0:n], L.maxes[:, 0:n], -1.0, None, ALU.mult)\
                .then_inc(L.S(tag + " max"), 1)
            yield
            dve.wait_ge(L.S(tag + " exp"), (u + 1) * n)
            c.do(nc.vector.reciprocal(L.recs[:, 0:n], L.sums[:, 0:n]))
            pr = L.PR[:, 0:n * nk].rearrange("p (h k) -> p h k", k=nk)
            nc.vector.tensor_tensor(pr, pr, L.recs[:, 0:n].unsqueeze(2).broadcast_to([P, n, nk]), ALU.mult)\
                .then_inc(L.S(tag + " probs"), 1)

    def attention_scalar(L, act, tag, nk, mask, after=None):
        kc = min(nk, P)
        src = L.psS if mask is None else L.SM
        for u, (b, pairs) in enumerate(units(nk)):
            n = len(pairs)
            yield
            act.wait_ge(L.S(tag + " max"), u + 1)
            for p in range(n):
                nc.scalar.activation(L.PR[:, p * nk:(p + 1) * nk], src[:, p * nk:(p + 1) * nk], ACT.Exp,
                                     bias=L.maxes[:, p:p + 1], accum_out=L.sums[:, p:p + 1])\
                    .then_inc(L.S(tag + " exp"), 1)
            yield
            act.wait_ge(L.S(tag + " probs turned"), u + 1)
            m = n * (nk // kc) * P
            nc.scalar.copy(L.PT[0:kc, 0:m], L.psS[0:kc, 0:m]).then_inc(L.S(tag + " probsT"), 1)
            if after:
                yield from after(u)

    def project_tensor(L, pe, tag, weight):
        yield
        pe.wait_ge(L.S(tag + " o"), 1)
        for i in range(DC):
            last = nc.tensor.transpose(L.psS[:, i * P:(i + 1) * P], L.OO[:, i * P:(i + 1) * P], ident)
        last.then_inc(L.S(tag + " o turned"), 1)
        yield
        pe.wait_ge(L.S(tag + " oT"), 1)
        product(L.psA[:, 0:D], lambda i: L.OT[:, i * P:(i + 1) * P], lambda i: weight[:, i, :], DC)\
            .then_inc(L.S(tag + " y"), 1)

    def project_scalar(L, act, tag, count):
        yield
        act.wait_ge(L.S(tag + " mixed"), count)
        nc.scalar.copy(L.OO[:, 0:D], L.psO[:, 0:D]).then_inc(L.S(tag + " o"), 1)
        yield
        act.wait_ge(L.S(tag + " o turned"), 1)
        nc.scalar.copy(L.OT[:, 0:D], L.psS[:, 0:D]).then_inc(L.S(tag + " oT"), 1)

    def residual(L, dve, c, tag, bias):
        yield
        dve.wait_ge(L.S(tag + " y"), 1)
        c.do(nc.vector.tensor_tensor(L.XT, L.XT, L.psA[:, 0:D], ALU.add))
        if bias is not None:
            c.do(nc.vector.tensor_tensor(L.XT, L.XT, bias, ALU.add))

    def tell(L, name):
        nc.vector.tensor_copy(L.one[7][:], L.mv[:, 0, 0:1]).then_inc(L.S(name), 1)

    def normed(L, c, tag):
        layer_norm(L, c, [(L.XT, L.XN)])
        tell(L, tag + " normed")

    def fetch_tile(L, c, t):
        c.do(nc.vector.tensor_copy(L.XT.unsqueeze(1), X[:, bass.ds(t, 1), :]))

    def to_experts_vector(L, dve, c, t):
        c.do(nc.vector.tensor_copy(X[:, bass.ds(t, 1), :], L.XT.unsqueeze(1)))
        normed(L, c, "router")
        c.do(nc.vector.tensor_copy(XN_ALL[:, bass.ds(t, 1), :], L.XN.unsqueeze(1)))
        yield
        dve.wait_ge(L.S("router turned"), 1)
        c.do(nc.vector.tensor_copy(XNT_ALL[:, :, bass.ds(t * P, P)], L.psA[:, 0:D].rearrange("p (c t) -> p c t", t=P)))

    def head_queries(L, c, src, tag):
        for blk in range(DC):
            for b in range(2):
                at = 8 * (2 * blk + b)
                c.go(nc.vector.tensor_tensor(
                    L.QBD[:, at:at + 8, :],
                    src[:, blk, 64 * b:64 * b + 64].unsqueeze(1).broadcast_to([P, 8, SEQ]),
                    K["headmask"].unsqueeze(2).broadcast_to([P, 8, SEQ]), ALU.mult))
        c.settle()
        tell(L, tag + " queries")

    def masked_query(L):
        def query(b, p):
            at = 8 * (2 * (p // 4) + b) + 2 * (p % 4)
            return L.QBD[:, at:at + 2, :].rearrange("p h t -> p (h t)")
        return query

    def column16(p, s):
        return (2 * p + s) * DH

    def lanes_block(i, load, vector, scalar, tensor):
        with nc.Block(no_gpsimd_drain=True) as block:
            @block.sync
            def _(sp):
                for L in LANES:
                    load(L, sp, 2 * i + L.n)

            @block.vector
            def _(dve):
                in_turn(*(vector(L, dve, Chain(dve, L.S("vector")), 2 * i + L.n) for L in LANES))

            @block.scalar
            def _(act):
                in_turn(*(scalar(L, act) for L in LANES))

            @block.tensor
            def _(pe):
                in_turn(*(tensor(L, pe) for L in LANES))
        end()

    with nc.Block(no_gpsimd_drain=True) as block:
        @block.sync
        def _(sp):
            sp.dma_start(X[:], dram["x"]).then_inc(S("loaded"), 16)
            sp.dma_start(CONST[:], dram["consts"]).then_inc(S("loaded"), 16)
            sp.dma_start(PARAM[:, 0:width(PARAMS_A)], dram["params_a"]).then_inc(S("loaded"), 16)
            sp.wait_ge(S("loaded"), 48)
            sp.wait_ge(S("zeros"), 1)
            zeros = W1Q[:].rearrange("p a b -> p (a b)").bitcast(F32)
            for at in range(0, SLOTS, CLEARING):
                n = min(P, (SLOTS - at) // 4)
                sp.dma_start(slots_in[at:at + 4 * n, :].rearrange("(p a) d -> p (a d)", a=4), zeros[0:n, :])\
                    .then_inc(SLOTS_CLEARED, 16)
            sp.dma_start(slots_out[0:1, :], zeros[0:1, 0:D]).then_inc(SLOTS_CLEARED, 16)

        @block.vector
        def _(dve):
            nc.vector.memset(W1Q[:], 0.0).then_inc(S("zeros"), 1)
    end()

    A = views(PARAM, PARAMS_A)
    work = Work(REGION)
    for L in LANES:
        L.XT, L.XN, L.XNT = work(D), work(D), work(DC, P)
        L.SM, L.PR, L.PT = work(1024), work(1024), work(1024)
        L.OO, L.OT = work(512), work(512)
        L.CTX, L.CTXT = work(4, D), work(DC, 512)
        L.KT, L.V, L.QT = work(512), work(4, 64), work(2, 8, SEQ)
        L.MASK = work(2, KEYS)
        L.HH, L.HHT = work(1024), L.CTX.rearrange("p j d -> p (j d)")
        L.V256 = L.HHT[:, 0:D]
        L.QK = L.HH[:, 0:512].rearrange("p (c t) -> p c t", t=P)

    def a_load(L, sp, t):
        sp.dma_start(L.CTX.rearrange("p j d -> p (j d)"), stacked("ctx", t)).then_inc(L.S("ctx"), 16)
        sp.dma_start(L.MASK.rearrange("p b k -> p (b k)"), stacked("mask_f", t)).then_inc(L.S("mask"), 16)

    def a_vector(L, dve, c, t):
        dve.wait_ge(L.S("ctx"), 16)
        layer_norm(L, c, [(L.CTX[:, j, :], L.CTX[:, j, :]) for j in range(4)])
        c.do(nc.vector.tensor_tensor(L.CTX, L.CTX, A["l0x_cln_g"].unsqueeze(1).broadcast_to([P, 4, D]), ALU.mult))
        nc.vector.tensor_tensor(L.CTX, L.CTX, A["l0x_cln_b"].unsqueeze(1).broadcast_to([P, 4, D]), ALU.add)\
            .then_inc(L.S("ctx normed"), 1)
        fetch_tile(L, c, t)
        yield
        layer_norm(L, c, [(L.XT, L.XN)])
        layer_norm(L, c, [(L.XN, L.XN)])
        affine(c, L.XN, A["l0x_ln_g"], A["l0x_ln_b"])
        tell(L, "l0x normed")
        for h in range(2):
            yield
            dve.wait_ge(L.S("tanh"), h + 1)
            hh = L.HH[:, 512 * h:512 * h + 512]
            c.do(nc.vector.scalar_tensor_tensor(hh, L.OO, 1.0, L.psS[:, 512:1024], ALU.add, ALU.mult))
            nc.vector.scalar_tensor_tensor(hh, hh, 0.5, L.psS[:, 0:512], ALU.mult, ALU.mult)\
                .then_inc(L.S("gated"), 1)
        dve.wait_ge(L.S("mask"), 16)
        yield from attention_vector(L, dve, c, "l0x", KEYS, lambda b: L.MASK[:, b, :])
        yield from residual(L, dve, c, "l0x", None)
        normed(L, c, "l0a")
        yield
        dve.wait_ge(L.S("l0a qkv"), 1)
        nc.vector.tensor_copy(L.V256, L.psO[:, 0:D]).then_inc(L.S("l0a values"), 1)
        yield
        dve.wait_ge(L.S("l0a scores"), 1)
        c.do(nc.vector.tensor_reduce(L.one[0][:], L.psS[:, 512:576], AX, ALU.max))
        nc.vector.tensor_scalar(L.one[1][:], L.one[0][:], -1.0, None, ALU.mult).then_inc(L.S("l0a max"), 1)
        yield
        dve.wait_ge(L.S("l0a exp"), 1)
        c.do(nc.vector.reciprocal(L.one[3][:], L.one[2][:]))
        c.do(nc.vector.tensor_scalar(L.PR[:, 0:64], L.PR[:, 0:64], L.one[3][:], None, ALU.mult))
        c.do(nc.vector.tensor_reduce(L.one[4][:], L.PR[:, 0:64], AX, ALU.add))
        dve.wait_ge(L.S("l0a value sums"), 1)
        nc.vector.tensor_scalar(L.OO[:, 0:D], L.psO[:, 0:D], L.one[4][:], None, ALU.mult).then_inc(L.S("l0a o"), 1)
        yield
        dve.wait_ge(L.S("l0a y"), 1)
        c.do(nc.vector.tensor_tensor(L.XN, L.XN, L.psA[:, 0:D], ALU.add))
        c.do(nc.vector.tensor_tensor(L.XN, L.XN, A["l0a_bfc"], ALU.add))
        layer_norm(L, c, [(L.XN, L.XN)])
        affine(c, L.XN, A["l0a_gamma"], A["l0a_beta"])
        c.do(nc.vector.tensor_tensor(L.XT, L.XT, L.XN, ALU.add))
        yield from to_experts_vector(L, dve, c, t)

    def a_scalar(L, act):
        yield
        act.wait_ge(L.S("ctx turned"), 1)
        nc.scalar.copy(L.CTXT.rearrange("p c t -> p (c t)"), L.psS).then_inc(L.S("ctxT"), 1)
        yield
        act.wait_ge(L.S("l0x kv"), 1)
        nc.scalar.copy(L.KT, L.psA).then_inc(L.S("l0x kvs"), 1)
        nc.scalar.copy(L.V.rearrange("p j d -> p (j d)"), L.psO[:, 0:256]).then_inc(L.S("l0x kvs"), 1)
        yield from transpose_x_scalar(L, act, "l0x")
        yield
        act.wait_ge(L.S("l0x q"), 1)
        nc.scalar.mul(L.QT.rearrange("p b h t -> p h b t"),
                      L.psS.rearrange("p (h b t) -> p h b t", b=2, t=SEQ), 0.125).then_inc(L.S("l0x qT"), 1)
        for h in range(2):
            yield
            act.wait_ge(L.S("hidden"), h + 1)
            nc.scalar.activation(L.OO, L.psS[:, 512:1024], ACT.Tanh, scale=0.5).then_inc(L.S("tanh"), 1)
        yield
        act.wait_ge(L.S("hidden turned"), 1)
        nc.scalar.copy(L.HHT, L.psS).then_inc(L.S("hiddenT"), 1)

        def evict(u):
            if u % 2:
                yield
                act.wait_ge(L.S("l0x mixed"), u + 1)
                nc.scalar.copy(L.OO, L.psO).then_inc(L.S("l0x o"), 1)
                yield
                act.wait_ge(L.S("l0x o turned"), u // 2 + 1)
                nc.scalar.copy(L.OT, L.psS[:, 0:512]).then_inc(L.S("l0x oT"), 1)

        yield from attention_scalar(L, act, "l0x", KEYS, True, evict)
        yield from transpose_x_scalar(L, act, "l0a")
        yield
        act.wait_ge(L.S("l0a qkv"), 1)
        nc.scalar.mul(L.QK[:, 0:2, :], L.psS[:, 0:256].rearrange("p (c t) -> p c t", t=P), D ** -0.5)\
            .then_inc(L.S("l0a qk"), 1)
        nc.scalar.copy(L.QK[:, 2:4, :], L.psS[:, 256:512].rearrange("p (c t) -> p c t", t=P))\
            .then_inc(L.S("l0a qk"), 1)
        yield
        act.wait_ge(L.S("l0a max"), 1)
        nc.scalar.activation(L.PR[:, 0:64], L.psS[:, 512:576], ACT.Exp, bias=L.one[1][:], accum_out=L.one[2][:])\
            .then_inc(L.S("l0a exp"), 1)
        yield
        act.wait_ge(L.S("l0a o turned"), 1)
        nc.scalar.copy(L.OT[:, 0:D], L.psS[:, 0:D]).then_inc(L.S("l0a oT"), 1)

    def a_tensor(L, pe):
        yield
        pe.wait_ge(L.S("ctx normed"), 1)
        for c in range(DC):
            for j in range(4):
                last = nc.tensor.transpose(L.psS[:, c * 512 + j * P:c * 512 + (j + 1) * P],
                                           L.CTX[:, j, c * P:(c + 1) * P], ident)
        last.then_inc(L.S("ctx turned"), 1)
        yield
        pe.wait_ge(L.S("ctxT"), 1)
        product(L.psA, lambda i: A["l0x_wk"][:, i, :], lambda i: L.CTXT[:, i, :], DC)
        for j in range(4):
            last = product(L.psO[:, 64 * j:64 + 64 * j], lambda i: L.CTXT[:, i, j * P:(j + 1) * P],
                           lambda i: A["l0x_wv"][:, i, :], DC)
        last.then_inc(L.S("l0x kv"), 1)
        yield
        pe.wait_ge(L.S("l0x kvs"), 2)
        yield from transpose_x_tensor(L, pe, "l0x")
        yield
        pe.wait_ge(L.S("l0x xnT"), 1)
        for j in range(8):
            last = product(L.psS[:, j * P:(j + 1) * P], lambda i: A["l0x_wq"][:, i, j * P:(j + 1) * P],
                           lambda i: L.XNT[:, i, :], DC)
        last.then_inc(L.S("l0x q"), 1)
        yield
        pe.wait_ge(L.S("l0x qT"), 1)
        for h in range(2):
            for j in range(2):
                last = product(L.psS[:, j * 512:(j + 1) * 512], lambda i: L.XNT[:, i, :],
                               lambda i: A["l0x_w1"][:, i, (2 * h + j) * 512:(2 * h + j + 1) * 512], DC)
            last.then_inc(L.S("hidden"), 1)
            yield
            pe.wait_ge(L.S("gated"), h + 1)
        for i in range(8):
            last = nc.tensor.transpose(L.psS[:, i * P:(i + 1) * P], L.HH[:, i * P:(i + 1) * P], ident)
        last.then_inc(L.S("hidden turned"), 1)
        yield
        pe.wait_ge(L.S("hiddenT"), 1)
        product(L.psA[:, 0:D], lambda i: L.HHT[:, i * P:(i + 1) * P], lambda i: A["l0x_w2"][:, i, :], 8, last_=False)

        def query(b, p):
            r, k = p // 4, p % 4
            return L.QT[64 * r:64 * r + 64, b, 2 * k:2 * k + 2, :].rearrange("p h t -> p (h t)")

        def out_of_four_pairs(u):
            if u % 2 == 0:
                g = u // 2 - 1
                yield
                pe.wait_ge(L.S("l0x o"), g + 1)
                for i in range(4):
                    last = nc.tensor.transpose(L.psS[:, i * P:(i + 1) * P], L.OO[:, i * P:(i + 1) * P], ident)
                last.then_inc(L.S("l0x o turned"), 1)
                yield
                pe.wait_ge(L.S("l0x oT"), g + 1)
                last = product(L.psA[:, 0:D], lambda i: L.OT[:, i * P:(i + 1) * P],
                               lambda i: A["l0x_wout"][:, 4 * g + i, :], 4, first=False, last_=(g == 1))
                if g == 1:
                    last.then_inc(L.S("l0x y"), 1)

        yield from attention_tensor(
            L, pe, "l0x", KEYS, 64, query,
            lambda b, p: L.KT[64 * (p // 4):64 * (p // 4) + 64, 256 * b:256 * b + 256],
            lambda b, c, p, s: L.V[:, 2 * b + c, :], lambda p, s: 64 * (2 * (p % 4) + s),
            [("gated", 2)], out_of_four_pairs)
        yield from out_of_four_pairs(4)
        yield from transpose_x_tensor(L, pe, "l0a")
        yield
        pe.wait_ge(L.S("l0a xnT"), 1)
        for j in range(4):
            product(L.psS[:, j * P:(j + 1) * P], lambda i: A["l0a_wqkv"][:, i, j * P:(j + 1) * P],
                    lambda i: L.XNT[:, i, :], DC)
        product(L.psO[:, 0:D], lambda i: L.XNT[:, i, :], lambda i: A["l0a_wqkv"][:, i, 2 * D:3 * D], DC)\
            .then_inc(L.S("l0a qkv"), 1)
        yield
        pe.wait_ge(L.S("l0a qk"), 2)
        for b in range(2):
            last = product(L.psS[64 * b:64 * b + 64, 512:576], lambda i: L.QK[:, i, 64 * b:64 * b + 64],
                           lambda i: L.QK[:, 2 + i, 64 * b:64 * b + 64], DC)
        last.then_inc(L.S("l0a scores"), 1)
        pe.wait_ge(L.S("l0a values"), 1)
        nc.tensor.matmul(L.psO[:, 0:D], K["batch_ones"], L.V256, start=True, stop=True)\
            .then_inc(L.S("l0a value sums"), 1)
        yield from project_tensor(L, pe, "l0a", A["l0a_wfc"])
        yield from transpose_x_tensor(L, pe, "router")

    with nc.Fori(0, TILES // 2) as i:
        lanes_block(i, a_load, a_vector, a_scalar, a_tensor)

    def experts(layer, turn, capacity, softmax_first, next_params):
        size = capacity or FREE_BLOCK
        blocks = EXPERTS if capacity else FREE_BLOCKS
        parts = [(u * P, min(P, size - u * P)) for u in range(-(-size // P))]
        passes = (blocks - 1) // 2
        work = Work(REGION)
        WEIGHTS = [work(EXPERT_ROW), work(EXPERT_ROW)]
        W1 = [w[:, 0:2048].rearrange("p (c h) -> p c h", h=HID) for w in WEIGHTS]
        W2 = [w[:, 2048:4096].rearrange("p (j d) -> p j d", d=D) for w in WEIGHTS]
        B1 = [w[:, 4096:4096 + HB] for w in WEIGHTS]
        B2 = [w[:, 4096 + HB:EXPERT_ROW] for w in WEIGHTS]
        ROWS, Y = [work(len(parts), D), work(len(parts), D)], [work(len(parts), D), work(len(parts), D)]
        SLOTS_T = [work(DC, size), work(DC, size)]
        HT = work(HB, size)
        FETCHED = work(2 * TILES, D)
        LG, VALUES, TOP = work(TILES, EXPERTS), work(TILES, EXPERTS), work(TILES, 8)
        INDEX, INDEXF = work(TILES, 8), work(TILES, 8)
        CHOICE, RANK, PREFIX = (work(2 * TILES, EXPERTS) for _ in range(3))
        W, KEPT, SLOT, SPILL = (work(2 * TILES) for _ in range(4))
        BASE, BLOCKS_OF, UP_TO = work(EXPERTS), work(EXPERTS), work(EXPERTS)
        BELOW, EXPERT_OF = work(FREE_BLOCKS, EXPERTS), work(FREE_BLOCKS)
        SLOT_TO, SLOT_FROM = work(2 * TILES).bitcast(I32), work(2 * TILES).bitcast(I32)
        EXPERT_OF_BLOCK, EXPERT_AHEAD = work(FREE_BLOCKS).bitcast(I32), work(2).bitcast(I32)
        A8, B8 = work(TILES), work(TILES)
        wide = lambda x: x.unsqueeze(2).broadcast_to([P, x.shape[1], EXPERTS])

        def turn_slots(rows):
            for u, (at, n) in enumerate(parts):
                for q in range(DC):
                    last = nc.tensor.transpose(TURNED[q][:, at:at + n], rows[0:n, u, q * P:(q + 1) * P], ident[0:n, 0:n])
            last.then_inc(S("slots turned"), 1)

        def keep_slots(dve, n, s):
            dve.wait_ge(S("slots turned"), n + 1)
            for q in range(DC):
                nc.vector.tensor_copy(SLOTS_T[s][:, q, :], TURNED[q][:, 0:size]).then_inc(S("slots here"), 1)

        with nc.Block(no_gpsimd_drain=True) as block:
            @block.sync
            def _(sp):
                sp.dma_start(GATE_W[:], dram[layer + "_gate_w"]).then_inc(S("gate_w"), 16)
                if capacity:
                    sp.dma_start(WEIGHTS[0], dram[layer + "_experts"][0:P, :]).then_inc(S("weights"), 16)
                else:
                    sp.wait_ge(S("slots"), 1)
                    expert = sp.value_load(EXPERT_OF_BLOCK[0:1, 0:1], min_val=0, max_val=EXPERTS - 1)
                    sp.dma_start(WEIGHTS[0], stacked(layer + "_experts", expert)).then_inc(S("weights"), 16)
                for name, at, params in next_params:
                    sp.dma_start(PARAM[:, at:at + width(params)], dram[name]).then_inc(PARAMS_LOADED, 16)
                sp.wait_ge(SCATTERED, 16 * 2 * TILES * turn)
                for u, (at, n) in enumerate(parts):
                    sp.dma_start(ROWS[0][0:n, u, :], slots_in[at:at + n, :]).then_inc(S("rows"), 16)
                sp.wait_ge(S("rows"), 16 * len(parts))
                sp.wait_ge(S("weights"), 16)

            @block.gpsimd
            def _(pool):
                pool.wait_ge(SLOTS_CLEARED, 16 * CLEARINGS)
                pool.wait_ge(S("slots"), 1)
                for n in range(2 * TILES):
                    nc.gpsimd.indirect_dma_start(slots_in[:, :], bass.IndirectOffsetOnAxis(ap=SLOT_TO[:, n:n + 1], axis=0),
                                                 XN_ALL[:, n % TILES, :], None).then_inc(SCATTERED, 16)

            @block.tensor
            def _(pe):
                pe.wait_ge(S("gate_w"), 16)
                for t in range(TILES):
                    last = product(PS[:, t * EXPERTS:(t + 1) * EXPERTS], lambda i: XNT_ALL[:, i, t * P:(t + 1) * P],
                                   lambda i: GATE_W[:, i * EXPERTS:(i + 1) * EXPERTS], DC)
                last.then_inc(S("logits"), 1)
                pe.wait_ge(S("choices"), 1)
                nc.tensor.matmul(PS[:, 2048:2176], K["tri"], CHOICE.rearrange("p n e -> p (n e)"),
                                 start=True, stop=True)
                nc.tensor.matmul(PS[:, 2560:2688], K["ones"], CHOICE.rearrange("p n e -> p (n e)"),
                                 start=True, stop=True).then_inc(S("counts"), 1)
                pe.wait_ge(S("rows"), 16 * len(parts))
                turn_slots(ROWS[0])

            @block.scalar
            def _(act):
                act.wait_ge(S("to exp"), 1)
                if softmax_first:
                    nc.scalar.activation(VALUES, VALUES, ACT.Exp).then_inc(S("exp"), 1)
                else:
                    nc.scalar.activation(A8, A8, ACT.Exp).then_inc(S("exp"), 1)

            @block.vector
            def _(dve):
                c = Chain(dve, S("vector"))
                dve.wait_ge(S("logits"), 1)
                c.do(nc.vector.tensor_copy(LG.rearrange("p t e -> p (t e)"), PS[:, 0:TILES * EXPERTS]))
                values = LG
                if softmax_first:
                    c.do(nc.vector.tensor_reduce(A8, LG, AX, ALU.max))
                    nc.vector.tensor_tensor(VALUES, LG, wide(A8), ALU.subtract).then_inc(S("to exp"), 1)
                    dve.wait_ge(S("exp"), 1)
                    c.do(nc.vector.tensor_reduce(A8, VALUES, AX, ALU.add))
                    c.do(nc.vector.reciprocal(B8, A8))
                    c.do(nc.vector.tensor_tensor(VALUES, VALUES, wide(B8), ALU.mult))
                    values = VALUES
                for t in range(TILES):
                    c.go(nc.vector.max(TOP[:, t, :], values[:, t, :]))
                c.settle()
                for t in range(TILES):
                    c.go(nc.vector.max_index(INDEX[:, t, :].bitcast(U32), TOP[:, t, :], values[:, t, :]))
                c.settle()
                c.do(nc.vector.tensor_copy(INDEXF, INDEX.bitcast(U32)))
                for k in range(2):
                    c.go(nc.vector.tensor_tensor(
                        CHOICE[:, k * TILES:(k + 1) * TILES, :],
                        K["experts"].unsqueeze(1).broadcast_to([P, TILES, EXPERTS]),
                        INDEXF[:, :, k:k + 1].broadcast_to([P, TILES, EXPERTS]), ALU.is_equal))
                c.settle()
                nc.vector.tensor_copy(RECS2[:, 0:1], CHOICE[:, 0, 0:1]).then_inc(S("choices"), 1)
                if softmax_first:
                    for k in range(2):
                        c.go(nc.vector.tensor_copy(W[:, k * TILES:(k + 1) * TILES], TOP[:, :, k]))
                    c.settle()
                else:
                    nc.vector.tensor_tensor(A8, TOP[:, :, 1], TOP[:, :, 0], ALU.subtract).then_inc(S("to exp"), 1)
                    dve.wait_ge(S("exp"), 1)
                    c.do(nc.vector.tensor_scalar(B8, A8, 1.0, None, ALU.add))
                    c.do(nc.vector.reciprocal(W[:, 0:TILES], B8))
                    c.do(nc.vector.tensor_tensor(W[:, TILES:2 * TILES], A8, W[:, 0:TILES], ALU.mult))
                dve.wait_ge(S("counts"), 1)
                c.do(nc.vector.memset(PREFIX[:, 0, :], 0.0))
                for n in range(1, 2 * TILES):
                    c.do(nc.vector.tensor_tensor(PREFIX[:, n, :], PREFIX[:, n - 1, :],
                                                 PS[:, 2560 + (n - 1) * EXPERTS:2560 + n * EXPERTS], ALU.add))
                flat = lambda x: x.rearrange("p n e -> p (n e)")
                c.do(nc.vector.tensor_tensor(flat(RANK), PS[:, 2048:2176], flat(PREFIX), ALU.add))
                if capacity:
                    c.do(nc.vector.tensor_scalar(flat(PREFIX), flat(RANK), capacity + 0.5, None, ALU.is_lt))
                    c.do(nc.vector.tensor_tensor(CHOICE, CHOICE, PREFIX, ALU.mult))
                    c.do(nc.vector.tensor_scalar(BASE, K["experts"], float(size), -1.0, ALU.mult, ALU.add))
                else:
                    c.do(nc.vector.tensor_tensor(BLOCKS_OF, PREFIX[:, 2 * TILES - 1, :],
                                                 PS[:, 2560 + (2 * TILES - 1) * EXPERTS:2560 + 2 * TILES * EXPERTS],
                                                 ALU.add))
                    c.do(nc.vector.tensor_scalar(BLOCKS_OF, BLOCKS_OF, 1.0 / size, (size - 0.5) / size - 0.5,
                                                 ALU.mult, ALU.add))
                    c.do(nc.vector.tensor_scalar(BLOCKS_OF, BLOCKS_OF, ROUND, None, ALU.add))
                    c.do(nc.vector.tensor_scalar(BLOCKS_OF, BLOCKS_OF, -ROUND, None, ALU.add))
                    c.do(nc.vector.tensor_copy(UP_TO[:, 0:1], BLOCKS_OF[:, 0:1]))
                    for e in range(1, EXPERTS):
                        c.do(nc.vector.tensor_tensor(UP_TO[:, e:e + 1], UP_TO[:, e - 1:e], BLOCKS_OF[:, e:e + 1], ALU.add))
                    c.do(nc.vector.tensor_tensor(BASE, UP_TO, BLOCKS_OF, ALU.subtract))
                    c.do(nc.vector.tensor_scalar(BASE, BASE, float(size), -1.0, ALU.mult, ALU.add))
                    c.do(nc.vector.tensor_tensor(BELOW, UP_TO.unsqueeze(1).broadcast_to([P, blocks, EXPERTS]),
                                                 wide(K["blocks"]), ALU.is_le))
                    c.do(nc.vector.tensor_reduce(EXPERT_OF, BELOW, AX, ALU.add))
                    c.do(nc.vector.tensor_scalar(EXPERT_OF_BLOCK, EXPERT_OF, EXPERTS - 1.0, None, ALU.min))
                c.do(nc.vector.tensor_tensor(RANK, RANK, BASE.unsqueeze(1).broadcast_to([P, 2 * TILES, EXPERTS]), ALU.add))
                c.do(nc.vector.tensor_tensor(RANK, RANK, CHOICE, ALU.mult))
                c.go(nc.vector.tensor_reduce(SLOT, RANK, AX, ALU.add))
                c.go(nc.vector.tensor_reduce(KEPT, CHOICE, AX, ALU.add))
                c.settle()
                c.do(nc.vector.tensor_tensor(SLOT_FROM, SLOT, KEPT, ALU.add))
                if capacity:
                    c.do(nc.vector.tensor_scalar(SPILL, KEPT, -1.0, 1.0, ALU.mult, ALU.add))
                    c.do(nc.vector.tensor_tensor(SPILL, SPILL, K["spill"], ALU.mult))
                    c.do(nc.vector.tensor_tensor(SLOT, SLOT, SPILL, ALU.add))
                nc.vector.tensor_copy(SLOT_TO, SLOT).then_inc(S("slots"), 1)
                c.do(nc.vector.tensor_tensor(WEIGHT[:], W, KEPT, ALU.mult))
                keep_slots(dve, 0, 0)
        end()

        def some_blocks(i, count, more):
            ahead = [1] * (count == 2) + [0] * more
            with nc.Block(no_gpsimd_drain=True) as block:
                @block.sync
                def _(sp):
                    if ahead and not capacity:
                        sp.wait_ge(S("experts ahead"), 1)
                    expert = [2 * i + 1 + m if capacity else
                              sp.value_load(EXPERT_AHEAD[0:1, m:m + 1], min_val=0, max_val=EXPERTS - 1)
                              for m in range(len(ahead))]
                    if count == 2:
                        sp.dma_start(WEIGHTS[1], stacked(layer + "_experts", expert[0])).then_inc(S("weights"), 16)
                    for m, s in enumerate(ahead):
                        for u, (at, n) in enumerate(parts):
                            sp.dma_start(ROWS[s][0:n, u, :], slots_in[bass.ds((2 * i + 1 + m) * size + at, n), :])\
                                .then_inc(S(f"rows {s}"), 16)
                    if more:
                        sp.wait_ge(S("y"), len(parts))
                        sp.dma_start(WEIGHTS[0], stacked(layer + "_experts", expert[-1]))\
                            .then_inc(S("next weights"), 16)
                    for m in range(count):
                        for u, (at, n) in enumerate(parts):
                            sp.wait_ge(S("y"), m * len(parts) + u + 1)
                            sp.dma_start(slots_out[bass.ds((2 * i + m) * size + 1 + at, n), :], Y[m][0:n, u, :])\
                                .then_inc(S("y stored"), 16)
                    if more:
                        sp.wait_ge(S("next weights"), 16)
                    sp.wait_ge(S("y stored"), 16 * count * len(parts))

                @block.tensor
                def _(pe):
                    for m in range(count):
                        if m:
                            pe.wait_ge(S("weights"), 16)
                            pe.wait_ge(S("slots here"), DC)
                        for j in range(HB):
                            n = m * HB + j
                            if n >= 4:
                                pe.wait_ge(S("gelu"), n - 3)
                            product(PS[:, n % 4 * 512:n % 4 * 512 + size], lambda q: W1[m][:, q, j * P:(j + 1) * P],
                                    lambda q: SLOTS_T[m][:, q, :], DC).then_inc(S("up"), 1)
                        if m < len(ahead):
                            pe.wait_ge(S(f"rows {ahead[m]}"), 16 * len(parts))
                            if m:
                                pe.wait_ge(S("slots here"), DC)
                            turn_slots(ROWS[ahead[m]])
                        pe.wait_ge(S("gelu"), (m + 1) * HB)
                        for u, (at, n) in enumerate(parts):
                            k = m * len(parts) + u
                            if k >= 2:
                                pe.wait_ge(S("y"), k - 1)
                            product(DOWN[k % 2][0:n, :], lambda q: HT[:, q, at:at + n], lambda q: W2[m][:, q, :], HB)\
                                .then_inc(S("down"), 1)

                @block.scalar
                def _(act):
                    for m in range(count):
                        if m:
                            act.wait_ge(S("down"), m * len(parts))
                        for j in range(HB):
                            n = m * HB + j
                            act.wait_ge(S("up"), n + 1)
                            nc.scalar.activation(HT[:, j, :], PS[:, n % 4 * 512:n % 4 * 512 + size],
                                                 ACT.Gelu, bias=B1[m][:, j:j + 1]).then_inc(S("gelu"), 1)

                @block.vector
                def _(dve):
                    if ahead and not capacity:
                        nc.vector.tensor_copy(EXPERT_AHEAD[:, 0:len(ahead)], EXPERT_OF_BLOCK[:, bass.ds(2 * i + 1, len(ahead))])\
                            .then_inc(S("experts ahead"), 1)
                    for m in range(count):
                        if m < len(ahead):
                            keep_slots(dve, m, ahead[m])
                        for u, (at, n) in enumerate(parts):
                            k = m * len(parts) + u
                            dve.wait_ge(S("down"), k + 1)
                            nc.vector.tensor_tensor(Y[m][0:n, u, :], DOWN[k % 2][0:n, :], B2[m][0:n, :], ALU.add)\
                                .then_inc(S("y"), 1)
            end()

        with nc.Fori(0, passes) as i:
            some_blocks(i, 2, True)
        some_blocks(passes, blocks - 2 * passes, False)

        with nc.Block(no_gpsimd_drain=True) as block:
            @block.gpsimd
            def _(pool):
                for n in range(2 * TILES):
                    nc.gpsimd.indirect_dma_start(FETCHED[:, n, :], None, slots_out[0:1 + blocks * size, :],
                                                 bass.IndirectOffsetOnAxis(ap=SLOT_FROM[:, n:n + 1], axis=0))\
                        .then_inc(FETCHED_Y[n], 16)

            @block.vector
            def _(dve):
                for n in range(2 * TILES):
                    dve.wait_ge(FETCHED_Y[n], 16 * turn)
                    if n >= TILES:
                        dve.wait_ge(S("weighted"), n - TILES + 1)
                    nc.vector.scalar_tensor_tensor(X[:, n % TILES, :], FETCHED[:, n, :], WEIGHT[:, n:n + 1],
                                                   X[:, n % TILES, :], ALU.mult, ALU.add).then_inc(S("weighted"), 1)
                dve.wait_ge(S("weighted"), 2 * TILES)
        end()

    experts("l0f", 1, int(1.25 * TOKENS * 2 / EXPERTS), False,
            [("params_b", 0, PARAMS_B), ("params_e", width(PARAMS_B), PARAMS_E)])

    B = views(PARAM, PARAMS_B)
    WKB = sb("l1a_wkb_rotated", [64, D])
    bit = Work(REGION)
    W1F, W2F = bit(DC * HID), bit(HB * D)
    SIZES = [bit(2048), bit(2048)]

    with nc.Block(no_gpsimd_drain=True) as block:
        @block.sync
        def _(sp):
            sp.dma_start(W1F, dram["bitnet"][:, 0:2048]).then_inc(S("bitnet"), 16)
            sp.dma_start(W2F, dram["bitnet"][:, 2048:4096]).then_inc(S("bitnet"), 16)

        @block.scalar
        def _(act):
            act.wait_ge(S("bitnet"), 32)
            for n, w in enumerate((W1F, W2F)):
                nc.scalar.activation(SIZES[n], w, ACT.Abs, accum_out=ABS[:, n:n + 1]).then_inc(S("abs"), 1)

        @block.tensor
        def _(pe):
            pe.wait_ge(PARAMS_LOADED, 32)
            for j in range(DC):
                for m in range(DC):
                    nc.tensor.matmul(PS[:, m * D + j * P:m * D + (j + 1) * P], B["l1a_wq"][:, j, m * P:(m + 1) * P],
                                     K["rope"][:, j, :], start=True, stop=True)
                last = nc.tensor.matmul(PS[0:64, 512 + j * P:512 + (j + 1) * P], B["l1a_wkb"][:, j, :],
                                        K["rope"][:, j, :], start=True, stop=True)
            last.then_inc(S("rotated"), 1)
            pe.wait_ge(S("abs"), 2)
            nc.tensor.matmul(PS[:, 1024:1026], K["ones"], ABS[:], start=True, stop=True).then_inc(S("abs sums"), 1)

        @block.vector
        def _(dve):
            c = Chain(dve, S("vector"))
            c.go(nc.vector.tensor_copy(IDB[:], ident))
            dve.wait_ge(S("rotated"), 1)
            c.go(nc.vector.tensor_copy(B["l1a_wq"].rearrange("p c n -> p (c n)"), PS[:, 0:2 * D]))
            c.go(nc.vector.tensor_copy(WKB[:], PS[0:64, 512:512 + D]))
            dve.wait_ge(S("abs sums"), 1)
            c.do(nc.vector.tensor_scalar(WSCALE[:], PS[:, 1024:1026], 1.0 / (D * HID), EPS, ALU.mult, ALU.max))
            c.do(nc.vector.reciprocal(RECS2[:], WSCALE[:]))
            for n, (w, q) in enumerate(((W1F, W1Q[:]), (W2F, W2Q[:]))):
                q = q.rearrange("p a b -> p (a b)")
                c.do(nc.vector.tensor_scalar(w, w, RECS2[:, n:n + 1], ROUND, ALU.mult, ALU.add))
                c.do(nc.vector.tensor_scalar(w, w, -ROUND, -1.0, ALU.add, ALU.max))
                c.do(nc.vector.tensor_scalar(q, w, 1.0, None, ALU.min))
    end()

    work = Work(REGION)
    for L in LANES:
        L.XT, L.XN, L.XNT = work(D), work(D), work(DC, P)
        L.SM, L.PR, L.PT = work(1024), work(1024), work(1024)
        L.OO, L.OT = work(512), work(512)
        L.QBD = work(32, SEQ)
        L.CTXT64, L.KT = work(DC, 2 * SEQ), work(DC, P)
        L.V64, L.KA = work(2, D, parts=64), work(2, P, parts=64)
        L.CAUSAL = work(2, SEQ)
        L.RAW_I = work(2 * SEQ).bitcast(I32)
        L.Q1, L.Q2 = L.OT[:, 0:128].bitcast(BF16), L.OO.bitcast(BF16)
        L.Q1T, L.Q2T = L.OT[:, 128:256].bitcast(BF16), L.OT.bitcast(BF16)
        L.psA16 = L.psA.bitcast(BF16)

    def quantize(L, c, x, q, back, scale):
        one = L.one
        c.do(nc.vector.tensor_reduce(one[0][:], x, AX, ALU.max, apply_absolute_value=True))
        c.do(nc.vector.tensor_scalar(one[1][:], one[0][:], EPS, None, ALU.max))
        c.do(nc.vector.reciprocal(one[2][:], one[1][:]))
        c.go(nc.vector.tensor_scalar(one[3][:], one[2][:], 127.0, None, ALU.mult))
        c.go(nc.vector.tensor_scalar(back, one[1][:], 1.0 / 127.0, scale, ALU.mult, ALU.mult))
        c.settle()
        c.do(nc.vector.tensor_scalar(x, x, one[3][:], ROUND, ALU.mult, ALU.add))
        c.do(nc.vector.tensor_scalar(x, x, -ROUND, -128.0, ALU.add, ALU.max))
        c.do(nc.vector.tensor_scalar(q, x, 127.0, None, ALU.min))

    def b_load(L, sp, t):
        sp.dma_start(L.RAW_I, stacked("mask_i", t)).then_inc(L.S("mask"), 16)
        sp.dma_start(L.CTXT64.rearrange("p c t -> p (c t)"), stacked("ctxT64", t)).then_inc(L.S("ctxT"), 16)
        sp.dma_start(L.V64.rearrange("p b d -> p (b d)"), dram["ctx64"][bass.ds(t * SEQ, SEQ), :])\
            .then_inc(L.S("ctx64"), 16)

    def b_vector(L, dve, c, t):
        fetch_tile(L, c, t)
        normed(L, c, "l1x")
        yield
        dve.wait_ge(L.S("mask"), 16)
        c.do(nc.vector.tensor_scalar(L.CAUSAL.rearrange("p b k -> p (b k)"), L.RAW_I, 1.0, FAR, ALU.is_equal, ALU.mult))
        c.do(nc.vector.tensor_tensor(L.CAUSAL, L.CAUSAL, K["causal"].unsqueeze(1).broadcast_to([P, 2, SEQ]), ALU.add))
        yield
        dve.wait_ge(L.S("l1x turned"), 1)
        head_queries(L, c, L.psA[:, 0:D].rearrange("p (c t) -> p c t", t=P), "l1x")
        yield from attention_vector(L, dve, c, "l1x", SEQ, lambda b: L.CAUSAL[:, b, :])
        yield from residual(L, dve, c, "l1x", B["l1x_b"])
        normed(L, c, "l1a")
        yield
        dve.wait_ge(L.S("l1a q"), 1)
        head_queries(L, c, L.psS[:, 0:D].rearrange("p (c t) -> p c t", t=P), "l1a")
        yield from attention_vector(L, dve, c, "l1a", SEQ, None)
        yield from residual(L, dve, c, "l1a", None)
        layer_norm(L, c, [(L.XT, L.XN)])
        layer_norm(L, c, [(L.XN, L.XN)])
        affine(c, L.XN, B["l1f_ln1_w"], B["l1f_ln1_b"])
        quantize(L, c, L.XN, L.Q1, L.one[4][:], WSCALE[:, 0:1])
        tell(L, "l1f q1")
        yield
        dve.wait_ge(L.S("l1f up"), 1)
        nc.vector.scalar_tensor_tensor(L.SM, L.psS, L.one[4][:], B["l1f_b1"], ALU.mult, ALU.add)\
            .then_inc(L.S("l1f hidden"), 1)
        yield
        dve.wait_ge(L.S("l1f gelu"), 1)
        layer_norm(L, c, [(L.PR, L.PR)])
        affine(c, L.PR, B["l1f_ln2_w"], B["l1f_ln2_b"])
        quantize(L, c, L.PR, L.Q2, L.one[5][:], WSCALE[:, 1:2])
        tell(L, "l1f q2")
        yield
        dve.wait_ge(L.S("l1f y"), 1)
        c.do(nc.vector.scalar_tensor_tensor(L.XT, L.psO[:, 0:D], L.one[5][:], L.XT, ALU.mult, ALU.add))
        c.do(nc.vector.tensor_tensor(L.XT, L.XT, B["l1f_b2"], ALU.add))
        c.do(nc.vector.tensor_copy(X[:, bass.ds(t, 1), :], L.XT.unsqueeze(1)))

    def b_scalar(L, act):
        yield from attention_scalar(L, act, "l1x", SEQ, True)
        yield from project_scalar(L, act, "l1x", 2)
        yield from transpose_x_scalar(L, act, "l1a")
        yield
        act.wait_ge(L.S("l1a latent"), 1)
        nc.scalar.copy(L.KA.rearrange("p c t -> p (c t)"), L.psO[0:64, 0:256]).then_inc(L.S("l1a latents"), 1)
        yield
        act.wait_ge(L.S("l1a kv"), 1)
        nc.scalar.copy(L.KT.rearrange("p c t -> p (c t)"), L.psS[:, 512:768]).then_inc(L.S("l1a kvs"), 1)
        nc.scalar.copy(L.V64.rearrange("p b d -> p (b d)"), L.psA[0:64, :]).then_inc(L.S("l1a kvs"), 1)
        yield from attention_scalar(L, act, "l1a", SEQ, None)
        yield from project_scalar(L, act, "l1a", 2)
        yield
        act.wait_ge(L.S("l1f q1 turned"), 1)
        nc.scalar.copy(L.Q1T, L.psA16[:, 0:256]).then_inc(L.S("l1f q1T"), 1)
        yield
        act.wait_ge(L.S("l1f hidden"), 1)
        nc.scalar.activation(L.PR, L.SM, ACT.Gelu).then_inc(L.S("l1f gelu"), 1)
        yield
        act.wait_ge(L.S("l1f q2 turned"), 1)
        nc.scalar.copy(L.Q2T, L.psA16).then_inc(L.S("l1f q2T"), 1)

    def b_tensor(L, pe):
        yield from transpose_x_tensor(L, pe, "l1x")
        value = lambda b, c, p, s: L.V64[:, b, column16(p, s):column16(p, s) + DH]
        yield from attention_tensor(L, pe, "l1x", SEQ, DH, masked_query(L),
                                    lambda b, p: L.CTXT64[:, p // 4, SEQ * b:SEQ * (b + 1)], value, column16,
                                    [("ctxT", 16), ("ctx64", 16), ("l1x queries", 1)])
        yield from project_tensor(L, pe, "l1x", B["l1x_w"])
        yield from transpose_x_tensor(L, pe, "l1a")
        yield
        pe.wait_ge(L.S("l1a xnT"), 1)
        for j in range(DC):
            last = product(L.psS[:, j * P:(j + 1) * P], lambda i: B["l1a_wq"][:, i, j * P:(j + 1) * P],
                           lambda i: L.XNT[:, i, :], DC)
        last.then_inc(L.S("l1a q"), 1)
        for j, w in enumerate(("l1a_wka", "l1a_wva")):
            last = product(L.psO[0:64, j * P:(j + 1) * P], lambda i: B[w][:, i, :], lambda i: L.XNT[:, i, :], DC)
        last.then_inc(L.S("l1a latent"), 1)
        yield
        pe.wait_ge(L.S("l1a latents"), 1)
        for j in range(DC):
            nc.tensor.matmul(L.psS[:, 512 + j * P:512 + (j + 1) * P], WKB[:, j * P:(j + 1) * P], L.KA[:, 0, :],
                             start=True, stop=True)
        for b in range(2):
            last = nc.tensor.matmul(L.psA[0:64, D * b:D * (b + 1)], L.KA[:, 1, SEQ * b:SEQ * (b + 1)], B["l1a_wvb"],
                                    start=True, stop=True)
        last.then_inc(L.S("l1a kv"), 1)
        yield from attention_tensor(L, pe, "l1a", SEQ, DH, masked_query(L),
                                    lambda b, p: L.KT[:, p // 4, SEQ * b:SEQ * (b + 1)], value, column16,
                                    [("l1a kvs", 2), ("l1a queries", 1)])
        yield from project_tensor(L, pe, "l1a", B["l1a_wo"])
        yield
        pe.wait_ge(L.S("l1f q1"), 1)
        for i in range(DC):
            last = nc.tensor.transpose(L.psA16[:, i * P:(i + 1) * P], L.Q1[:, i * P:(i + 1) * P], IDB[:])
        last.then_inc(L.S("l1f q1 turned"), 1)
        yield
        pe.wait_ge(L.S("l1f q1T"), 1)
        for j in range(2):
            last = product(L.psS[:, j * 512:(j + 1) * 512], lambda i: L.Q1T[:, i * P:(i + 1) * P],
                           lambda i: W1Q[:, i, j * 512:(j + 1) * 512], DC)
        last.then_inc(L.S("l1f up"), 1)
        yield
        pe.wait_ge(L.S("l1f q2"), 1)
        for i in range(HB):
            last = nc.tensor.transpose(L.psA16[:, i * P:(i + 1) * P], L.Q2[:, i * P:(i + 1) * P], IDB[:])
        last.then_inc(L.S("l1f q2 turned"), 1)
        yield
        pe.wait_ge(L.S("l1f q2T"), 1)
        product(L.psO[:, 0:D], lambda i: L.Q2T[:, i * P:(i + 1) * P], lambda i: W2Q[:, i, :], HB)\
            .then_inc(L.S("l1f y"), 1)

    with nc.Fori(0, TILES // 2) as i:
        lanes_block(i, b_load, b_vector, b_scalar, b_tensor)

    E = views(PARAM[:, width(PARAMS_B):], PARAMS_E)
    E.update(views(PARAM, PARAMS_E_LATE))
    work = Work(REGION)
    for L in LANES:
        L.XT, L.XN, L.XNT = work(D), work(D), work(DC, P)
        L.SM, L.PR, L.PT = work(1024), work(1024), work(1024)
        L.OO, L.OT = work(D), work(D)
        L.QBD = work(32, SEQ)
        L.CTXT, L.KT, L.V = work(DC, 512), work(DC, 512), work(4, D)
        L.QF = work(DC, P)
        L.KEYMASK = work(2, KEYS)
        L.RAW_B = work(2 * KEYS // 4).bitcast(dram["mask_b"].dtype)

    with nc.Block(no_gpsimd_drain=True) as block:
        @block.sync
        def _(sp):
            sp.dma_start(PARAM[:, 0:width(PARAMS_E_LATE)], dram["params_e_late"]).then_inc(S("late params"), 16)
            sp.wait_ge(S("late params"), 16)
    end()

    def e_load(L, sp, t):
        sp.dma_start(L.CTXT.rearrange("p c t -> p (c t)"), stacked("ctxT", t)).then_inc(L.S("ctxT"), 16)
        sp.dma_start(L.RAW_B, stacked("mask_b", t)).then_inc(L.S("mask"), 16)

    def e_vector(L, dve, c, t):
        fetch_tile(L, c, t)
        normed(L, c, "l2x")
        yield
        dve.wait_ge(L.S("mask"), 16)
        c.do(nc.vector.tensor_scalar(L.KEYMASK.rearrange("p b k -> p (b k)"), L.RAW_B, -1e9, None, ALU.mult))
        yield
        dve.wait_ge(L.S("l2x v"), 1)
        for j, ps in enumerate((L.psA, L.psO)):
            nc.vector.tensor_tensor(L.V[:, 2 * j:2 * j + 2, :], ps.rearrange("p (j d) -> p j d", d=D),
                                    E["l2x_bv"].unsqueeze(1).broadcast_to([P, 2, D]), ALU.add)\
                .then_inc(L.S("l2x vs"), 1)
        yield
        dve.wait_ge(L.S("l2x qT"), 2)
        head_queries(L, c, L.QF, "l2x")
        yield from attention_vector(L, dve, c, "l2x", KEYS, lambda b: L.KEYMASK[:, b, :])
        yield from residual(L, dve, c, "l2x", E["l2x_bo"])
        normed(L, c, "l2a")
        yield
        dve.wait_ge(L.S("l2a squares"), 3)
        c.do(nc.vector.tensor_tensor(L.one[0][:], L.one[1][:], L.one[2][:], ALU.add))
        c.do(nc.vector.tensor_tensor(L.one[0][:], L.one[0][:], L.one[3][:], ALU.add))
        rstd_of(L, c, 1, L.one[0][:], 0.0)
        nc.vector.tensor_scalar(L.one[4][:], L.rstd[:, 0:1], 2048.0 ** 0.5, None, ALU.mult)\
            .then_inc(L.S("l2a norm"), 1)
        yield from residual(L, dve, c, "l2a", None)
        yield from to_experts_vector(L, dve, c, t)

    def e_scalar(L, act):
        yield
        act.wait_ge(L.S("l2x k"), 1)
        for i in range(DC):
            nc.scalar.activation(L.KT[:, i, :], L.psS[:, i * 512:(i + 1) * 512], ACT.Identity,
                                 bias=E["l2x_bk"][:, i:i + 1]).then_inc(L.S("l2x ks"), 1)
        yield from transpose_x_scalar(L, act, "l2x")
        yield
        act.wait_ge(L.S("l2x q"), 1)
        for i in range(DC):
            nc.scalar.activation(L.QF[:, i, :], L.psS[:, i * P:(i + 1) * P], ACT.Identity,
                                 bias=E["l2x_bq"][:, i:i + 1]).then_inc(L.S("l2x qT"), 1)
        yield from attention_scalar(L, act, "l2x", KEYS, True)
        yield from project_scalar(L, act, "l2x", 4)
        yield from transpose_x_scalar(L, act, "l2a")
        yield
        act.wait_ge(L.S("l2a scores"), 1)
        nc.scalar.activation(L.PT, L.psS, ACT.Square, accum_out=L.one[1][:]).then_inc(L.S("l2a squares"), 1)
        nc.scalar.activation(L.SM[:, 0:512], L.psA, ACT.Square, accum_out=L.one[2][:]).then_inc(L.S("l2a squares"), 1)
        nc.scalar.activation(L.SM[:, 512:1024], L.psO, ACT.Square, accum_out=L.one[3][:])\
            .then_inc(L.S("l2a squares"), 1)
        yield
        act.wait_ge(L.S("l2a norm"), 1)
        nc.scalar.activation(L.PR, L.psS, ACT.Gelu, scale=L.one[4][:]).then_inc(L.S("l2a gelu"), 1)
        nc.scalar.activation(L.SM[:, 0:512], L.psA, ACT.Gelu, scale=L.one[4][:]).then_inc(L.S("l2a gelu"), 1)
        nc.scalar.activation(L.SM[:, 512:1024], L.psO, ACT.Gelu, scale=L.one[4][:]).then_inc(L.S("l2a gelu"), 1)
        for h in range(2):
            yield
            act.wait_ge(L.S("l2a gelu turned"), h + 1)
            if h:
                act.wait_ge(L.S("l2a half"), 1)
            nc.scalar.copy(L.PT, L.psS).then_inc(L.S("l2a gT"), 1)

    def e_tensor(L, pe):
        pe.wait_ge(L.S("ctxT"), 16)
        for j in range(DC):
            last = product(L.psS[:, j * 512:(j + 1) * 512], lambda i: E["l2x_wk"][:, i, j * P:(j + 1) * P],
                           lambda i: L.CTXT[:, i, :], DC)
        last.then_inc(L.S("l2x k"), 1)
        for j in range(4):
            ps = (L.psA, L.psO)[j // 2]
            last = product(ps[:, j % 2 * D:(j % 2 + 1) * D], lambda i: L.CTXT[:, i, j * P:(j + 1) * P],
                           lambda i: E["l2x_wv"][:, i, :], DC)
        last.then_inc(L.S("l2x v"), 1)
        yield
        pe.wait_ge(L.S("l2x vs"), 2)
        yield from transpose_x_tensor(L, pe, "l2x")
        yield
        pe.wait_ge(L.S("l2x xnT"), 1)
        pe.wait_ge(L.S("l2x ks"), 2)
        for j in range(DC):
            last = product(L.psS[:, j * P:(j + 1) * P], lambda i: E["l2x_wq"][:, i, j * P:(j + 1) * P],
                           lambda i: L.XNT[:, i, :], DC)
        last.then_inc(L.S("l2x q"), 1)
        yield from attention_tensor(
            L, pe, "l2x", KEYS, DH, masked_query(L), lambda b, p: L.KT[:, p // 4, KEYS * b:KEYS * (b + 1)],
            lambda b, c, p, s: L.V[:, 2 * b + c, column16(p, s):column16(p, s) + DH], column16,
            [("l2x queries", 1)])
        yield from project_tensor(L, pe, "l2x", E["l2x_wo"])
        yield from transpose_x_tensor(L, pe, "l2a")
        yield
        pe.wait_ge(L.S("l2a xnT"), 1)
        for j, ps in enumerate((L.psS[:, 0:512], L.psS[:, 512:1024], L.psA, L.psO)):
            last = product(ps, lambda i: L.XNT[:, i, :], lambda i: E["l2a_k"][:, i, j * 512:(j + 1) * 512], DC)
        last.then_inc(L.S("l2a scores"), 1)
        yield
        pe.wait_ge(L.S("l2a gelu"), 3)
        for h, g in enumerate((L.PR, L.SM)):
            for i in range(8):
                last = nc.tensor.transpose(L.psS[:, i * P:(i + 1) * P], g[:, i * P:(i + 1) * P], ident)
            last.then_inc(L.S("l2a gelu turned"), 1)
            yield
            pe.wait_ge(L.S("l2a gT"), h + 1)
            last = product(L.psA[:, 0:D], lambda i: L.PT[:, i * P:(i + 1) * P], lambda i: E["l2a_v"][:, 8 * h + i, :], 8,
                           first=(h == 0), last_=(h == 1))
            last.then_inc(L.S("l2a y" if h else "l2a half"), 1)
        yield from transpose_x_tensor(L, pe, "router")

    with nc.Fori(0, TILES // 2) as i:
        lanes_block(i, e_load, e_vector, e_scalar, e_tensor)

    experts("l2f", 2, None, False, [("params_c", 0, PARAMS_C)])

    C = views(PARAM, PARAMS_C)
    work = Work(REGION)
    for L in LANES:
        L.XT, L.XN, L.XNT = work(D), work(D), work(DC, P)
        L.PR, L.PT = work(KEYS), work(KEYS)
        L.OO, L.OT = work(64), work(P, parts=64)
        L.CTXT, L.KT, L.V = work(DC, 512), work(512, parts=64), work(4, 64)
        L.QT = work(P, parts=64)
        L.H, L.QKT, L.MIXED = work(P, parts=64), work(2, P, parts=64), work(2, SEQ, parts=64)
        L.POOLED, L.POOLED_T = work(8, parts=64), work(8, CHUNK, parts=64)
        L.VB, L.PICKED, L.ACTIVE, L.GATED = work(2, SEQ, parts=64), work(P, parts=64), work(P, parts=64), work(P, parts=64)
        L.DELTA, L.PICKS_T, L.HALF_BH = work(P, parts=64), work(P, parts=64), work(1, parts=64)
        L.SCORES, L.REST, L.WEIGHT, L.TOP8 = work(SEQ), work(SEQ), work(SEQ), work(8)

    def c_load(L, sp, t):
        sp.dma_start(L.CTXT.rearrange("p c t -> p (c t)"), stacked("ctxT", t)).then_inc(L.S("ctxT"), 16)

    def c_vector(L, dve, c, t):
        one = L.one
        fetch_tile(L, c, t)
        normed(L, c, "l3x")
        c.do(nc.vector.tensor_scalar(L.HALF_BH, C["l3a_bh"], 0.5, None, ALU.mult))
        yield
        dve.wait_ge(L.S("l3x v"), 1)
        nc.vector.tensor_tensor(L.V, L.psS[:, 0:256].rearrange("p (j d) -> p j d", d=64),
                                C["l3x_bq"].unsqueeze(1).broadcast_to([P, 4, 64]), ALU.add)\
            .then_inc(L.S("l3x vs"), 1)
        yield
        dve.wait_ge(L.S("l3x scores"), 1)
        c.do(nc.vector.tensor_reduce(one[0][:], L.psS[:, 512:512 + KEYS], AX, ALU.max))
        nc.vector.tensor_scalar(one[1][:], one[0][:], -(D ** -0.5), None, ALU.mult).then_inc(L.S("l3x max"), 1)
        yield
        dve.wait_ge(L.S("l3x exp"), 1)
        c.do(nc.vector.reciprocal(one[3][:], one[2][:]))
        nc.vector.tensor_scalar(L.PR, L.PR, one[3][:], None, ALU.mult).then_inc(L.S("l3x probs"), 1)
        yield from residual(L, dve, c, "l3x", C["l3x_bo"])
        normed(L, c, "l3a")
        for step in range(2):
            yield
            if step == 0:
                dve.wait_ge(L.S("l3a h"), 1)
            hb = L.H.rearrange("p (b s) -> p b s", s=SEQ)
            c.do(nc.vector.tensor_reduce(L.POOLED, L.H.rearrange("p (g s) -> p g s", s=CHUNK), AX, ALU.add))
            nc.vector.tensor_scalar(L.POOLED, L.POOLED, 1.0 / CHUNK, None, ALU.mult).then_inc(L.S("l3a pooled"), 1)
            c.do(nc.vector.tensor_scalar(L.MIXED.rearrange("p b s -> p (b s)"), L.H,
                                         C["l3a_conv"][:, KSIZE - 1:KSIZE], C["l3a_convb"], ALU.mult, ALU.add))
            for back in range(1, KSIZE):
                c.do(nc.vector.scalar_tensor_tensor(
                    L.MIXED[:, :, back:SEQ], hb[:, :, 0:SEQ - back],
                    C["l3a_conv"][:, KSIZE - 1 - back:KSIZE - back], L.MIXED[:, :, back:SEQ], ALU.mult, ALU.add))
            yield
            dve.wait_ge(L.S("l3a scores"), step + 1)
            c.do(nc.vector.scalar_tensor_tensor(L.SCORES, L.psS[:, 0:SEQ], STATE ** -0.5, K["strict"],
                                                ALU.mult, ALU.add))
            c.do(nc.vector.max(L.TOP8, L.SCORES))
            nc.vector.tensor_scalar(one[0][:], L.TOP8[:, 0:1], FAR / 10, -1.0, ALU.max, ALU.mult)\
                .then_inc(L.S("l3a max"), 1)
            c.do(nc.vector.match_replace(L.REST, L.TOP8, L.SCORES, TAKEN))
            c.do(nc.vector.tensor_scalar(L.REST, L.REST, TAKEN / 10, None, ALU.is_lt))
            dve.wait_ge(L.S("l3a pool product"), step + 1)
            c.go(nc.vector.tensor_scalar(L.POOLED_T, L.psS[0:64, 512:520].unsqueeze(2).broadcast_to([64, 8, CHUNK]),
                                         C["l3a_bp"], None, ALU.add))
            for b in range(2):
                c.go(nc.vector.tensor_tensor(L.VB[:, b, :], L.psA[0:64, 64 * b:64 * b + 64], C["l3a_bv"], ALU.add))
            c.settle()
            tell(L, "l3a inputs")
            yield
            dve.wait_ge(L.S("l3a exp"), step + 1)
            c.do(nc.vector.tensor_tensor(L.WEIGHT, L.WEIGHT, L.REST, ALU.mult))
            c.do(nc.vector.tensor_reduce(one[1][:], L.WEIGHT, AX, ALU.add))
            c.do(nc.vector.tensor_scalar(one[2][:], one[1][:], 1e-30, None, ALU.max))
            c.do(nc.vector.reciprocal(one[3][:], one[2][:]))
            nc.vector.tensor_scalar(L.WEIGHT, L.WEIGHT, one[3][:], None, ALU.mult).then_inc(L.S("l3a weights"), 1)
            yield
            dve.wait_ge(L.S("l3a gate"), step + 1)
            c.do(nc.vector.tensor_scalar(L.GATED, L.GATED, 0.5, 0.5, ALU.mult, ALU.add))
            dve.wait_ge(L.S("l3a delta"), step + 1)
            c.do(nc.vector.scalar_tensor_tensor(L.DELTA, L.psA[0:64, 256:256 + P], C["l3a_b2"], L.GATED,
                                                ALU.add, ALU.mult))
            nc.vector.tensor_tensor(L.H, L.H, L.DELTA, ALU.add).then_inc(L.S("l3a updated"), 1)
            dve.wait_ge(L.S("l3a updated"), step + 1)
        c.do(nc.vector.tensor_tensor(L.XT, L.XT, L.XN, ALU.add))
        yield from residual(L, dve, c, "l3a", C["l3a_bo"])
        yield from to_experts_vector(L, dve, c, t)

    def c_scalar(L, act):
        yield
        act.wait_ge(L.S("l3x k"), 1)
        nc.scalar.activation(L.KT, L.psA[0:64, :], ACT.Identity, bias=C["l3x_bqc"]).then_inc(L.S("l3x ks"), 1)
        yield from transpose_x_scalar(L, act, "l3x")
        yield
        act.wait_ge(L.S("l3x q"), 1)
        nc.scalar.activation(L.QT, L.psO[0:64, 0:P], ACT.Identity, bias=C["l3x_bqc"]).then_inc(L.S("l3x qT"), 1)
        yield
        act.wait_ge(L.S("l3x max"), 1)
        nc.scalar.activation(L.PR, L.psS[:, 512:512 + KEYS], ACT.Exp, bias=L.one[1][:], scale=D ** -0.5,
                             accum_out=L.one[2][:]).then_inc(L.S("l3x exp"), 1)
        yield
        act.wait_ge(L.S("l3x probs turned"), 1)
        nc.scalar.copy(L.PT, L.psA[:, 0:2 * P]).then_inc(L.S("l3x probsT"), 1)
        yield
        act.wait_ge(L.S("l3x mixed"), 1)
        nc.scalar.copy(L.OO, L.psO[:, 0:64]).then_inc(L.S("l3x o"), 1)
        yield
        act.wait_ge(L.S("l3x o turned"), 1)
        nc.scalar.copy(L.OT, L.psS[0:64, 0:P]).then_inc(L.S("l3x oT"), 1)
        yield from transpose_x_scalar(L, act, "l3a")
        yield
        act.wait_ge(L.S("l3a input product"), 1)
        nc.scalar.activation(L.H, L.psO[0:64, 0:P], ACT.Identity, bias=C["l3a_bi"]).then_inc(L.S("l3a h"), 1)
        for step in range(2):
            yield
            act.wait_ge(L.S("l3a qk"), step + 1)
            for j, bias in enumerate(("l3a_bq", "l3a_bk")):
                nc.scalar.activation(L.QKT[:, j, :], L.psO[0:64, j * P:(j + 1) * P], ACT.Identity, bias=C[bias])\
                    .then_inc(L.S("l3a qks"), 1)
            nc.scalar.activation(L.GATED, L.psO[0:64, 2 * P:3 * P], ACT.Tanh, scale=0.5, bias=L.HALF_BH)\
                .then_inc(L.S("l3a gate"), 1)
            yield
            act.wait_ge(L.S("l3a max"), step + 1)
            nc.scalar.activation(L.WEIGHT, L.SCORES, ACT.Exp, bias=L.one[0][:]).then_inc(L.S("l3a exp"), 1)
            yield
            act.wait_ge(L.S("l3a weights turned"), step + 1)
            nc.scalar.copy(L.PICKS_T, L.psS[0:64, 512:512 + P]).then_inc(L.S("l3a weightsT"), 1)
            yield
            act.wait_ge(L.S("l3a summed"), step + 1)
            nc.scalar.copy(L.PICKED, L.psO[0:64, 0:P]).then_inc(L.S("l3a picked"), 1)
            yield
            act.wait_ge(L.S("l3a up"), step + 1)
            nc.scalar.activation(L.ACTIVE, L.psS[0:64, 0:P], ACT.Tanh, bias=C["l3a_b1"]).then_inc(L.S("l3a tanh"), 1)

    def c_tensor(L, pe):
        pe.wait_ge(L.S("ctxT"), 16)
        product(L.psA[0:64, :], lambda i: C["l3x_wq"][:, i, :], lambda i: L.CTXT[:, i, :], DC)\
            .then_inc(L.S("l3x k"), 1)
        for j in range(4):
            last = product(L.psS[:, 64 * j:64 * j + 64], lambda i: L.CTXT[:, i, j * P:(j + 1) * P],
                           lambda i: C["l3x_wq"][:, i, :], DC)
        last.then_inc(L.S("l3x v"), 1)
        yield
        pe.wait_ge(L.S("l3x ks"), 1)
        yield from transpose_x_tensor(L, pe, "l3x")
        yield
        pe.wait_ge(L.S("l3x xnT"), 1)
        product(L.psO[0:64, 0:P], lambda i: C["l3x_wq"][:, i, :], lambda i: L.XNT[:, i, :], DC)\
            .then_inc(L.S("l3x q"), 1)
        yield
        pe.wait_ge(L.S("l3x qT"), 1)
        for b in range(2):
            last = nc.tensor.matmul(L.psS[64 * b:64 * b + 64, 512:512 + KEYS], L.QT[:, 64 * b:64 * b + 64],
                                    L.KT[:, KEYS * b:KEYS * (b + 1)], start=True, stop=True)
        last.then_inc(L.S("l3x scores"), 1)
        yield
        pe.wait_ge(L.S("l3x probs"), 1)
        for i in range(2):
            last = nc.tensor.transpose(L.psA[:, i * P:(i + 1) * P], L.PR[:, i * P:(i + 1) * P], ident)
        last.then_inc(L.S("l3x probs turned"), 1)
        yield
        pe.wait_ge(L.S("l3x probsT"), 1)
        pe.wait_ge(L.S("l3x vs"), 1)
        for b in range(2):
            last = product(L.psO[64 * b:64 * b + 64, 0:64], lambda i: L.PT[:, i * P + 64 * b:i * P + 64 * b + 64],
                           lambda i: L.V[:, 2 * b + i, :], 2)
        last.then_inc(L.S("l3x mixed"), 1)
        yield
        pe.wait_ge(L.S("l3x o"), 1)
        nc.tensor.transpose(L.psS[0:64, 0:P], L.OO, ident).then_inc(L.S("l3x o turned"), 1)
        yield
        pe.wait_ge(L.S("l3x oT"), 1)
        nc.tensor.matmul(L.psA[:, 0:D], L.OT, C["l3x_wo"], start=True, stop=True).then_inc(L.S("l3x y"), 1)
        yield from transpose_x_tensor(L, pe, "l3a")
        yield
        pe.wait_ge(L.S("l3a xnT"), 1)
        product(L.psO[0:64, 0:P], lambda i: C["l3a_wi"][:, i, :], lambda i: L.XNT[:, i, :], DC)\
            .then_inc(L.S("l3a input product"), 1)
        for step in range(2):
            yield
            if step == 0:
                pe.wait_ge(L.S("l3a h"), 1)
            else:
                pe.wait_ge(L.S("l3a updated"), 1)
            nc.tensor.matmul(L.psO[0:64, 0:P], C["l3a_wq"], L.H, start=True, stop=True)
            nc.tensor.matmul(L.psO[0:64, P:2 * P], C["l3a_wk"], L.H, start=True, stop=True)
            nc.tensor.matmul(L.psO[0:64, 2 * P:3 * P], C["l3a_wh"], L.H, start=True, stop=True)\
                .then_inc(L.S("l3a qk"), 1)
            for b in range(2):
                nc.tensor.matmul(L.psA[0:64, 64 * b:64 * b + 64], L.H[:, 64 * b:64 * b + 64], C["l3a_wv"],
                                 start=True, stop=True)
            pe.wait_ge(L.S("l3a pooled"), step + 1)
            nc.tensor.matmul(L.psS[0:64, 512:520], C["l3a_wp"], L.POOLED, start=True, stop=True)\
                .then_inc(L.S("l3a pool product"), 1)
            yield
            pe.wait_ge(L.S("l3a qks"), 2 * step + 2)
            for b in range(2):
                last = nc.tensor.matmul(L.psS[64 * b:64 * b + 64, 0:SEQ], L.QKT[:, 0, 64 * b:64 * b + 64],
                                        L.QKT[:, 1, 64 * b:64 * b + 64], start=True, stop=True)
            last.then_inc(L.S("l3a scores"), 1)
            yield
            pe.wait_ge(L.S("l3a weights"), step + 1)
            nc.tensor.transpose(L.psS[0:64, 512:512 + P], L.WEIGHT, ident).then_inc(L.S("l3a weights turned"), 1)
            yield
            pe.wait_ge(L.S("l3a weightsT"), step + 1)
            pe.wait_ge(L.S("l3a inputs"), step + 1)
            pe.wait_ge(L.S("l3a gate"), step + 1)
            for b in range(2):
                last = nc.tensor.matmul(L.psO[0:64, 64 * b:64 * b + 64], L.VB[:, b, :], L.PICKS_T[:, 64 * b:64 * b + 64],
                                        start=True, stop=True)
            last.then_inc(L.S("l3a summed"), 1)
            yield
            pe.wait_ge(L.S("l3a picked"), step + 1)
            parts = [L.H, L.MIXED.rearrange("p b s -> p (b s)"), L.POOLED_T.rearrange("p g s -> p (g s)"), L.PICKED]
            product(L.psS[0:64, 0:P], lambda i: C["l3a_w1"][:, i, :], lambda i: parts[i], 4)\
                .then_inc(L.S("l3a up"), 1)
            yield
            pe.wait_ge(L.S("l3a tanh"), step + 1)
            nc.tensor.matmul(L.psA[0:64, 256:256 + P], C["l3a_w2"], L.ACTIVE, start=True, stop=True)\
                .then_inc(L.S("l3a delta"), 1)
        yield
        pe.wait_ge(L.S("l3a updated"), 2)
        nc.tensor.matmul(L.psA[:, 0:D], L.H, C["l3a_wo"], start=True, stop=True).then_inc(L.S("l3a y"), 1)
        yield from transpose_x_tensor(L, pe, "router")

    with nc.Block(no_gpsimd_drain=True) as block:
        @block.sync
        def _(sp):
            sp.wait_ge(PARAMS_LOADED, 48)
    end()

    with nc.Fori(0, TILES // 2) as i:
        lanes_block(i, c_load, c_vector, c_scalar, c_tensor)

    experts("l3f", 3, int(round(2 * TOKENS * 1.05 / EXPERTS)), True, [])

    with nc.Block(no_gpsimd_drain=True) as block:
        @block.sync
        def _(sp):
            sp.dma_start(out, X[:]).then_inc(S("stored"), 16)
            sp.wait_ge(S("stored"), 16)


def kernel(**inputs):
    import numpy as np
    import concourse.bacc as bacc
    from concourse.bass_utils import run_bass_kernel_spmd as run

    f = {k: np.asarray(v) for k, v in inputs.items()}

    def rows(w):
        return w.reshape(-1, P, w.shape[1]).transpose(1, 0, 2)

    def bcast(b):
        return np.broadcast_to(b.reshape(1, -1), (P, b.size))

    def cols(b):
        return b.reshape(-1, P).T

    def col(b):
        return b.reshape(-1, 1)

    r = np.arange(P)
    seq = r % SEQ
    inv = 1.0 / 10000.0 ** (np.arange(0, DH, 2, dtype=np.float32) / np.float32(DH))
    angle = np.arange(HEADS, dtype=np.float32)[:, None] * inv[None, :].astype(np.float32)
    rope = np.zeros((D, D), np.float32)
    for h in range(HEADS):
        for j in range(DH // 2):
            a, b = h * DH + 2 * j, h * DH + 2 * j + 1
            cos, sin = np.cos(angle[h, j]), np.sin(angle[h, j])
            rope[a, a], rope[b, a], rope[a, b], rope[b, b] = cos, -sin, sin, cos
    consts = {
        "ident": np.eye(P), "tri": r[:, None] <= r[None, :], "ones": np.ones((P, P)),
        "batch_ones": r[:, None] // SEQ == r[None, :] // SEQ,
        "headmask": (r[:, None] // DH == np.arange(8)[None, :]) * 0.25,
        "causal": np.where(np.arange(SEQ)[None, :] > seq[:, None], FAR, 0.0),
        "strict": np.where(np.arange(SEQ)[None, :] >= seq[:, None], FAR, 0.0),
        "experts": bcast(np.arange(EXPERTS)),
        "blocks": bcast(np.arange(FREE_BLOCKS)),
        "spill": SLOTS + np.arange(2 * TILES)[None, :] * P + r[:, None],
        "rope": np.stack([rope[i * P:(i + 1) * P, i * P:(i + 1) * P] for i in range(DC)], 1),
    }
    g = lambda layer: {k[len(layer) + 1:]: v for k, v in f.items() if k.startswith(layer + "_")}
    x0, a0, x1, a1, f1 = g("L0_xattn"), g("L0_attn"), g("L1_xattn"), g("L1_attn"), g("L1_ffn")
    x2, a2, x3, a3 = g("L2_xattn"), g("L2_attn"), g("L3_xattn"), g("L3_attn")
    wk, wv = x0["Wkv"][:, :64], x0["Wkv"][:, 64:]
    wout = x0["Wout"].reshape(4, 2, 2, 64, D).transpose(2, 0, 1, 3, 4).reshape(8, P, D).transpose(1, 0, 2)
    params_a = {
        "l0x_wk": rows(np.concatenate([wk, wk], 1)), "l0x_wv": rows(wv), "l0x_wq": rows(x0["Wq"]),
        "l0x_w1": rows(x0["W1"].reshape(D, 2, 2, 512).transpose(0, 2, 1, 3).reshape(D, 2048)), "l0x_wout": wout, "l0x_w2": rows(x0["W2"]),
        "l0x_ln_g": bcast(x0["ln_g"]), "l0x_ln_b": bcast(x0["ln_b"]),
        "l0x_cln_g": bcast(x0["cln_g"]), "l0x_cln_b": bcast(x0["cln_b"]),
        "l0a_wqkv": rows(a0["w_qkv"].T), "l0a_wfc": rows(a0["w_fc"].T), "l0a_bfc": bcast(a0["b_fc"]),
        "l0a_gamma": bcast(a0["gamma"]), "l0a_beta": bcast(a0["beta"]),
    }
    params_b = {
        "l1x_w": rows(x1["W"].T), "l1x_b": bcast(x1["b"]),
        "l1a_wq": rows(a1["wq"]), "l1a_wka": rows(a1["wk_a"].T), "l1a_wkb": rows(a1["wk_b"]),
        "l1a_wva": rows(a1["wv_a"].T), "l1a_wvb": a1["wv_b"].T, "l1a_wo": rows(a1["wo"].T),
        "l1f_ln1_w": bcast(f1["ln1_w"]), "l1f_ln1_b": bcast(f1["ln1_b"]), "l1f_b1": bcast(f1["b1"]),
        "l1f_ln2_w": bcast(f1["ln2_w"]), "l1f_ln2_b": bcast(f1["ln2_b"]), "l1f_b2": bcast(f1["b2"]),
    }
    params_e = {
        "l2x_wq": rows(x2["Wq"].T), "l2x_wk": rows(x2["Wk"].T), "l2x_wv": rows(x2["Wv"].T),
        "l2x_wo": rows(x2["Wo"].T), "l2x_bq": cols(x2["bq"]), "l2x_bk": cols(x2["bk"]),
        "l2x_bv": bcast(x2["bv"]), "l2x_bo": bcast(x2["bo"]),
        "l2a_k": rows(a2["k"].T), "l2a_v": rows(a2["v"]),
    }
    bitnet = {"l1f_w1": rows(f1["w1"].T), "l1f_w2": rows(f1["w2"].T)}
    params_c = {
        "l3x_wq": rows(x3["Wq"]), "l3x_bq": bcast(x3["bq"]), "l3x_bqc": col(x3["bq"]), "l3x_wo": x3["Wo"],
        "l3x_bo": bcast(x3["bo"]), "l3a_wi": rows(a3["Wi"]), "l3a_bi": col(a3["bi"]), "l3a_conv": a3["conv_w"].T,
        "l3a_convb": col(a3["conv_b"]), "l3a_wp": a3["Wp"], "l3a_bp": col(a3["bp"]),
        "l3a_wh": np.broadcast_to(a3["Wh"][:, 2:3], (64, 64)), "l3a_bh": np.broadcast_to(a3["bh"][2:3], (64,)).reshape(64, 1),
        "l3a_wq": a3["Wq"], "l3a_bq": col(a3["bq"]), "l3a_wk": a3["Wk"], "l3a_bk": col(a3["bk"]),
        "l3a_wv": a3["Wv"], "l3a_bv": bcast(a3["bv"])[:64], "l3a_w1": a3["W1"].reshape(4, 64, 64).transpose(1, 0, 2),
        "l3a_b1": col(a3["b1"]), "l3a_w2": a3["W2"], "l3a_b2": col(a3["b2"]), "l3a_wo": a3["Wo"], "l3a_bo": bcast(a3["bo"]),
    }

    def pack(params, given):
        parts = []
        for name, n, shape in params:
            a = np.asarray(given[name])
            assert a.shape == (n, *shape), (name, a.shape)
            a = a.reshape(n, -1).astype(np.float32)
            parts.append(np.concatenate([a, np.zeros((P - n, a.shape[1]), np.float32)], 0))
        return np.concatenate(parts, 1)

    def experts(w1, b1, w2, b2):
        parts = [w1.reshape(EXPERTS, DC, P, HID).transpose(0, 2, 1, 3), w2.reshape(EXPERTS, HB, P, D).transpose(0, 2, 1, 3),
                 b1.reshape(EXPERTS, HB, P).transpose(0, 2, 1), np.broadcast_to(b2.reshape(EXPERTS, 1, D), (EXPERTS, P, D))]
        return np.concatenate([a.reshape(EXPERTS, P, -1) for a in parts], 2)

    f0, f2, f3 = g("L0_ffn"), g("L2_ffn"), g("L3_ffn")
    ctx = f["ctx_1024"]
    mask_f = f["mask_BxSxS2_ff0"].reshape(TILES, 2, SEQ, KEYS).transpose(0, 2, 1, 3)
    mask_i = f["mask_BxS2_if0"].reshape(TILES, 1, 2, KEYS)[:, :, :, :SEQ]
    mask_b = f["mask_BxS2_bf0"].reshape(TILES, 1, 2, KEYS)
    arrays = {
        "x": f["x"].reshape(TILES, P, D).transpose(1, 0, 2),
        "consts": pack(CONSTS, consts), "params_a": pack(PARAMS_A, params_a), "params_b": pack(PARAMS_B, params_b),
        "params_e": pack(PARAMS_E, params_e), "params_e_late": pack(PARAMS_E_LATE, params_e),
        "params_c": pack(PARAMS_C, params_c), "bitnet": pack(BITNET, bitnet),
        "ctx": ctx.reshape(TILES, 4, P, D).transpose(0, 2, 1, 3),
        "ctx64": ctx[:, :SEQ].reshape(TILES, 2, SEQ, D).transpose(0, 2, 1, 3),
        "ctxT64": ctx[:, :SEQ].reshape(TILES, 2 * SEQ, DC, P).transpose(0, 3, 2, 1),
        "ctxT": ctx.reshape(TILES, 512, DC, P).transpose(0, 3, 2, 1),
        "mask_f": np.concatenate([mask_f, mask_f], 1),
        "mask_i": np.broadcast_to(mask_i, (TILES, P, 2, SEQ)),
        "mask_b": np.broadcast_to(mask_b, (TILES, P, 2, KEYS)),
        "l0f_gate_w": rows(f0["gate_w"]).reshape(P, -1), "l2f_gate_w": rows(f2["Wg"].T).reshape(P, -1),
        "l3f_gate_w": rows(f3["Wg"].T).reshape(P, -1),
        "l0f_experts": experts(f0["c_fc"], f0["fc_bias"], f0["c_proj"], f0["proj_bias"]),
        "l2f_experts": experts(f2["W1"], f2["b1"], f2["W2"], f2["b2"]),
        "l3f_experts": experts(f3["W1"], f3["b1"], f3["W2"], f3["b2"]),
    }
    stacks = ["ctx", "ctx64", "ctxT", "ctxT64", "mask_f", "mask_i", "mask_b", "l0f_experts", "l2f_experts", "l3f_experts"]
    for name in stacks:
        a = arrays[name]
        arrays[name] = a.reshape(a.shape[0] * a.shape[1], -1)
    arrays = {k: np.ascontiguousarray(v) for k, v in arrays.items()}
    nc = bacc.Bacc("TRN2", target_bir_lowering=False, num_devices=1)
    dram = {k: nc.dram_tensor(k, v.shape, mybir.dt.from_np(v.dtype), kind="ExternalInput").ap() for k, v in arrays.items()}
    out = nc.dram_tensor("out", (P, TILES, D), F32, kind="ExternalOutput").ap()
    perceiver_kernel(nc, dram, out)
    got = run(nc, [arrays], core_ids=[0]).results[0]["out"]
    return got.reshape(P, TILES, D).transpose(1, 0, 2).reshape(BATCH, SEQ, D)
```
